# Optimizing a Trainium2 kernel written in Bass

```python
import numpy as np
import jax
import jax.numpy as jnp

def _softmax(x, axis=-1):
    return jax.nn.softmax(x, axis=axis)

def _gelu(x):
    return jax.nn.gelu(x, approximate=True)

def _silu(x):
    return jax.nn.silu(x)

def _sigmoid(x):
    return jax.nn.sigmoid(x)

def _layernorm(x, axis=-1, eps=1e-05):
    m = jnp.mean(x, axis=axis, keepdims=True)
    v = jnp.var(x, axis=axis, keepdims=True)
    return (x - m) / jnp.sqrt(v + eps)

def _scatter_add(tgt, idx, src, axis=0):
    return tgt.at[idx].add(src)

def _segment_sum(src, seg, n):
    return jax.ops.segment_sum(src, seg, n)
kernel_name = 'mk_xattn_ffn_d2_seqx_r8_026372'

def setup_inputs(seed: int=0):
    np.random.seed(seed)
    _w = jnp.asarray

    def _rec_inputs():
        import jax
        import jax.numpy as jnp
        _rk = jax.random.key(seed)
        x = 0.0003765 + 1 * jax.random.normal(jax.random.fold_in(_rk, 1), (16, 256, 128), jnp.float32)
        _lenS = 256 - jax.random.randint(jax.random.fold_in(_rk, 7), (16,), 0, max(1, 256 // 4) + 1, jnp.int32)
        _lenS2 = 1601 - jax.random.randint(jax.random.fold_in(_rk, 8), (16,), 0, max(1, 1601 // 4) + 1, jnp.int32)
        _ctx_1024P = jax.random.normal(jax.random.fold_in(_rk, 11), (16, 16, 128), jnp.float32)
        _ctx_1024c = jax.random.dirichlet(jax.random.fold_in(_rk, 511), 0.3 * jnp.ones((16,), jnp.float32), (16, 1601))
        _ctx_1024t = jnp.einsum('bsk,bkd->bsd', _ctx_1024c, _ctx_1024P)
        _ctx_1024t = _ctx_1024t * jax.lax.rsqrt(jnp.mean(jnp.square(_ctx_1024t)) + 1e-12) * 0.953939
        ctx_1024 = -0.000292821 + 1.00034 * (_ctx_1024t + 0.3 * jax.random.normal(jax.random.fold_in(_rk, 611), (16, 1601, 128), jnp.float32))
        _validS = jnp.arange(256)[None, :] < _lenS[:, None]
        _validS2 = jnp.arange(1601)[None, :] < _lenS2[:, None]
        _causal = jnp.tril(jnp.ones((256, 256), dtype=bool))
        mask_SxS2_ik0 = jnp.where(jnp.broadcast_to(_validS2[0:1, :], (256, 1601)), 0, 1).astype(jnp.int32)
        mask_BxS2_bk0 = jnp.logical_not(jnp.broadcast_to(_validS2[:, :], (16, 1601)))
        return (x, ctx_1024, mask_SxS2_ik0, mask_BxS2_bk0)
    x, ctx_1024, mask_SxS2_ik0, mask_BxS2_bk0 = _rec_inputs()

    def _L0_xattn_setup():
        import jax, jax.numpy as jnp
        import numpy as np
        N, S, E, H = (2, 256, 128, 16)
        D = E // H

        def _heads(x, W, b):
            n, l, _ = x.shape
            y = x @ W.T + b
            return y.reshape(n, l, H, D).transpose(0, 2, 1, 3)
        key = jax.random.key(seed)
        ks = jax.random.split(key, 12)
        s = 0.02
        inp = {'key': jax.random.normal(ks[0], (N, S, E), jnp.float32), 'value': jax.random.normal(ks[1], (N, S, E), jnp.float32), 'query': jax.random.normal(ks[2], (N, S, E), jnp.float32), 'mask': jnp.tril(jnp.ones((S, S), jnp.int32)), 'Wk': jax.random.normal(ks[3], (E, E), jnp.float32) * s, 'bk': jnp.zeros((E,), jnp.float32), 'Wq': jax.random.normal(ks[4], (E, E), jnp.float32) * s, 'bq': jnp.zeros((E,), jnp.float32), 'Wv': jax.random.normal(ks[5], (E, E), jnp.float32) * s, 'bv': jnp.zeros((E,), jnp.float32), 'Wp': jax.random.normal(ks[6], (E, E), jnp.float32) * s, 'bp': jnp.zeros((E,), jnp.float32)}
        return inp
    _L0_xattn_all = _L0_xattn_setup()
    _L0_xattn_in = {k: v for k, v in _L0_xattn_all.items() if k in ('Wk', 'bk', 'Wq', 'bq', 'Wv', 'bv', 'Wp', 'bp')}
    del _L0_xattn_all

    def _L0_ffn_setup():
        import jax, jax.numpy as jnp
        import numpy as np
        E = 16
        K = 4
        B, S, H, I = (4, 128, 128, 256)
        key = jax.random.key(seed)
        k0, k1, k2, k3 = jax.random.split(key, 4)
        scale = 0.02
        return {'hidden_states': jax.random.normal(k0, (B, S, H), jnp.float32), 'router_w': jax.random.normal(k1, (H, E), jnp.float32) * scale, 'router_b': jnp.zeros((E,), jnp.float32), 'w1': jax.random.normal(k2, (E, H, I), jnp.float32) * scale, 'b1': jnp.zeros((E, I), jnp.float32), 'w2': jax.random.normal(k3, (E, I, H), jnp.float32) * scale, 'b2': jnp.zeros((E, H), jnp.float32)}
    _L0_ffn_all = _L0_ffn_setup()
    _L0_ffn_in = {k: v for k, v in _L0_ffn_all.items() if k in ('router_w', 'router_b', 'w1', 'b1', 'w2', 'b2')}
    del _L0_ffn_all

    def _L1_xattn_setup():
        import jax, jax.numpy as jnp
        import numpy as np
        DIM = 128
        DIM_LATENT = 128
        DIM_HEAD = 64
        INNER = max(DIM, DIM_LATENT)
        HEADS = INNER // DIM_HEAD
        SCALE = DIM_HEAD ** (-0.5)
        LN_EPS = 1e-05
        RMS_EPS = 1e-08

        def layernorm(x, g, b):
            mu = jnp.mean(x, axis=-1, keepdims=True)
            var = jnp.mean(jnp.square(x - mu), axis=-1, keepdims=True)
            return (x - mu) * jax.lax.rsqrt(var + LN_EPS) * g + b

        def rmsnorm(x, gamma):
            n = jnp.linalg.norm(x, axis=-1, keepdims=True) * x.shape[-1] ** (-0.5)
            return x / jnp.maximum(n, RMS_EPS) * gamma
        key = jax.random.key(seed)
        ks = jax.random.split(key, 8)
        b, n, nl = (8, 256, 64)
        x = jax.random.normal(ks[0], (b, n, DIM), dtype=jnp.float32)
        latents = jax.random.normal(ks[1], (b, nl, DIM_LATENT), dtype=jnp.float32)
        mask = jax.random.randint(ks[2], (b, n), 0, 2).astype(bool)
        init = lambda k, shape, fan_in: jax.random.normal(k, shape, jnp.float32) * fan_in ** (-0.5)
        return {'x': x, 'latents': latents, 'mask': mask, 'ln_x_g': jnp.ones((DIM,), jnp.float32), 'ln_x_b': jnp.zeros((DIM,), jnp.float32), 'ln_l_g': jnp.ones((DIM_LATENT,), jnp.float32), 'ln_l_b': jnp.zeros((DIM_LATENT,), jnp.float32), 'q_gamma': jnp.ones((DIM_HEAD,), jnp.float32), 'k_gamma': jnp.ones((DIM_HEAD,), jnp.float32), 'W_q': init(ks[3], (DIM_LATENT, INNER), DIM_LATENT), 'W_kv': init(ks[4], (DIM, 2 * INNER), DIM), 'W_out': init(ks[5], (INNER, DIM_LATENT), INNER), 'b_out': jnp.zeros((DIM_LATENT,), jnp.float32)}
    _L1_xattn_all = _L1_xattn_setup()
    _L1_xattn_in = {k: v for k, v in _L1_xattn_all.items() if k in ('ln_x_g', 'ln_x_b', 'ln_l_g', 'ln_l_b', 'q_gamma', 'k_gamma', 'W_q', 'W_kv', 'W_out', 'b_out')}
    del _L1_xattn_all

    def _L1_ffn_setup():
        import jax, jax.numpy as jnp
        import numpy as np
        H = 128
        I = 256
        E = 32
        B, S = (4, 256)

        def _grouped_mm(a, w, group_sizes):
            return jax.lax.ragged_dot(a, w, group_sizes)

        def _swiglu(x, gw, uw, dw):
            return jax.nn.silu(x @ gw) * (x @ uw) @ dw
        key = jax.random.key(seed)
        ks = jax.random.split(key, 8)
        scale = 0.02
        inp = {'hidden_states': jax.random.normal(ks[0], (B, S, H), dtype=jnp.float32), 'gate_w': jax.random.normal(ks[1], (H, E), dtype=jnp.float32) * scale, 'shared_gate_w': jax.random.normal(ks[2], (H, I), dtype=jnp.float32) * scale, 'shared_up_w': jax.random.normal(ks[3], (H, I), dtype=jnp.float32) * scale, 'shared_down_w': jax.random.normal(ks[4], (I, H), dtype=jnp.float32) * scale, 'routed_gate_w': jax.random.normal(ks[5], (E, H, I), dtype=jnp.float32) * scale, 'routed_up_w': jax.random.normal(ks[6], (E, H, I), dtype=jnp.float32) * scale, 'routed_down_w': jax.random.normal(ks[7], (E, I, H), dtype=jnp.float32) * scale}
        return inp
    _L1_ffn_all = _L1_ffn_setup()
    _L1_ffn_in = {k: v for k, v in _L1_ffn_all.items() if k in ('gate_w', 'shared_gate_w', 'shared_up_w', 'shared_down_w', 'routed_gate_w', 'routed_up_w', 'routed_down_w')}
    del _L1_ffn_all
    return {'x': x, 'ctx_1024': ctx_1024, 'mask_SxS2_ik0': mask_SxS2_ik0, 'mask_BxS2_bk0': mask_BxS2_bk0, 'L0_xattn_Wk': _L0_xattn_in['Wk'], 'L0_xattn_bk': _L0_xattn_in['bk'], 'L0_xattn_Wq': _L0_xattn_in['Wq'], 'L0_xattn_bq': _L0_xattn_in['bq'], 'L0_xattn_Wv': _L0_xattn_in['Wv'], 'L0_xattn_bv': _L0_xattn_in['bv'], 'L0_xattn_Wp': _L0_xattn_in['Wp'], 'L0_xattn_bp': _L0_xattn_in['bp'], 'L0_ffn_router_w': _L0_ffn_in['router_w'], 'L0_ffn_router_b': _L0_ffn_in['router_b'], 'L0_ffn_w1': _L0_ffn_in['w1'], 'L0_ffn_b1': _L0_ffn_in['b1'], 'L0_ffn_w2': _L0_ffn_in['w2'], 'L0_ffn_b2': _L0_ffn_in['b2'], 'L1_xattn_ln_x_g': _L1_xattn_in['ln_x_g'], 'L1_xattn_ln_x_b': _L1_xattn_in['ln_x_b'], 'L1_xattn_ln_l_g': _L1_xattn_in['ln_l_g'], 'L1_xattn_ln_l_b': _L1_xattn_in['ln_l_b'], 'L1_xattn_q_gamma': _L1_xattn_in['q_gamma'], 'L1_xattn_k_gamma': _L1_xattn_in['k_gamma'], 'L1_xattn_W_q': _L1_xattn_in['W_q'], 'L1_xattn_W_kv': _L1_xattn_in['W_kv'], 'L1_xattn_W_out': _L1_xattn_in['W_out'], 'L1_xattn_b_out': _L1_xattn_in['b_out'], 'L1_ffn_gate_w': _L1_ffn_in['gate_w'], 'L1_ffn_shared_gate_w': _L1_ffn_in['shared_gate_w'], 'L1_ffn_shared_up_w': _L1_ffn_in['shared_up_w'], 'L1_ffn_shared_down_w': _L1_ffn_in['shared_down_w'], 'L1_ffn_routed_gate_w': _L1_ffn_in['routed_gate_w'], 'L1_ffn_routed_up_w': _L1_ffn_in['routed_up_w'], 'L1_ffn_routed_down_w': _L1_ffn_in['routed_down_w']}

def reference(x, ctx_1024, mask_SxS2_ik0, mask_BxS2_bk0, L0_xattn_Wk, L0_xattn_bk, L0_xattn_Wq, L0_xattn_bq, L0_xattn_Wv, L0_xattn_bv, L0_xattn_Wp, L0_xattn_bp, L0_ffn_router_w, L0_ffn_router_b, L0_ffn_w1, L0_ffn_b1, L0_ffn_w2, L0_ffn_b2, L1_xattn_ln_x_g, L1_xattn_ln_x_b, L1_xattn_ln_l_g, L1_xattn_ln_l_b, L1_xattn_q_gamma, L1_xattn_k_gamma, L1_xattn_W_q, L1_xattn_W_kv, L1_xattn_W_out, L1_xattn_b_out, L1_ffn_gate_w, L1_ffn_shared_gate_w, L1_ffn_shared_up_w, L1_ffn_shared_down_w, L1_ffn_routed_gate_w, L1_ffn_routed_up_w, L1_ffn_routed_down_w):
    import jax
    import jax.numpy as jnp

    def _L0_xattn_ref(key, value, query, mask, Wk, bk, Wq, bq, Wv, bv, Wp, bp):
        import jax, jax.numpy as jnp
        import numpy as np
        N, S, E, H = (2, 256, 128, 16)
        D = E // H

        def _heads(x, W, b):
            n, l, _ = x.shape
            y = x @ W.T + b
            return y.reshape(n, l, H, D).transpose(0, 2, 1, 3)
        q = _heads(query, Wq, bq)
        k = _heads(key, Wk, bk)
        v = _heads(value, Wv, bv)
        scale = 1.0 / jnp.sqrt(jnp.float32(D))
        scores = jnp.einsum('bhsd,bhtd->bhst', q, k) * scale
        scores = jnp.where(mask == 0, jnp.float32(-1000000000000.0), scores)
        probs = jax.nn.softmax(scores, axis=-1)
        ctx = jnp.einsum('bhst,bhtd->bhsd', probs, v)
        ctx = ctx.transpose(0, 2, 1, 3).reshape(query.shape[0], -1, E)
        return ctx @ Wp.T + bp

    def _L0_ffn_ref(hidden_states, router_w, router_b, w1, b1, w2, b2):
        import jax, jax.numpy as jnp
        import numpy as np
        E = 16
        K = 4
        B, S, H, I = (4, 128, 128, 256)
        b, s, h = hidden_states.shape
        logits = hidden_states @ router_w + router_b
        probs = jax.nn.softmax(logits, axis=-1)
        topw, topi = jax.lax.top_k(probs, K)
        topw = topw / jnp.sum(topw, axis=-1, keepdims=True)
        combine = jnp.sum(jax.nn.one_hot(topi, E, dtype=hidden_states.dtype) * topw[..., None], axis=2)
        x = hidden_states.reshape(b * s, h)
        c = combine.reshape(b * s, E)

        def body(acc, expert):
            w1e, b1e, w2e, b2e, ce = expert
            hmid = jax.nn.gelu(x @ w1e + b1e, approximate=False)
            return (acc + (hmid @ w2e + b2e) * ce[:, None], None)
        out, _ = jax.lax.scan(body, jnp.zeros_like(x), (w1, b1, w2, b2, c.T))
        return out.reshape(b, s, h)

    def _L1_xattn_ref(x, latents, mask, ln_x_g, ln_x_b, ln_l_g, ln_l_b, q_gamma, k_gamma, W_q, W_kv, W_out, b_out):
        import jax, jax.numpy as jnp
        import numpy as np
        DIM = 128
        DIM_LATENT = 128
        DIM_HEAD = 64
        INNER = max(DIM, DIM_LATENT)
        HEADS = INNER // DIM_HEAD
        SCALE = DIM_HEAD ** (-0.5)
        LN_EPS = 1e-05
        RMS_EPS = 1e-08

        def layernorm(x, g, b):
            mu = jnp.mean(x, axis=-1, keepdims=True)
            var = jnp.mean(jnp.square(x - mu), axis=-1, keepdims=True)
            return (x - mu) * jax.lax.rsqrt(var + LN_EPS) * g + b

        def rmsnorm(x, gamma):
            n = jnp.linalg.norm(x, axis=-1, keepdims=True) * x.shape[-1] ** (-0.5)
            return x / jnp.maximum(n, RMS_EPS) * gamma
        b, n, _ = x.shape
        nl = latents.shape[1]
        xn = layernorm(x, ln_x_g, ln_x_b)
        ln = layernorm(latents, ln_l_g, ln_l_b)
        q = ln @ W_q
        kv = jnp.concatenate([xn @ W_kv, ln @ W_kv], axis=1)
        k, v = (kv[..., :INNER], kv[..., INNER:])
        to_heads = lambda t: t.reshape(t.shape[0], t.shape[1], HEADS, DIM_HEAD).transpose(0, 2, 1, 3)
        q, k, v = (to_heads(q), to_heads(k), to_heads(v))
        qn = rmsnorm(q, q_gamma) * SCALE
        kn = rmsnorm(k, k_gamma)
        sim = jnp.einsum('bhid,bhjd->bhij', qn, kn)
        full_mask = jnp.pad(mask, ((0, 0), (0, nl)), constant_values=True)
        neg = -jnp.finfo(sim.dtype).max
        sim = jnp.where(full_mask[:, None, None, :], sim, neg)
        attn = jax.nn.softmax(sim.astype(jnp.float32), axis=-1).astype(sim.dtype)
        out = jnp.einsum('bhij,bhjd->bhid', attn, v)
        out = out.transpose(0, 2, 1, 3).reshape(b, nl, INNER)
        return out @ W_out + b_out

    def _L1_ffn_ref(hidden_states, gate_w, shared_gate_w, shared_up_w, shared_down_w, routed_gate_w, routed_up_w, routed_down_w):
        import jax, jax.numpy as jnp
        import numpy as np
        H = 128
        I = 256
        E = 32
        B, S = (4, 256)

        def _grouped_mm(a, w, group_sizes):
            return jax.lax.ragged_dot(a, w, group_sizes)

        def _swiglu(x, gw, uw, dw):
            return jax.nn.silu(x @ gw) * (x @ uw) @ dw
        b, s, h = hidden_states.shape
        x = hidden_states.reshape(-1, h)
        shared_out = _swiglu(x, shared_gate_w, shared_up_w, shared_down_w)
        logits = x @ gate_w
        topk_ids = jnp.argmax(logits, axis=-1)
        topk_val = jnp.max(logits, axis=-1)
        scores = jax.nn.sigmoid(topk_val)[:, None]
        xs = x * scores
        tokens_per_expert = jnp.zeros((E,), jnp.int32).at[topk_ids].add(1)
        order = jnp.argsort(topk_ids)
        sorted_x = xs[order]
        g = _grouped_mm(sorted_x, routed_gate_w, tokens_per_expert)
        u = _grouped_mm(sorted_x, routed_up_w, tokens_per_expert)
        d = _grouped_mm(jax.nn.silu(g) * u, routed_down_w, tokens_per_expert)
        inv = jnp.argsort(order)
        routed_out = d[inv]
        return (shared_out + routed_out).reshape(b, s, h)
    x = x + _L0_xattn_ref(ctx_1024, ctx_1024, _layernorm(x, axis=-1), mask_SxS2_ik0, L0_xattn_Wk, L0_xattn_bk, L0_xattn_Wq, L0_xattn_bq, L0_xattn_Wv, L0_xattn_bv, L0_xattn_Wp, L0_xattn_bp)
    x = x + _L0_ffn_ref(_layernorm(x, axis=-1), L0_ffn_router_w, L0_ffn_router_b, L0_ffn_w1, L0_ffn_b1, L0_ffn_w2, L0_ffn_b2)
    x = x + _L1_xattn_ref(ctx_1024, _layernorm(x, axis=-1), mask_BxS2_bk0, L1_xattn_ln_x_g, L1_xattn_ln_x_b, L1_xattn_ln_l_g, L1_xattn_ln_l_b, L1_xattn_q_gamma, L1_xattn_k_gamma, L1_xattn_W_q, L1_xattn_W_kv, L1_xattn_W_out, L1_xattn_b_out)
    x = x + _L1_ffn_ref(_layernorm(x, axis=-1), L1_ffn_gate_w, L1_ffn_shared_gate_w, L1_ffn_shared_up_w, L1_ffn_shared_down_w, L1_ffn_routed_gate_w, L1_ffn_routed_up_w, L1_ffn_routed_down_w)
    return x

_drawn_inputs = setup_inputs


def setup_inputs(seed=0):
    import zlib

    import numpy as np

    out = dict(_drawn_inputs(seed))
    spreads = {'L0_xattn_bk': (0.0, 0.8),
     'L0_xattn_bq': (0.0, 0.8),
     'L0_xattn_bv': (0.0, 0.1),
     'L0_xattn_bp': (0.0, 0.1),
     'L0_ffn_router_b': (0.0, 0.1),
     'L0_ffn_b1': (0.0, 0.8),
     'L0_ffn_b2': (0.0, 0.1),
     'L1_xattn_ln_x_g': (1.0, 0.2),
     'L1_xattn_ln_x_b': (0.0, 0.1),
     'L1_xattn_ln_l_g': (1.0, 0.2),
     'L1_xattn_ln_l_b': (0.0, 0.1),
     'L1_xattn_q_gamma': (1.0, 0.2),
     'L1_xattn_k_gamma': (1.0, 0.2),
     'L1_xattn_b_out': (0.0, 0.1)}
    factors = {'L0_xattn_Wk': 8.0,
     'L0_xattn_Wq': 8.0,
     'L0_ffn_w1': 3.087,
     'L0_ffn_w2': 2.765,
     'L1_ffn_gate_w': 8.0,
     'L1_ffn_shared_gate_w': 7.183,
     'L1_ffn_shared_up_w': 7.142,
     'L1_ffn_shared_down_w': 7.215,
     'L1_ffn_routed_gate_w': 8.0,
     'L1_ffn_routed_up_w': 8.0,
     'L1_ffn_routed_down_w': 8.0}
    for name, (base, spread) in spreads.items():
        noise = np.random.default_rng([zlib.crc32(name.encode()), seed]).standard_normal(out[name].shape)
        drawn = base * np.exp(spread * noise) if base else spread * noise
        out[name] = jnp.asarray(drawn.astype(out[name].dtype))
    for name, factor in factors.items():
        out[name] = (out[name] * factor).astype(out[name].dtype)
    return out
```

```python
from contextlib import ExitStack

import concourse.bass as bass
from concourse import mybir

F32 = mybir.dt.float32
BF16 = mybir.dt.bfloat16
I32 = mybir.dt.int32
U32 = mybir.dt.uint32
U8 = mybir.dt.uint8
ALU = mybir.AluOpType
ACT = mybir.ActivationFunctionType
AX = mybir.AxisListType.X

P = 128
B, S, E = 16, 256, 128
QT = S // P
NT = B * QT
KEYS = 1601
W = 512
NW = -(-KEYS // W)
KT = W // P
START = [max(KEYS - W * (NW - w), 0) for w in range(NW)]
FIRST_OWN = KEYS - W * (NW - 1)
MASKED = -float(2.0 ** 100)
DOUBLED = -float(2.0 ** 101)
NO_MAX = -float(2.0 ** 102)
EPS = 1e-5


class Alloc:

    def __init__(self, nc, stack):
        self.nc, self.stack, self.sems = nc, stack, []
        stack.callback(self.clear)

    def clear(self):
        if self.sems:
            self.nc.clear_and_free_semaphores(self.sems)
            self.nc.all_engine_barrier()

    def sb(self, name, shape, dt=F32):
        return self.stack.enter_context(self.nc.sbuf_tensor(name, shape, dt))

    def ps(self, name, shape, dt=F32):
        return self.stack.enter_context(self.nc.psum_tensor(name, shape, dt))

    def sem(self, name):
        self.sems.append(self.nc.alloc_semaphore(name))
        return self.sems[-1]


class Awaited:

    def __init__(self, eng, sem, name, step=1):
        self.eng, self.sem, self.step = eng, sem, step
        self.value = eng.alloc_register(name)
        eng.reg_mov(self.value, step)

    def at(self):
        return self.eng.snap(self.value)

    def wait(self, at=None):
        self.eng.wait_ge(self.sem, self.at() if at is None else at)
        self.eng.reg_add(self.value, self.value, self.step)


class Steps:

    def __init__(self, eng, sem, base=0):
        self.eng, self.sem, self.base, self.n = eng, sem, base, 0

    def mark(self, ins):
        self.n += 1
        ins.then_inc(self.sem, 1)

    def settle(self):
        self.eng.wait_ge(self.sem, self.base + self.n)


def load_tokens(nc, x, x_sb, ident):
    with ExitStack() as st:
        a = Alloc(nc, st)
        loaded, zeroed, made = a.sem("x_loaded"), a.sem("ident_zeroed"), a.sem("ident_made")
        block = st.enter_context(nc.Block())

        @block.sync
        def _(sp):
            sp.dma_start(x_sb[:], x.rearrange("b (t p) e -> p (b t) e", p=P)).then_inc(loaded, 16)
            sp.wait_ge(loaded, 16)

        @block.gpsimd
        def _(pool):
            pool.memset(ident[:], 0.0).then_inc(zeroed, 1)
            pool.wait_ge(zeroed, 1)
            pool.affine_select(out=ident[:], in_=ident[:], compare_op=ALU.not_equal, fill=1.0, base=0,
                               pattern=[[-1, P]], channel_multiplier=1).then_inc(made, 1)
            pool.wait_ge(made, 1)


def layer_norm(nc, tag, src, dst, tiles, transposed=None, ident=None, affine=None):
    with ExitStack() as st:
        a = Alloc(nc, st)
        stats = a.sb(tag + "_stats", [P, tiles, 6])
        mv = a.sb(tag + "_mv", [P, tiles, 2])
        var = a.sb(tag + "_var", [P, tiles])
        rstd = a.sb(tag + "_rstd", [P, tiles])
        shift = a.sb(tag + "_shift", [P, tiles])
        expo = a.sb(tag + "_expo", [P, tiles])
        counted, merged, var_ready, root_ready = (a.sem(tag + n) for n in ("_counted", "_merged", "_varr", "_root"))
        expo_set = a.sem(tag + "_expo_set")
        scaled, normed, turned, moved = (a.sem(tag + n) for n in ("_scaled", "_normed", "_turned", "_moved"))
        if transposed is not None:
            pt = [a.ps(f"{tag}_pt{i}", [P, 4, P]) for i in range(2)]
        block = st.enter_context(nc.Block())

        @block.vector
        def _(dve):
            with dve.Fori(0, tiles) as t:
                dve.bn_stats(stats[:, bass.ds(t, 1), :].rearrange("p o s -> p (o s)"),
                             src[:, bass.ds(t, 1), :].rearrange("p o e -> p (o e)")).then_inc(counted, 1)
            dve.wait_ge(counted, tiles)
            for t in range(tiles):
                dve.bn_aggr(mv[:, t, :], stats[:, t, :]).then_inc(merged, 1)
            dve.wait_ge(merged, tiles)
            dve.tensor_scalar(var[:], mv[:, :, 1], EPS, None, ALU.add).then_inc(var_ready, 1)
            dve.wait_ge(root_ready, 1)
            dve.scalar_tensor_tensor(shift[:], mv[:, :, 0], -1.0, rstd[:], ALU.mult, ALU.mult).then_inc(scaled, 1)
            dve.wait_ge(scaled, 1)
            with dve.Fori(0, tiles) as t:
                dve.tensor_scalar(dst[:, bass.ds(t, 1), :].rearrange("p o e -> p (o e)"),
                                  src[:, bass.ds(t, 1), :].rearrange("p o e -> p (o e)"),
                                  rstd[:, bass.ds(t, 1)], shift[:, bass.ds(t, 1)],
                                  ALU.mult, ALU.add).then_inc(normed, 1)
            dve.wait_ge(normed, tiles)

        @block.gpsimd
        def _(pool):
            pool.memset(expo[:], -0.5).then_inc(expo_set, 1)
            pool.wait_ge(expo_set, 1)
            pool.wait_ge(var_ready, 1)
            pool.tensor_tensor(rstd[:], var[:], expo[:], ALU.pow).then_inc(root_ready, 1)

        @block.scalar
        def _(act):
            if transposed is None:
                return
            for g in range(tiles // 4):
                act.wait_ge(turned, g + 1)
                out = transposed[:, g * 4 * P:(g + 1) * 4 * P]
                src_ps = pt[g % 2][:].rearrange("p t q -> p (t q)")
                if affine is None:
                    act.activation(out, src_ps, ACT.Copy).then_inc(moved, 1)
                else:
                    act.activation(out, src_ps, ACT.Identity, bias=affine[1], scale=affine[0]).then_inc(moved, 1)
            act.wait_ge(moved, tiles // 4)

        if transposed is not None:
            @block.tensor
            def _(pe):
                for g in range(tiles // 4):
                    pe.wait_ge(normed, 4 * (g + 1))
                    if g >= 2:
                        pe.wait_ge(moved, g - 1)
                    for t in range(4):
                        mm = pe.transpose(pt[g % 2][:, t, :], dst[:, 4 * g + t, :], ident[:])
                    mm.then_inc(turned, 1)


def turn_weights(nc, tag, loads, ident, columns=(), rows=(), others=()):
    with ExitStack() as st:
        a = Alloc(nc, st)
        n = len(loads)
        raw = a.sb(tag + "_raw", [P, max(n, 1), P])
        pt = a.ps(tag + "_pt", [P, 4, P])
        loaded, turned, moved = a.sem(tag + "_loaded"), a.sem(tag + "_turned"), a.sem(tag + "_moved")
        block = st.enter_context(nc.Block())
        total = n + len(columns) + len(rows) + len(others)

        @block.sync
        def _(sp):
            for i, (src, _) in enumerate(loads):
                sp.dma_start(raw[:, i, :], src).then_inc(loaded, 16)
            for src, dst in columns:
                sp.dma_start(dst, src.rearrange("(p o) -> p o", o=1)).then_inc(loaded, 16)
            for src, dst in rows:
                sp.dma_start(dst, src.partition_broadcast(P)).then_inc(loaded, 16)
            for src, dst in others:
                sp.dma_start(dst, src).then_inc(loaded, 16)
            sp.wait_ge(loaded, 16 * total)

        if not n:
            return

        @block.tensor
        def _(pe):
            pe.wait_ge(loaded, 16 * total)
            for i in range(n):
                mm = pe.transpose(pt[:, i, :], raw[:, i, :], ident[:])
            mm.then_inc(turned, 1)

        @block.vector
        def _(dve):
            dve.wait_ge(turned, 1)
            for i, (_, dst) in enumerate(loads):
                dve.tensor_copy(dst, pt[:, i, :]).then_inc(moved, 1)
            dve.wait_ge(moved, n)


def l0_mask(nc, mask, mneg, flags, ident):
    with ExitStack() as st:
        a = Alloc(nc, st)
        raw = a.sb("m_raw", [P, QT, KEYS], I32)
        best = a.sb("m_best", [P, QT, NW])
        some = a.sb("m_some", [P, QT])
        need = a.sb("m_need", [P, QT, NW])
        row = a.sb("m_row", [QT * NW, 1])
        turned_sb = a.sb("m_turned_sb", [QT * NW, P])
        line = a.sb("m_line", [1, QT * NW])
        merged = a.sb("m_merged", [1, NW])
        pt = a.ps("m_pt", [P, P])
        loaded, steps, turned, topped, line_ps = (a.sem(n) for n in ("m_loaded", "m_steps", "m_turn", "m_top", "m_line_ps"))
        block = st.enter_context(nc.Block())

        @block.sync
        def _(sp):
            sp.dma_start(raw[:], mask.rearrange("(t p) k -> p t k", p=P)).then_inc(loaded, 16)
            sp.wait_ge(loaded, 16)

        @block.vector
        def _(dve):
            s = Steps(dve, steps)
            s.mark(dve.memset(mneg[:, :, 0, FIRST_OWN:], DOUBLED))
            dve.wait_ge(loaded, 16)
            for w in range(NW):
                own = FIRST_OWN if w == 0 else W
                s.mark(dve.tensor_scalar(mneg[:, :, w, 0:own], raw[:, :, START[w]:START[w] + own], 0.0, MASKED,
                                         ALU.is_equal, ALU.mult))
            s.settle()
            s.mark(dve.tensor_reduce(best[:], mneg[:], AX, ALU.max))
            s.settle()
            s.mark(dve.tensor_reduce(some[:], best[:], AX, ALU.max))
            s.settle()
            s.mark(dve.tensor_scalar(some[:], some[:], 0.0, None, ALU.is_lt))
            s.mark(dve.tensor_scalar(best[:], best[:], 0.0, None, ALU.is_equal))
            s.settle()
            for t in range(QT):
                s.mark(dve.tensor_scalar(need[:, t, :], best[:, t, :], some[:, t:t + 1], None, ALU.max))
            s.settle()
            dve.engine_nop().then_inc(topped, 1)
            dve.wait_ge(turned, 1)
            s.mark(dve.tensor_reduce(row[:], pt[0:QT * NW, :], AX, ALU.max))
            s.settle()
            dve.engine_nop().then_inc(topped, 1)
            dve.wait_ge(line_ps, 1)
            s.mark(dve.tensor_copy(line[:], pt[0:1, 0:QT * NW]))
            s.settle()
            s.mark(dve.tensor_tensor(merged[:], line[:, 0:NW], line[:, NW:2 * NW], ALU.max))
            s.settle()
            s.mark(dve.tensor_copy(flags[:], merged[:]))
            s.settle()

        @block.tensor
        def _(pe):
            pe.wait_ge(topped, 1)
            pe.transpose(pt[0:QT * NW, :], need[:].rearrange("p t w -> p (t w)"), ident[:]).then_inc(turned, 1)
            pe.wait_ge(topped, 2)
            pe.transpose(pt[0:1, 0:QT * NW], row[:], ident[0:QT * NW, 0:QT * NW]).then_inc(line_ps, 1)


H0, D0 = 16, 8
QUADS = H0 // 4
HQ = 4 * QT
SCALE0 = float(D0) ** -0.5


def l0_attention(nc, x_sb, xlnT, mneg, flags, ident, ctx, w):
    wqT, wkT, wvT, wpT, bq, bk, bv, bp = w
    ctx_rows = ctx.rearrange("b k e -> (b k) e")
    with ExitStack() as st:
        a = Alloc(nc, st)
        head_rows = a.sb("head_rows", [P, H0])
        qT = a.sb("qT", [P, NT * P])
        q_b = a.sb("q_b", [P, S])
        qbd = a.sb("qbd", [P, 2, H0, S])
        ctx_sb = a.sb("ctx_sb", [P, KT, E])
        ctxT = a.sb("ctxT", [P, W])
        kT = a.sb("kT", [P, W])
        v = a.sb("v", [P, KT, E])
        scores = a.sb("scores", [P, 2, HQ, W])
        probsT = a.sb("probsT", [P, 2, KT, 4, S])
        oT = a.sb("oT", [P, QUADS, S])
        m_old = a.sb("m_old", [P, H0 * QT])
        m_win = a.sb("m_win", [P, H0 * QT])
        m_new = a.sb("m_new", [P, H0 * QT])
        m_diff = a.sb("m_diff", [P, H0 * QT])
        alpha = a.sb("alpha", [P, H0 * QT])
        neg_m = a.sb("neg_m", [P, H0 * QT])
        l_win = a.sb("l_win", [P, H0 * QT])
        l_sum = a.sb("l_sum", [P, H0 * QT])
        acc = a.sb("acc", [P, QT, H0, D0])
        heads = a.sb("heads", [P, QT, E])
        headsT = a.sb("headsT", [P, S])
        ps_s = [a.ps(f"ps_s{i}", [P, W]) for i in range(2)]
        ps_t = [a.ps(f"ps_t{i}", [P, KT, P]) for i in range(2)]
        ps_o = a.ps("ps_o", [P, QUADS, S])
        ps_m = [a.ps(f"ps_m{i}", [P, 512]) for i in range(2)]

        sem = {n: a.sem("a0_" + n) for n in (
            "rows_zeroed rows_made q_ps q_sb q_b_ready qbd_ready flags_seen ctx_loaded ctxT_ps ctxT_sb kv_ps k_sb v_sb s_ps s_sb "
            "neg_m_ready p_sb t_ps t_act t_dve o_ps o_sb oT_ps acc_done alpha_ready heads_ready headsT_ps headsT_sb "
            "y_ps x_done dve_steps state_ready").split()}
        block = st.enter_context(nc.Block())

        def windows(eng):
            live = [eng.value_load(flags[0:1, i:i + 1], min_val=0, max_val=1) for i in range(NW)]
            n = eng.alloc_register("n_windows")
            eng.reg_mov(n, 0)
            return live, n

        @block.sync
        def _(sp):
            live, n = windows(sp)
            with sp.Fori(0, B) as b:
                for wi in range(NW):
                    with sp.If(live[wi] != 0):
                        done = sp.snap(n)
                        sp.wait_ge(sem["ctxT_ps"], done)
                        sp.dma_start(ctx_sb[:], ctx_rows[bass.ds(b * KEYS + START[wi], W), :].rearrange(
                            "(t p) e -> p t e", p=P)).then_inc(sem["ctx_loaded"], 16)
                        sp.reg_add(n, n, 1)

        @block.gpsimd
        def _(pool):
            pool.memset(head_rows[:], 1.0).then_inc(sem["rows_zeroed"], 1)
            pool.wait_ge(sem["rows_zeroed"], 1)
            pool.affine_select(out=head_rows[:], in_=head_rows[:], compare_op=ALU.is_ge, fill=0.0, base=0,
                               pattern=[[-D0, H0]], channel_multiplier=1).then_inc(sem["rows_made"], 1)
            pool.wait_ge(sem["rows_made"], 1)
            pool.affine_select(out=head_rows[:], in_=head_rows[:], compare_op=ALU.is_ge, fill=0.0, base=D0 - 1,
                               pattern=[[D0, H0]], channel_multiplier=-1).then_inc(sem["rows_made"], 1)
            pool.wait_ge(sem["rows_made"], 2)
            pool.wait_ge(sem["q_sb"], NT * P // 512)

            q_b_ready = Awaited(pool, sem["q_b_ready"], "a0_q_b_ready_at")

            def spread(b, half):
                pool.wait_ge(sem["qbd_ready"], b)
                pool.tensor_copy(q_b[:], qT[:, bass.ds(b * S, S)]).then_inc(sem["q_b_ready"], 1)
                q_b_ready.wait()
                for h in range(H0):
                    ins = pool.tensor_scalar(qbd[:, half, h, :], q_b[:], head_rows[:, h:h + 1], None, ALU.mult)
                ins.then_inc(sem["qbd_ready"], 1)

            with pool.Fori(0, B // 2) as i:
                pool.wait_ge(sem["headsT_ps"], i * 2)
                spread(i * 2, 0)
                spread(i * 2 + 1, 1)

        @block.tensor
        def _(pe):
            for g in range(NT * P // 512):
                if g >= 2:
                    pe.wait_ge(sem["q_sb"], g - 1)
                pe.matmul(ps_m[g % 2][:], wqT[:], xlnT[:, g * 512:(g + 1) * 512], start=True,
                          stop=True).then_inc(sem["q_ps"], 1)
            live, n = windows(pe)
            pe.wait_ge(sem["q_sb"], NT * P // 512)
            pe.wait_ge(sem["state_ready"], 1)

            def one_score(u, quad, half, j):
                h, t = 4 * quad + j // QT, j % QT
                if not (quad == 0 and j < 2):
                    pe.wait_ge(sem["s_sb"], u * HQ + j - 1)
                pe.matmul(ps_s[j % 2][:], qbd[:, half, h, t * P:(t + 1) * P], kT[:], start=True,
                          stop=True).then_inc(sem["s_ps"], 1)

            def one_turn(u, quad, j):
                pe.wait_ge(sem["p_sb"], u * HQ + j + 1)
                if j % 2 == 0:
                    pe.wait_ge(sem["t_act"], u * HQ // 2 + j // 2)
                else:
                    pe.wait_ge(sem["t_dve"], u * HQ // 2 + j // 2)
                for k in range(KT):
                    mm = pe.transpose(ps_t[j % 2][:, k, :], scores[:, quad % 2, j, k * P:(k + 1) * P], ident[:])
                mm.then_inc(sem["t_ps"], 1)

            def values(u, quad):
                pe.wait_ge(sem["t_act"], (u + 1) * HQ // 2)
                pe.wait_ge(sem["t_dve"], (u + 1) * HQ // 2)
                for k in range(KT):
                    for i in range(4):
                        h = 4 * quad + i
                        mm = pe.matmul(ps_o[32 * i:32 * i + D0, quad, :], v[:, k, D0 * h:D0 * (h + 1)],
                                       probsT[:, quad % 2, k, i, :], start=(k == 0), stop=(k == KT - 1),
                                       tile_position=(0, 32 * i))
                mm.then_inc(sem["o_ps"], 1)

            def window(done, half):
                pe.wait_ge(sem["ctx_loaded"], (done + 1) * 16)
                pe.wait_ge(sem["acc_done"], done)
                for k in range(KT):
                    mm = pe.transpose(ps_m[0][:, k * P:(k + 1) * P], ctx_sb[:, k, :], ident[:])
                mm.then_inc(sem["ctxT_ps"], 1)
                pe.wait_ge(sem["ctxT_sb"], done + 1)
                pe.matmul(ps_m[1][:], wkT[:], ctxT[:], start=True, stop=True).then_inc(sem["kv_ps"], 1)
                for k in range(KT):
                    mm = pe.matmul(ps_m[0][:, k * P:(k + 1) * P], ctxT[:, k * P:(k + 1) * P], wvT[:], start=True,
                                   stop=True)
                mm.then_inc(sem["kv_ps"], 1)
                pe.wait_ge(sem["k_sb"], done + 1)
                pe.wait_ge(sem["s_sb"], done * HQ * QUADS)
                for j in range(HQ):
                    one_score(done * QUADS, 0, half, j)
                pe.wait_ge(sem["v_sb"], done + 1)
                for quad in range(QUADS):
                    u = done * QUADS + quad
                    for j in range(HQ):
                        if quad + 1 < QUADS:
                            one_score(u + 1, quad + 1, half, j)
                        one_turn(u, quad, j)
                    if quad == 0:
                        pe.wait_ge(sem["o_sb"], done)
                    values(u, quad)
                pe.wait_ge(sem["o_sb"], done + 1)
                for t in range(QT):
                    for quad in range(QUADS):
                        mm = pe.transpose(ps_m[t][:, quad * P:(quad + 1) * P], oT[:, quad, t * P:(t + 1) * P], ident[:])
                    mm.then_inc(sem["oT_ps"], 1)

            def batch(b, half):
                pe.wait_ge(sem["qbd_ready"], b + 1)
                for wi in range(NW):
                    with pe.If(live[wi] != 0):
                        window(pe.snap(n), half)
                        pe.reg_add(n, n, 1)
                pe.wait_ge(sem["heads_ready"], b + 1)
                for t in range(QT):
                    mm = pe.transpose(ps_m[0][:, t * P:(t + 1) * P], heads[:, t, :], ident[:])
                mm.then_inc(sem["headsT_ps"], 1)
                pe.wait_ge(sem["headsT_sb"], b + 1)
                for t in range(QT):
                    mm = pe.matmul(ps_m[1][:, t * P:(t + 1) * P], headsT[:, t * P:(t + 1) * P], wpT[:], start=True,
                                   stop=True)
                mm.then_inc(sem["y_ps"], 1)
                pe.wait_ge(sem["x_done"], b + 1)

            with pe.Fori(0, B // 2) as i:
                batch(i * 2, 0)
                batch(i * 2 + 1, 1)

        @block.scalar
        def _(act):
            for g in range(NT * P // 512):
                act.wait_ge(sem["q_ps"], g + 1)
                act.activation(qT[:, g * 512:(g + 1) * 512], ps_m[g % 2][:], ACT.Identity,
                               bias=bq[:]).then_inc(sem["q_sb"], 1)
            live, n = windows(act)

            def window(done):
                act.wait_ge(sem["ctxT_ps"], done + 1)
                act.wait_ge(sem["kv_ps"], done * 2)
                act.activation(ctxT[:], ps_m[0][:], ACT.Copy).then_inc(sem["ctxT_sb"], 1)
                act.wait_ge(sem["kv_ps"], done * 2 + 1)
                act.wait_ge(sem["s_ps"], done * HQ * QUADS)
                act.activation(kT[:], ps_m[1][:], ACT.Identity, bias=bk[:]).then_inc(sem["k_sb"], 1)
                for quad in range(QUADS):
                    u = done * QUADS + quad
                    act.wait_ge(sem["neg_m_ready"], u + 1)
                    c = quad * HQ
                    if quad == 0:
                        act.wait_ge(sem["acc_done"], done)
                    act.activation(alpha[:, c:c + HQ], m_diff[:, c:c + HQ], ACT.Exp,
                                   scale=SCALE0).then_inc(sem["alpha_ready"], 1)

                    def move(j):
                        act.wait_ge(sem["t_ps"], u * HQ + j + 1)
                        i, t = j // QT, j % QT
                        if j == 0:
                            if quad >= 2:
                                act.wait_ge(sem["o_ps"], u - 1)
                            else:
                                act.wait_ge(sem["o_ps"], done * QUADS)
                        act.activation(probsT[:, quad % 2, :, i, t * P:(t + 1) * P], ps_t[0][:],
                                       ACT.Copy).then_inc(sem["t_act"], 1)

                    for j in range(HQ):
                        act.activation(scores[:, quad % 2, j, :], scores[:, quad % 2, j, :], ACT.Exp,
                                       bias=neg_m[:, c + j:c + j + 1], scale=SCALE0,
                                       accum_out=l_win[:, c + j:c + j + 1]).then_inc(sem["p_sb"], 1)
                        if j % 2 == 1:
                            move(j - 1)
                act.wait_ge(sem["o_ps"], (done + 1) * QUADS)
                act.wait_ge(sem["oT_ps"], done * QT)
                act.activation(oT[:], ps_o[:], ACT.Copy).then_inc(sem["o_sb"], 1)

            with act.Fori(0, B) as b:
                for wi in range(NW):
                    with act.If(live[wi] != 0):
                        window(act.snap(n))
                        act.reg_add(n, n, 1)
                act.wait_ge(sem["headsT_ps"], b + 1)
                act.wait_ge(sem["y_ps"], b)
                act.activation(headsT[:], ps_m[0][:, 0:S], ACT.Copy).then_inc(sem["headsT_sb"], 1)

        @block.vector
        def _(dve):
            dve.memset(ps_o[:], 0.0).then_inc(sem["state_ready"], 1)
            live, n = windows(dve)
            steps = dve.alloc_register("n_steps")
            dve.reg_mov(steps, 0)
            scores_in = Awaited(dve, sem["s_ps"], "a0_s_ps_at")

            def window(done, wi):
                s = Steps(dve, sem["dve_steps"], dve.snap(steps))
                dve.wait_ge(sem["kv_ps"], done * 2 + 2)
                dve.wait_ge(sem["o_ps"], done * QUADS)
                dve.tensor_tensor(v[:], ps_m[0][:].rearrange("p (k e) -> p k e", k=KT),
                                  bv[:].unsqueeze(1).broadcast_to([P, KT, E]), ALU.add).then_inc(sem["v_sb"], 1)

                def reduce_one(u, quad, j):
                    at = scores_in.at()
                    if j == 0:
                        if quad >= 2:
                            dve.wait_ge(sem["t_ps"], (u - 1) * HQ)
                        else:
                            dve.wait_ge(sem["t_ps"], done * QUADS * HQ)
                    scores_in.wait(at)
                    c = quad * HQ + j
                    dve.tensor_tensor_reduce(scores[:, quad % 2, j, :], ps_s[j % 2][:], mneg[:, j % QT, wi, :], 1.0,
                                             NO_MAX, ALU.add, ALU.max,
                                             m_win[:, c:c + 1]).then_inc(sem["s_sb"], 1)

                def shift(u, quad):
                    c = slice(quad * HQ, (quad + 1) * HQ)
                    dve.wait_ge(sem["s_sb"], (u + 1) * HQ)
                    s.mark(dve.tensor_tensor(m_new[:, c], m_old[:, c], m_win[:, c], ALU.max))
                    s.settle()
                    s.mark(dve.tensor_tensor(m_diff[:, c], m_old[:, c], m_new[:, c], ALU.subtract))
                    s.settle()
                    s.mark(dve.tensor_copy(m_old[:, c], m_new[:, c]))
                    dve.tensor_scalar(neg_m[:, c], m_new[:, c], -SCALE0, None, ALU.mult).then_inc(sem["neg_m_ready"], 1)

                for j in range(HQ):
                    reduce_one(done * QUADS, 0, j)
                shift(done * QUADS, 0)
                for quad in range(QUADS):
                    u = done * QUADS + quad
                    for j in range(HQ):
                        if quad + 1 < QUADS:
                            reduce_one(u + 1, quad + 1, j)
                        if j % 2:
                            dve.wait_ge(sem["t_ps"], u * HQ + j + 1)
                            if j == 1:
                                if quad >= 2:
                                    dve.wait_ge(sem["o_ps"], u - 1)
                                else:
                                    dve.wait_ge(sem["o_ps"], done * QUADS)
                            i, t = j // QT, j % QT
                            dve.tensor_copy(probsT[:, quad % 2, :, i, t * P:(t + 1) * P],
                                            ps_t[1][:]).then_inc(sem["t_dve"], 1)
                    if quad + 1 < QUADS:
                        shift(u + 1, quad + 1)
                dve.wait_ge(sem["alpha_ready"], (done + 1) * QUADS)
                dve.wait_ge(sem["p_sb"], (done + 1) * QUADS * HQ)
                dve.wait_ge(sem["acc_done"], done)
                s.mark(dve.tensor_tensor(l_sum[:], l_sum[:], alpha[:], ALU.mult))
                for t in range(QT):
                    by_head = alpha[:].rearrange("p (h t) -> p h t", t=QT)[:, :, t:t + 1].broadcast_to([P, H0, D0])
                    s.mark(dve.tensor_tensor(acc[:, t, :, :], acc[:, t, :, :], by_head, ALU.mult))
                s.settle()
                s.mark(dve.tensor_tensor(l_sum[:], l_sum[:], l_win[:], ALU.add))
                for t in range(QT):
                    dve.wait_ge(sem["oT_ps"], done * QT + t + 1)
                    got = ps_m[t][:].rearrange("p (h d) -> p h d", d=32)[:, :, 0:D0]
                    ins = dve.tensor_tensor(acc[:, t, :, :], acc[:, t, :, :], got, ALU.add)
                    if t + 1 < QT:
                        s.mark(ins)
                ins.then_inc(sem["acc_done"], 1)
                s.settle()
                dve.reg_add(steps, steps, s.n)

            with dve.Fori(0, B) as b:
                s = Steps(dve, sem["dve_steps"], dve.snap(steps))
                s.mark(dve.memset(m_old[:], NO_MAX))
                s.mark(dve.memset(l_sum[:], 0.0))
                s.mark(dve.memset(acc[:], 0.0))
                s.settle()
                dve.reg_add(steps, steps, s.n)
                for wi in range(NW):
                    with dve.If(live[wi] != 0):
                        window(dve.snap(n), wi)
                        dve.reg_add(n, n, 1)
                s = Steps(dve, sem["dve_steps"], dve.snap(steps))
                dve.wait_ge(sem["acc_done"], dve.snap(n))
                s.mark(dve.reciprocal(l_sum[:], l_sum[:]))
                s.settle()
                for t in range(QT):
                    by_head = l_sum[:].rearrange("p (h t) -> p h t", t=QT)[:, :, t:t + 1].broadcast_to([P, H0, D0])
                    ins = dve.tensor_tensor(heads[:, t, :].rearrange("p (h d) -> p h d", d=D0), acc[:, t, :, :],
                                            by_head, ALU.mult)
                    if t + 1 < QT:
                        s.mark(ins)
                ins.then_inc(sem["heads_ready"], 1)
                dve.wait_ge(sem["y_ps"], b + 1)
                x_b = x_sb[:, bass.ds(b * QT, QT), :]
                s.mark(dve.tensor_tensor(x_b, x_b, ps_m[1][:, 0:S].rearrange("p (t e) -> p t e", t=QT), ALU.add))
                s.settle()
                dve.tensor_tensor(x_b, x_b, bp[:].unsqueeze(1).broadcast_to([P, QT, E]),
                                  ALU.add).then_inc(sem["x_done"], 1)
                dve.reg_add(steps, steps, s.n)
            dve.wait_ge(sem["x_done"], B)


E0, K0, I0 = 16, 4, 256
CH = 512
CT = CH // P


def l0_router(nc, x_sb, xlnT, ident, rw, rb, b2, weight):
    with ExitStack() as st:
        a = Alloc(nc, st)
        logits = a.sb("r_logits", [P, NT, E0])
        e = a.sb("r_e", [P, NT, E0])
        sel = a.sb("r_sel", [P, NT, E0])
        eq = [a.sb(f"r_eq{i}", [P, NT, E0]) for i in range(2)]
        top = a.sb("r_top", [P, NT, 8])
        need = a.sb("r_need", [P, NT])
        total = a.sb("r_total", [P, NT])
        wT = a.sb("r_wT", [E0, 4, P])
        ps_l = a.ps("r_ps_l", [P, NT, E0])
        ps_w = a.ps("r_ps_w", [P, 4, P])
        ps_b = a.ps("r_ps_b", [P, 4, P])
        s_logit, s_steps, s_centred, s_exp, s_weight, s_turn, s_moved, s_bias, s_added = (
            a.sem("r_s" + n) for n in "logit steps centred exp weight turn moved bias added".split())
        block = st.enter_context(nc.Block())
        per_tile = lambda t: t[:].unsqueeze(2).broadcast_to([P, NT, E0])

        @block.tensor
        def _(pe):
            for t in range(NT):
                mm = pe.matmul(ps_l[:, t, :], xlnT[:, t * P:(t + 1) * P], rw[:], start=True, stop=True)
            mm.then_inc(s_logit, 1)
            pe.wait_ge(s_weight, 1)
            for g in range(NT // 4):
                pe.wait_ge(s_moved, g)
                for i in range(4):
                    mm = pe.transpose(ps_w[0:E0, i, :], weight[:, 4 * g + i, :], ident[:])
                mm.then_inc(s_turn, 1)
                pe.wait_ge(s_moved, g + 1)
                pe.wait_ge(s_added, g)
                for i in range(4):
                    mm = pe.matmul(ps_b[:, i, :], wT[:, i, :], b2[:], start=True, stop=True)
                mm.then_inc(s_bias, 1)

        @block.scalar
        def _(act):
            act.wait_ge(s_centred, 1)
            act.activation(e[:], logits[:], ACT.Exp).then_inc(s_exp, 1)
            for g in range(NT // 4):
                act.wait_ge(s_turn, g + 1)
                act.wait_ge(s_bias, g)
                act.activation(wT[:], ps_w[0:E0, :, :], ACT.Copy).then_inc(s_moved, 1)

        @block.vector
        def _(dve):
            s = Steps(dve, s_steps)
            dve.wait_ge(s_logit, 1)
            s.mark(dve.tensor_tensor(logits[:], ps_l[:], rb[:].unsqueeze(1).broadcast_to([P, NT, E0]), ALU.add))
            s.settle()
            for t in range(NT):
                s.mark(dve.max(top[:, t, :], logits[:, t, :]))
            s.settle()
            kth = top[:, :, K0 - 1:K0].broadcast_to([P, NT, E0])
            s.mark(dve.tensor_tensor(sel[:], logits[:], kth, ALU.is_gt))
            s.mark(dve.tensor_tensor(eq[0][:], logits[:], kth, ALU.is_equal))
            s.mark(dve.tensor_tensor(logits[:], logits[:], top[:, :, 0:1].broadcast_to([P, NT, E0]), ALU.subtract))
            s.settle()
            dve.engine_nop().then_inc(s_centred, 1)
            s.mark(dve.tensor_reduce(need[:], sel[:], AX, ALU.add))
            s.settle()
            s.mark(dve.tensor_scalar(need[:], need[:], -1.0, float(K0), ALU.mult, ALU.add))
            dve.wait_ge(s_exp, 1)
            s.mark(dve.tensor_copy(logits[:], eq[0][:]))
            s.settle()
            step, cur = 1, 0
            while step < E0:
                s.mark(dve.tensor_copy(eq[1 - cur][:, :, 0:step], eq[cur][:, :, 0:step]))
                s.mark(dve.tensor_tensor(eq[1 - cur][:, :, step:], eq[cur][:, :, step:], eq[cur][:, :, 0:E0 - step],
                                         ALU.add))
                s.settle()
                cur, step = 1 - cur, step * 2
            s.mark(dve.tensor_tensor(eq[cur][:], eq[cur][:], per_tile(need), ALU.is_le))
            s.settle()
            s.mark(dve.tensor_tensor(eq[cur][:], eq[cur][:], logits[:], ALU.mult))
            s.settle()
            s.mark(dve.tensor_tensor(sel[:], sel[:], eq[cur][:], ALU.add))
            s.settle()
            s.mark(dve.tensor_tensor(e[:], e[:], sel[:], ALU.mult))
            s.settle()
            s.mark(dve.tensor_reduce(total[:], e[:], AX, ALU.add))
            s.settle()
            s.mark(dve.reciprocal(total[:], total[:]))
            s.settle()
            dve.tensor_tensor(weight[:], e[:], per_tile(total), ALU.mult).then_inc(s_weight, 1)
            for g in range(NT // 4):
                dve.wait_ge(s_bias, g + 1)
                dve.tensor_tensor(x_sb[:, 4 * g:4 * g + 4, :], x_sb[:, 4 * g:4 * g + 4, :], ps_b[:],
                                  ALU.add).then_inc(s_added, 1)
            dve.wait_ge(s_added, NT // 4)


def l0_experts(nc, x_sb, xlnT, w1, b1, w2, weight):
    with ExitStack() as st:
        a = Alloc(nc, st)
        hid = a.sb("e_hid", [P, 2, 2, CH])
        ps_h = [a.ps(f"e_ps_h{i}", [P, 2, CH]) for i in range(2)]
        ps_y = [a.ps(f"e_ps_y{i}", [P, CT, E]) for i in range(2)]
        h_ps, h_sb, y_ps, y_added = (a.sem("e_" + n) for n in "h_ps h_sb y_ps y_added".split())
        block = st.enter_context(nc.Block())

        @block.tensor
        def _(pe):
            def up(u, c, e):
                if not (isinstance(u, int) and u < 2):
                    pe.wait_ge(h_sb, u * 2 - 2)
                for half in range(2):
                    mm = pe.matmul(ps_h[e % 2][:, half, :], w1[:, e, half * P:(half + 1) * P],
                                   xlnT[:, bass.ds(c * CH, CH)], start=True, stop=True)
                    mm.then_inc(h_ps, 1)

            def down(u, e):
                pe.wait_ge(h_sb, u * 2 + 2)
                if e >= 2:
                    pe.wait_ge(y_added, u * CT - CT)
                else:
                    pe.wait_ge(y_added, u * CT - CT * e)
                for t in range(CT):
                    for half in range(2):
                        mm = pe.matmul(ps_y[e % 2][:, t, :], hid[:, e % 2, half, t * P:(t + 1) * P], w2[:, e, half, :],
                                       start=(half == 0), stop=(half == 1))
                mm.then_inc(y_ps, 1)

            with pe.Fori(0, NT * P // CH) as c:
                u0 = c * E0
                for half in range(2):
                    pe.wait_ge(h_sb, u0 * 2)
                    pe.matmul(ps_h[0][:, half, :], w1[:, 0, half * P:(half + 1) * P], xlnT[:, bass.ds(c * CH, CH)],
                              start=True, stop=True).then_inc(h_ps, 1)
                for e in range(E0):
                    if e + 1 < E0:
                        if e == 0:
                            pe.wait_ge(h_sb, u0 * 2)
                            for half in range(2):
                                pe.matmul(ps_h[1][:, half, :], w1[:, 1, half * P:(half + 1) * P],
                                          xlnT[:, bass.ds(c * CH, CH)], start=True, stop=True).then_inc(h_ps, 1)
                        else:
                            up(u0 + e + 1, c, e + 1)
                    down(u0 + e, e)

        @block.scalar
        def _(act):
            with act.Fori(0, NT * P // CH) as c:
                for e in range(E0):
                    u = c * E0 + e
                    if e >= 2:
                        act.wait_ge(y_ps, u - 1)
                    else:
                        act.wait_ge(y_ps, u - e)
                    for half in range(2):
                        act.wait_ge(h_ps, u * 2 + half + 1)
                        act.activation(hid[:, e % 2, half, :], ps_h[e % 2][:, half, :], ACT.Gelu,
                                       bias=b1[:, e, half:half + 1]).then_inc(h_sb, 1)

        @block.vector
        def _(dve):
            with dve.Fori(0, NT * P // CH) as c:
                for e in range(E0):
                    u = c * E0 + e
                    dve.wait_ge(y_ps, u + 1)
                    if e:
                        dve.wait_ge(y_added, u * CT)
                    for t in range(CT):
                        x_t = x_sb[:, bass.ds(c * CT + t, 1), :].rearrange("p o e -> p (o e)")
                        w_t = weight[:, bass.ds(c * CT + t, 1), e:e + 1].rearrange("p o e -> p (o e)")
                        dve.scalar_tensor_tensor(x_t, ps_y[e % 2][:, t, :], w_t, x_t, ALU.mult,
                                                 ALU.add).then_inc(y_added, 1)
            dve.wait_ge(y_added, NT * P // CH * E0 * CT)


H1, D1 = 2, 64
PAIRS = H1 * QT
RMS_EPS = 1e-8
SCALE1 = float(D1) ** -0.5
GT = 4
LK = S // P


def l1_flags(nc, mask, scratch, flags):
    with ExitStack() as st:
        a = Alloc(nc, st)
        raw = a.sb("f_raw", [B, KEYS], U8)
        best = a.sb("f_best", [B, NW])
        seen = a.sb("f_seen", [B, NW], I32)
        loaded, steps, stored, done = a.sem("f_loaded"), a.sem("f_steps"), a.sem("f_stored"), a.sem("f_done")
        block = st.enter_context(nc.Block())

        @block.sync
        def _(sp):
            sp.dma_start(raw[:], mask).then_inc(loaded, 16)
            sp.wait_ge(steps, NW + 1)
            sp.dma_start(scratch, seen[:]).then_inc(stored, 16)
            sp.wait_ge(stored, 16)
            sp.dma_start(flags[:], scratch.rearrange("b w -> (b w)").unsqueeze(0)).then_inc(done, 16)
            sp.wait_ge(done, 16)

        @block.vector
        def _(dve):
            s = Steps(dve, steps)
            dve.wait_ge(loaded, 16)
            for w in range(NW):
                own = FIRST_OWN if w == 0 else W
                s.mark(dve.tensor_reduce(best[:, w:w + 1], raw[:, START[w]:START[w] + own], AX, ALU.max))
            s.settle()
            s.mark(dve.tensor_scalar(seen[:], best[:], 0.0, None, ALU.not_equal))


def l1_project(nc, tag, ident, gain, shift, wkv, gk, latents=None, context=None):
    NORMS = 2 if latents else 1
    with ExitStack() as st:
        a = Alloc(nc, st)
        rows = a.sb(tag + "rows", [P, GT, E]) if context else None
        stats = a.sb(tag + "stats", [P, GT, 6])
        mv = a.sb(tag + "mv", [P, GT, 2])
        var = a.sb(tag + "var", [P, GT])
        rstd = a.sb(tag + "rstd", [P, GT])
        off = a.sb(tag + "off", [P, GT])
        expo = a.sb(tag + "expo", [P, NORMS * GT * H1])
        xn = a.sb(tag + "xn", [P, GT, E])
        xnT = a.sb(tag + "xnT", [P, GT * P])
        sq = a.sb(tag + "sq", [P, NORMS, GT, E])
        ms = a.sb(tag + "ms", [P, NORMS * GT * H1])
        rms = a.sb(tag + "rms", [P, NORMS * GT * H1])
        normed_rows = a.sb(tag + "nr", [P, NORMS, GT, E])
        if context:
            kT_out = a.sb(tag + "kT_out", [P, GT * P])
            v_out = a.sb(tag + "v_out", [P, GT, E])
        ps_x = a.ps(tag + "ps_x", [P, GT, P])
        ps_k = a.ps(tag + "ps_k", [P, GT, E])
        ps_v = a.ps(tag + "ps_v", [P, GT, E])
        ps_q = a.ps(tag + "ps_q", [P, GT, E]) if latents else None
        ps_t = [a.ps(f"{tag}ps_t{i}", [P, GT, P]) for i in range(NORMS)]
        sem = {n: a.sem(tag + n) for n in (
            "loaded expo_set steps stats_ready var_ready rstd_ready xn_ready xnT_ps xnT_sb kv_ps sq_sb v_sb ms_ready rms_ready "
            "nr_ready nT_ps nT_sb k_stored v_stored").split()}
        block = st.enter_context(nc.Block())

        def each(eng, body):
            if latents:
                with eng.Fori(0, NT // GT) as g:
                    body(g, g, 0)
                return
            _, flags = context[:2]
            n = eng.alloc_register(tag + "n")
            eng.reg_mov(n, 0)
            with eng.Fori(0, B) as b:
                for w in range(NW):
                    live = eng.value_load(flags[0:1, bass.ds(b * NW + w, 1)], min_val=0, max_val=1)
                    with eng.If(live != 0):
                        body(eng.snap(n), b, w)
                        eng.reg_add(n, n, 1)

        @block.sync
        def _(sp):
            if latents:
                return
            ctx, _, kT_dram, v_dram = context
            ctx_rows = ctx.rearrange("b k e -> (b k) e")

            def body(done, b, w):
                sp.wait_ge(sem["xn_ready"], done)
                sp.dma_start(rows[:], ctx_rows[bass.ds(b * KEYS + START[w], W), :].rearrange(
                    "(t p) e -> p t e", p=P)).then_inc(sem["loaded"], 16)
            each(sp, body)

        @block.gpsimd
        def _(pool):
            pool.memset(expo[:], -0.5).then_inc(sem["expo_set"], 1)
            pool.wait_ge(sem["expo_set"], 1)
            if context:
                v_in = Awaited(pool, sem["v_sb"], tag + "v_sb_at")
                k_in = Awaited(pool, sem["nT_sb"], tag + "nT_sb_at")

            def body(done, b, w):
                pool.wait_ge(sem["var_ready"], done + 1)
                pool.tensor_tensor(rstd[:], var[:], expo[:, 0:GT], ALU.pow).then_inc(sem["rstd_ready"], 1)
                pool.wait_ge(sem["ms_ready"], done + 1)
                pool.tensor_tensor(rms[:], ms[:], expo[:], ALU.pow).then_inc(sem["rms_ready"], 1)
                if context:
                    v_in.wait()
                    pool.dma_start(context[3][bass.ds(b, 1), w, :, :].rearrange("o p c -> (o p) c"),
                                   v_out[:].rearrange("p t e -> p (t e)")).then_inc(sem["v_stored"], 16)
                    k_in.wait()
                    pool.dma_start(context[2][bass.ds(b, 1), w, :, :].rearrange("o p c -> (o p) c"),
                                   kT_out[:]).then_inc(sem["k_stored"], 16)
                    pool.wait_ge(sem["v_stored"], (done + 1) * 16)
                    pool.wait_ge(sem["k_stored"], (done + 1) * 16)
            each(pool, body)

        @block.tensor
        def _(pe):
            def body(done, b, w):
                pe.wait_ge(sem["xn_ready"], done + 1)
                for i in range(GT):
                    mm = pe.transpose(ps_x[:, i, :], xn[:, i, :], ident[:])
                mm.then_inc(sem["xnT_ps"], 1)
                pe.wait_ge(sem["xnT_sb"], done + 1)
                for bank, weights in ((ps_k, wkv[:, 0:E]), (ps_q, latents[1][:] if latents else None),
                                      (ps_v, wkv[:, E:])):
                    for i in range(GT):
                        if weights is not None:
                            mm = pe.matmul(bank[:, i, :], xnT[:, i * P:(i + 1) * P], weights, start=True, stop=True)
                mm.then_inc(sem["kv_ps"], 1)
                pe.wait_ge(sem["nr_ready"], done + 1)
                for c in range(NORMS):
                    for i in range(GT):
                        mm = pe.transpose(ps_t[c][:, i, :], normed_rows[:, c, i, :], ident[:])
                mm.then_inc(sem["nT_ps"], 1)
                pe.wait_ge(sem["nT_sb"], done + 1)
                pe.wait_ge(sem["v_sb"], done + 1)
            each(pe, body)

        @block.scalar
        def _(act):
            def body(done, b, w):
                act.wait_ge(sem["xnT_ps"], done + 1)
                act.activation(xnT[:], ps_x[:].rearrange("p t q -> p (t q)"), ACT.Identity, bias=shift[:],
                               scale=gain[:]).then_inc(sem["xnT_sb"], 1)
                act.wait_ge(sem["kv_ps"], done + 1)
                mm = act.activation(sq[:, 0, :, :], ps_k[:], ACT.Square)
                if latents:
                    mm = act.activation(sq[:, 1, :, :], ps_q[:], ACT.Square)
                mm.then_inc(sem["sq_sb"], 1)
                if context:
                    act.wait_ge(sem["v_stored"], done * 16)
                    v_to = v_out[:]
                else:
                    v_to = latents[5][:, bass.ds(b * GT, GT), :]
                act.activation(v_to, ps_v[:], ACT.Copy).then_inc(sem["v_sb"], 1)
                act.wait_ge(sem["nT_ps"], done + 1)
                if context:
                    act.wait_ge(sem["k_stored"], done * 16)
                    act.activation(kT_out[:], ps_t[0][:].rearrange("p t q -> p (t q)"), ACT.Copy,
                                   scale=gk[:]).then_inc(sem["nT_sb"], 1)
                else:
                    act.activation(latents[4][:, bass.ds(b * GT * P, GT * P)], ps_t[0][:].rearrange(
                        "p t q -> p (t q)"), ACT.Copy, scale=gk[:])
                    act.activation(latents[3][:, bass.ds(b * GT * P, GT * P)], ps_t[1][:].rearrange(
                        "p t q -> p (t q)"), ACT.Copy, scale=latents[2][:]).then_inc(sem["nT_sb"], 1)
            each(act, body)

        @block.vector
        def _(dve):
            total = dve.alloc_register(tag + "steps")
            dve.reg_mov(total, 0)
            stats_in = Awaited(dve, sem["stats_ready"], tag + "stats_at")

            def body(done, b, w):
                s = Steps(dve, sem["steps"], dve.snap(total))
                if context:
                    dve.wait_ge(sem["loaded"], (done + 1) * 16)
                    row = lambda i: rows[:, i, :]
                else:
                    row = lambda i: latents[0][:, bass.ds(b * GT + i, 1), :].rearrange("p o e -> p (o e)")
                for i in range(GT):
                    ins = dve.bn_stats(stats[:, i, :], row(i))
                ins.then_inc(sem["stats_ready"], 1)
                stats_in.wait()
                for i in range(GT):
                    s.mark(dve.bn_aggr(mv[:, i, :], stats[:, i, :]))
                s.settle()
                dve.tensor_scalar(var[:], mv[:, :, 1], EPS, None, ALU.add).then_inc(sem["var_ready"], 1)
                dve.wait_ge(sem["rstd_ready"], done + 1)
                s.mark(dve.scalar_tensor_tensor(off[:], mv[:, :, 0], -1.0, rstd[:], ALU.mult, ALU.mult))
                s.settle()
                dve.wait_ge(sem["xnT_ps"], done)
                for i in range(GT):
                    ins = dve.tensor_scalar(xn[:, i, :], row(i), rstd[:, i:i + 1], off[:, i:i + 1], ALU.mult, ALU.add)
                ins.then_inc(sem["xn_ready"], 1)
                dve.wait_ge(sem["sq_sb"], done + 1)
                s.mark(dve.tensor_reduce(ms[:], sq[:].rearrange("p c t (h d) -> p (c t h) d", d=D1), AX, ALU.add))
                s.settle()
                dve.tensor_scalar(ms[:], ms[:], 1.0 / D1, RMS_EPS ** 2, ALU.mult, ALU.max).then_inc(sem["ms_ready"], 1)
                dve.wait_ge(sem["rms_ready"], done + 1)
                dve.wait_ge(sem["nT_ps"], done)
                for c in range(NORMS):
                    from_ps = ps_k[:] if c == 0 else ps_q[:]
                    by_head = rms[:, c * GT * H1:(c + 1) * GT * H1].rearrange("p (t h) -> p t h", h=H1).unsqueeze(
                        3).broadcast_to([P, GT, H1, D1])
                    ins = dve.tensor_tensor(normed_rows[:, c, :, :].rearrange("p t (h d) -> p t h d", d=D1),
                                            from_ps.rearrange("p t (h d) -> p t h d", d=D1), by_head, ALU.mult)
                ins.then_inc(sem["nr_ready"], 1)
                dve.reg_add(total, total, s.n)
            each(dve, body)


def l1_attention(nc, x_sb, ident, flags, mask, qT, klT, vl, kT_dram, v_dram, wout, bout):
    mask_flat = mask.rearrange("b k -> (b k)")
    with ExitStack() as st:
        a = Alloc(nc, st)
        qbd = a.sb("b_qbd", [P, 2, H1, S])
        kT = a.sb("b_kT", [P, W])
        v = a.sb("b_v", [P, KT, E])
        raw = a.sb("b_raw", [P, W], U8)
        neg = a.sb("b_neg", [P, W])
        none = a.sb("b_none", [P, S])
        scores = a.sb("b_scores", [P, PAIRS, W])
        probsT = a.sb("b_probsT", [P, PAIRS, KT, P])
        m_old, m_src, m_new, m_diff, alpha, neg_m, l_src, l_sum = (
            a.sb("b_" + n, [P, PAIRS]) for n in "m_old m_src m_new m_diff alpha neg_m l_src l_sum".split())
        acc = a.sb("b_acc", [P, QT, H1, D1])
        heads = a.sb("b_heads", [P, QT, E])
        headsT = a.sb("b_headsT", [P, S])
        ps_s = [a.ps(f"b_ps_s{i}", [P, W]) for i in range(2)]
        ps_t = [a.ps(f"b_ps_t{i}", [P, KT, P]) for i in range(2)]
        ps_o = a.ps("b_ps_o", [P, QT, H1, D1])
        ps_h = a.ps("b_ps_h", [P, S])
        ps_y = a.ps("b_ps_y", [P, QT, E])
        sem = {n: a.sem("b_" + n) for n in (
            "qbd_zeroed qbd_ready k_loaded v_loaded m_loaded s_ps s_sb neg_m_ready alpha_ready p_sb t_ps t_act t_dve "
            "o_ps acc_done heads_ready headsT_ps headsT_sb y_ps x_done steps src_done").split()}
        block = st.enter_context(nc.Block())

        def each_window(eng, n, m, b, body):
            for w in range(NW):
                live = eng.value_load(flags[0:1, bass.ds(b * NW + w, 1)], min_val=0, max_val=1)
                with eng.If(live != 0):
                    body(eng.snap(n), eng.snap(m), w)
                    eng.reg_add(n, n, 1)
                    eng.reg_add(m, m, 1)

        def counters(eng):
            n, m = eng.alloc_register("b_n_sources"), eng.alloc_register("b_n_windows")
            eng.reg_mov(n, 0)
            eng.reg_mov(m, 0)
            return n, m

        @block.sync
        def _(sp):
            n, m = counters(sp)
            with sp.Fori(0, B) as b:
                sp.reg_add(n, n, 1)

                def load(src, win, w):
                    sp.wait_ge(sem["o_ps"], src)
                    sp.dma_start(kT[:], kT_dram[bass.ds(b, 1), w, :, :].rearrange("o p c -> (o p) c")).then_inc(
                        sem["k_loaded"], 16)
                    sp.dma_start(raw[:], mask_flat[bass.ds(b * KEYS + START[w], W)].partition_broadcast(P)).then_inc(
                        sem["m_loaded"], 16)
                    sp.dma_start(v[:].rearrange("p t e -> p (t e)"), v_dram[bass.ds(b, 1), w, :, :].rearrange(
                        "o p c -> (o p) c")).then_inc(sem["v_loaded"], 16)
                each_window(sp, n, m, b, load)

        @block.gpsimd
        def _(pool):
            pool.memset(qbd[:], 0.0).then_inc(sem["qbd_zeroed"], 1)
            pool.wait_ge(sem["qbd_zeroed"], 1)

            def spread(b, half):
                pool.wait_ge(sem["headsT_ps"], b - half)
                for h in range(H1):
                    rows = slice(h * D1, (h + 1) * D1)
                    ins = pool.tensor_copy(qbd[rows, half, h, :], qT[rows, bass.ds(b * S, S)])
                    ins.then_inc(sem["qbd_ready"], 1)
            with pool.Fori(0, B // 2) as i:
                spread(i * 2, 0)
                spread(i * 2 + 1, 1)

        @block.tensor
        def _(pe):
            n, m = counters(pe)

            def source(src, half, tiles, key, value):
                for j in range(PAIRS):
                    h, t = j // QT, j % QT
                    pe.wait_ge(sem["s_sb"], src * PAIRS + max(j - 1, 0))
                    pe.matmul(ps_s[j % 2][:, 0:tiles * P], qbd[:, half, h, t * P:(t + 1) * P], key, start=True,
                              stop=True).then_inc(sem["s_ps"], 1)
                for j in range(PAIRS):
                    pe.wait_ge(sem["p_sb"], src * PAIRS + j + 1)
                    pe.wait_ge(sem["t_act" if j % 2 == 0 else "t_dve"], src * (PAIRS // 2) + j // 2)
                    for k in range(tiles):
                        mm = pe.transpose(ps_t[j % 2][:, k, :], scores[:, j, k * P:(k + 1) * P], ident[:])
                    mm.then_inc(sem["t_ps"], 1)
                pe.wait_ge(sem["acc_done"], src)
                for j in range(PAIRS):
                    h, t = j // QT, j % QT
                    pe.wait_ge(sem["t_act" if j % 2 == 0 else "t_dve"], src * (PAIRS // 2) + j // 2 + 1)
                    for k in range(tiles):
                        mm = pe.matmul(ps_o[:, t, h, :], probsT[:, j, k, :], value(k, h), start=(k == 0),
                                       stop=(k == tiles - 1))
                mm.then_inc(sem["o_ps"], 1)

            def batch(b, half):
                pe.wait_ge(sem["qbd_ready"], b * H1 + H1)
                source(pe.snap(n), half, LK, klT[:, bass.ds(b * S, S)],
                       lambda k, h: vl[:, bass.ds(b * LK + k, 1), h * D1:(h + 1) * D1].rearrange("p o d -> p (o d)"))
                pe.reg_add(n, n, 1)

                def window(src, win, w):
                    pe.wait_ge(sem["k_loaded"], (win + 1) * 16)
                    pe.wait_ge(sem["v_loaded"], (win + 1) * 16)
                    source(src, half, KT, kT[:], lambda k, h: v[:, k, h * D1:(h + 1) * D1])
                each_window(pe, n, m, b, window)
                pe.wait_ge(sem["heads_ready"], b + 1)
                for t in range(QT):
                    mm = pe.transpose(ps_h[:, t * P:(t + 1) * P], heads[:, t, :], ident[:])
                mm.then_inc(sem["headsT_ps"], 1)
                pe.wait_ge(sem["headsT_sb"], b + 1)
                pe.wait_ge(sem["x_done"], b)
                for t in range(QT):
                    mm = pe.matmul(ps_y[:, t, :], headsT[:, t * P:(t + 1) * P], wout[:], start=True, stop=True)
                mm.then_inc(sem["y_ps"], 1)

            with pe.Fori(0, B // 2) as i:
                batch(i * 2, 0)
                batch(i * 2 + 1, 1)

        @block.scalar
        def _(act):
            n, m = counters(act)

            def source(src, tiles):
                act.wait_ge(sem["neg_m_ready"], src + 1)
                act.wait_ge(sem["acc_done"], src)
                act.activation(alpha[:], m_diff[:], ACT.Exp).then_inc(sem["alpha_ready"], 1)
                for j in range(PAIRS):
                    act.activation(scores[:, j, 0:tiles * P], scores[:, j, 0:tiles * P], ACT.Exp,
                                   bias=neg_m[:, j:j + 1], accum_out=l_src[:, j:j + 1]).then_inc(sem["p_sb"], 1)
                    if j % 2:
                        act.wait_ge(sem["t_ps"], src * PAIRS + j)
                        act.wait_ge(sem["o_ps"], src)
                        act.activation(probsT[:, j - 1, 0:tiles, :], ps_t[0][:, 0:tiles, :],
                                       ACT.Copy).then_inc(sem["t_act"], 1)

            with act.Fori(0, B) as b:
                source(act.snap(n), LK)
                act.reg_add(n, n, 1)
                each_window(act, n, m, b, lambda src, win, w: source(src, KT))
                act.wait_ge(sem["headsT_ps"], b + 1)
                act.wait_ge(sem["y_ps"], b)
                act.activation(headsT[:], ps_h[:], ACT.Copy).then_inc(sem["headsT_sb"], 1)

        @block.vector
        def _(dve):
            n, m = counters(dve)
            total = dve.alloc_register("b_n_steps")
            dve.reg_mov(total, 0)
            scores_in = Awaited(dve, sem["s_ps"], "b_s_ps_at")
            dve.memset(none[:], 0.0).then_inc(sem["steps"], 1)
            dve.reg_add(total, total, 1)

            def source(src, s, tiles, added):
                for j in range(PAIRS):
                    at = scores_in.at()
                    if j == 0:
                        dve.wait_ge(sem["t_ps"], src * PAIRS)
                    scores_in.wait(at)
                    dve.tensor_tensor_reduce(scores[:, j, 0:tiles * P], ps_s[j % 2][:, 0:tiles * P], added, 1.0,
                                             NO_MAX, ALU.add, ALU.max, m_src[:, j:j + 1]).then_inc(sem["s_sb"], 1)
                dve.wait_ge(sem["s_sb"], src * PAIRS + PAIRS)
                s.mark(dve.tensor_tensor(m_new[:], m_old[:], m_src[:], ALU.max))
                s.settle()
                s.mark(dve.tensor_tensor(m_diff[:], m_old[:], m_new[:], ALU.subtract))
                s.settle()
                s.mark(dve.tensor_copy(m_old[:], m_new[:]))
                dve.tensor_scalar(neg_m[:], m_new[:], -1.0, None, ALU.mult).then_inc(sem["neg_m_ready"], 1)
                for j in range(1, PAIRS, 2):
                    dve.wait_ge(sem["t_ps"], src * PAIRS + j + 1)
                    dve.wait_ge(sem["o_ps"], src)
                    dve.tensor_copy(probsT[:, j, 0:tiles, :], ps_t[1][:, 0:tiles, :]).then_inc(sem["t_dve"], 1)
                dve.wait_ge(sem["alpha_ready"], src + 1)
                dve.wait_ge(sem["p_sb"], src * PAIRS + PAIRS)
                by_head = alpha[:].rearrange("p (h t) -> p t h", t=QT).unsqueeze(3).broadcast_to([P, QT, H1, D1])
                dve.wait_ge(sem["acc_done"], src)
                s.mark(dve.tensor_tensor(l_sum[:], l_sum[:], alpha[:], ALU.mult))
                s.mark(dve.tensor_tensor(acc[:], acc[:], by_head, ALU.mult))
                s.settle()
                s.mark(dve.tensor_tensor(l_sum[:], l_sum[:], l_src[:], ALU.add))
                dve.wait_ge(sem["o_ps"], src + 1)
                dve.tensor_tensor(acc[:], acc[:], ps_o[:], ALU.add).then_inc(sem["acc_done"], 1)
                s.settle()

            with dve.Fori(0, B) as b:
                s = Steps(dve, sem["steps"], dve.snap(total))
                s.mark(dve.memset(m_old[:], NO_MAX))
                s.mark(dve.memset(l_sum[:], 0.0))
                s.mark(dve.memset(acc[:], 0.0))
                s.settle()
                source(dve.snap(n), s, LK, none[:])
                dve.reg_add(n, n, 1)
                dve.reg_add(total, total, s.n)

                def window(src, win, w):
                    s = Steps(dve, sem["steps"], dve.snap(total))
                    dve.wait_ge(sem["m_loaded"], (win + 1) * 16)
                    own = FIRST_OWN if w == 0 else W
                    s.mark(dve.tensor_scalar(neg[:, 0:own], raw[:, 0:own], 0.0, MASKED, ALU.is_equal, ALU.mult))
                    if own < W:
                        s.mark(dve.memset(neg[:, own:], DOUBLED))
                    s.settle()
                    source(src, s, KT, neg[:])
                    dve.reg_add(total, total, s.n)
                each_window(dve, n, m, b, window)
                s = Steps(dve, sem["steps"], dve.snap(total))
                dve.wait_ge(sem["acc_done"], dve.snap(n))
                s.mark(dve.reciprocal(l_sum[:], l_sum[:]))
                s.settle()
                by_head = l_sum[:].rearrange("p (h t) -> p t h", t=QT).unsqueeze(3).broadcast_to([P, QT, H1, D1])
                dve.wait_ge(sem["headsT_ps"], b)
                dve.tensor_tensor(heads[:].rearrange("p t (h d) -> p t h d", d=D1), acc[:], by_head,
                                  ALU.mult).then_inc(sem["heads_ready"], 1)
                dve.wait_ge(sem["y_ps"], b + 1)
                x_b = x_sb[:, bass.ds(b * QT, QT), :]
                s.mark(dve.tensor_tensor(x_b, x_b, ps_y[:], ALU.add))
                s.settle()
                dve.tensor_tensor(x_b, x_b, bout[:].unsqueeze(1).broadcast_to([P, QT, E]),
                                  ALU.add).then_inc(sem["x_done"], 1)
                dve.reg_add(total, total, s.n)
            dve.wait_ge(sem["x_done"], B)


E1, I1 = 32, 256
TILES = NT + E1 - 1
TP = -(-TILES // 2)
SLOTS = 2 * TP * P


def l1_route(nc, xln, xlnT, gate, position, expert_of, n_tiles):
    with ExitStack() as st:
        a = Alloc(nc, st)
        best = a.sb("g_best", [P, NT])
        score = a.sb("g_score", [P, NT])
        choice = a.sb("g_choice", [P, NT])
        num = a.sb("g_num", [P, E1], I32)
        num_f = a.sb("g_num_f", [P, E1])
        mark = a.sb("g_mark", [P, NT, E1])
        hot = a.sb("g_hot", [P, NT, E1], BF16)
        below = a.sb("g_below", [P, P], BF16)
        ones = a.sb("g_ones", [P, P], BF16)
        before = [a.sb(f"g_before{i}", [P, NT, E1]) for i in range(2)]
        size = a.sb("g_size", [P, E1])
        tiles_of = a.sb("g_tiles_of", [P, E1])
        end = [a.sb(f"g_end{i}", [P, E1]) for i in range(2)]
        slot = a.sb("g_slot", [P, NT])
        tile_num = a.sb("g_tile_num", [1, 2 * TP], I32)
        tile_num_f = a.sb("g_tile_num_f", [1, 2 * TP])
        past = a.sb("g_past", [1, 2 * TP, E1])
        tile_expert = a.sb("g_tile_expert", [1, 2 * TP])
        ps_l = a.ps("g_ps_l", [P, NT, E1])
        ps_r = a.ps("g_ps_r", [P, NT, E1])
        ps_c = a.ps("g_ps_c", [P, NT, E1])
        logits, consts, best_ready, scored, hot_ready, counted, steps = (
            a.sem("g_s_" + n) for n in "logits consts best scored hot counted steps".split())
        block = st.enter_context(nc.Block())
        HALF = NT // 2

        @block.gpsimd
        def _(pool):
            pool.iota(num[:], [[1, E1]], base=0, channel_multiplier=0).then_inc(consts, 1)
            pool.iota(tile_num[:], [[1, 2 * TP]], base=0, channel_multiplier=0).then_inc(consts, 1)
            pool.memset(ones[:], 1.0).then_inc(consts, 1)
            pool.memset(below[:], 1.0).then_inc(consts, 1)
            pool.wait_ge(consts, 4)
            pool.affine_select(out=below[:], in_=below[:], compare_op=ALU.is_gt, fill=0.0, base=0,
                               pattern=[[1, P]], channel_multiplier=-1).then_inc(consts, 1)

        @block.tensor
        def _(pe):
            for t in range(NT):
                mm = pe.matmul(ps_l[:, t, :], xlnT[:, t * P:(t + 1) * P], gate[:], start=True, stop=True)
            mm.then_inc(logits, 1)
            pe.wait_ge(hot_ready, 1)
            pe.wait_ge(consts, 5)
            for i in range(2):
                pe.matmul(ps_r[:, i * HALF:(i + 1) * HALF, :], below[:], hot[:, i * HALF:(i + 1) * HALF, :],
                          start=True, stop=True)
                mm = pe.matmul(ps_c[:, i * HALF:(i + 1) * HALF, :], ones[:], hot[:, i * HALF:(i + 1) * HALF, :],
                               start=True, stop=True)
            mm.then_inc(counted, 1)

        @block.scalar
        def _(act):
            act.wait_ge(best_ready, 1)
            act.activation(score[:], best[:], ACT.Sigmoid).then_inc(scored, 1)

        @block.vector
        def _(dve):
            s = Steps(dve, steps)
            full = [P, NT, E1]
            dve.wait_ge(logits, 1)
            dve.tensor_reduce(best[:], ps_l[:], AX, ALU.max).then_inc(best_ready, 1)
            dve.wait_ge(best_ready, 1)
            dve.wait_ge(consts, 5)
            s.mark(dve.tensor_copy(num_f[:], num[:]))
            s.mark(dve.tensor_copy(tile_num_f[:], tile_num[:]))
            s.mark(dve.tensor_tensor(mark[:], ps_l[:], best[:].unsqueeze(2).broadcast_to(full), ALU.is_equal))
            s.settle()
            s.mark(dve.tensor_scalar(size[:], num_f[:], -float(E1), None, ALU.add))
            s.settle()
            s.mark(dve.tensor_tensor(mark[:], mark[:], size[:].unsqueeze(1).broadcast_to(full), ALU.mult))
            s.settle()
            s.mark(dve.tensor_reduce(choice[:], mark[:], AX, ALU.min))
            s.settle()
            s.mark(dve.tensor_scalar(choice[:], choice[:], float(E1), None, ALU.add))
            s.settle()
            dve.tensor_tensor(hot[:], num_f[:].unsqueeze(1).broadcast_to(full),
                              choice[:].unsqueeze(2).broadcast_to(full), ALU.is_equal).then_inc(hot_ready, 1)
            dve.wait_ge(scored, 1)
            s.mark(dve.tensor_tensor(xln[:], xln[:], score[:].unsqueeze(2).broadcast_to([P, NT, E]), ALU.mult))
            dve.wait_ge(counted, 1)
            s.mark(dve.tensor_copy(before[0][:], ps_c[:]))
            s.settle()
            step, cur = 1, 0
            while step < NT:
                s.mark(dve.tensor_copy(before[1 - cur][:, 0:step, :], before[cur][:, 0:step, :]))
                s.mark(dve.tensor_tensor(before[1 - cur][:, step:, :], before[cur][:, step:, :],
                                         before[cur][:, 0:NT - step, :], ALU.add))
                s.settle()
                cur, step = 1 - cur, step * 2
            s.mark(dve.tensor_copy(size[:], before[cur][:, NT - 1, :]))
            s.settle()
            s.mark(dve.tensor_scalar(end[0][:], num_f[:], float(P), None, ALU.mult))
            s.settle()
            s.mark(dve.tensor_tensor(mark[:, 0:E1, :], size[:].unsqueeze(2).broadcast_to([P, E1, NT]),
                                     end[0][:].unsqueeze(1).broadcast_to([P, E1, NT]), ALU.is_gt))
            s.settle()
            s.mark(dve.tensor_reduce(tiles_of[:], mark[:], AX, ALU.add))
            s.settle()
            s.mark(dve.tensor_copy(end[0][:], tiles_of[:]))
            s.settle()
            step, at = 1, 0
            while step < E1:
                s.mark(dve.tensor_copy(end[1 - at][:, 0:step], end[at][:, 0:step]))
                s.mark(dve.tensor_tensor(end[1 - at][:, step:], end[at][:, step:], end[at][:, 0:E1 - step], ALU.add))
                s.settle()
                at, step = 1 - at, step * 2
            s.mark(dve.tensor_tensor(past[:], end[at][0:1, :].unsqueeze(1).broadcast_to([1, 2 * TP, E1]),
                                     tile_num_f[:].unsqueeze(2).broadcast_to([1, 2 * TP, E1]), ALU.is_le))
            s.mark(dve.tensor_copy(n_tiles[:], end[at][0:1, E1 - 1:E1]))
            s.mark(dve.tensor_tensor(size[:], end[at][:], tiles_of[:], ALU.subtract))
            s.settle()
            s.mark(dve.tensor_reduce(tile_expert[:], past[:], AX, ALU.add))
            s.mark(dve.tensor_scalar(size[:], size[:], float(P), None, ALU.mult))
            s.mark(dve.tensor_tensor(before[cur][:], before[cur][:], ps_c[:], ALU.subtract))
            s.settle()
            s.mark(dve.tensor_scalar(expert_of[:], tile_expert[:], float(E1 - 1), None, ALU.min))
            s.mark(dve.tensor_tensor(before[cur][:], before[cur][:], ps_r[:], ALU.add))
            s.settle()
            s.mark(dve.tensor_tensor(before[cur][:], before[cur][:], size[:].unsqueeze(1).broadcast_to(full), ALU.add))
            s.settle()
            s.mark(dve.tensor_tensor(before[cur][:], before[cur][:], hot[:], ALU.mult))
            s.settle()
            s.mark(dve.tensor_reduce(slot[:], before[cur][:], AX, ALU.add))
            s.settle()
            s.mark(dve.tensor_copy(position[:], slot[:]))
            s.settle()


def l1_scatter(nc, xln, position, sorted_x, sorted_y):
    with ExitStack() as st:
        a = Alloc(nc, st)
        zeros = a.sb("z_zeros", [P, 8, E])
        zero_ready, cleared, sent = a.sem("z_ready"), a.sem("z_cleared"), a.sem("z_sent")
        block = st.enter_context(nc.Block())
        parts = SLOTS // P // 8

        @block.vector
        def _(dve):
            dve.memset(zeros[:], 0.0).then_inc(zero_ready, 1)

        @block.sync
        def _(sp):
            sp.wait_ge(zero_ready, 1)
            for i in range(parts):
                for table in (sorted_x, sorted_y):
                    sp.dma_start(table[i * 8 * P:(i + 1) * 8 * P, :].rearrange("(p t) e -> p t e", p=P),
                                 zeros[:]).then_inc(cleared, 16)
            sp.wait_ge(cleared, 32 * parts)

        @block.gpsimd
        def _(pool):
            pool.wait_ge(cleared, 32 * parts)
            for t in range(NT):
                pool.indirect_dma_start(sorted_x, bass.IndirectOffsetOnAxis(ap=position[:, t:t + 1], axis=0),
                                        xln[:, t, :], None).then_inc(sent, 16)
            pool.wait_ge(sent, 16 * NT)


def l1_shared(nc, x_sb, xlnT, wgu, wd):
    with ExitStack() as st:
        a = Alloc(nc, st)
        act_g = a.sb("s_act_g", [P, 2, CH])
        hid = a.sb("s_hid", [P, 2, CH])
        ps_g = a.ps("s_ps_g", [P, 2, CH])
        ps_u = a.ps("s_ps_u", [P, 2, CH])
        ps_y = [a.ps(f"s_ps_y{i}", [P, CT, E]) for i in range(1)]
        g_ps, u_ps, g_sb, hid_ready, y_ps, y_added = (a.sem("s_" + n) for n in "g_ps u_ps g_sb hid y_ps y_added".split())
        block = st.enter_context(nc.Block())
        CHUNKS = NT * P // CH

        @block.tensor
        def _(pe):
            with pe.Fori(0, CHUNKS) as c:
                for bank, off, free, seen in ((ps_g, 0, g_sb, g_ps), (ps_u, I1, hid_ready, u_ps)):
                    pe.wait_ge(free, c * 2)
                    for half in range(2):
                        pe.matmul(bank[:, half, :], wgu[:, off + half * P:off + (half + 1) * P],
                                  xlnT[:, bass.ds(c * CH, CH)], start=True, stop=True).then_inc(seen, 1)
                pe.wait_ge(hid_ready, c * 2 + 2)
                pe.wait_ge(y_added, c)
                for t in range(CT):
                    for half in range(2):
                        mm = pe.matmul(ps_y[0][:, t, :], hid[:, half, t * P:(t + 1) * P], wd[:, half, :],
                                       start=(half == 0), stop=(half == 1))
                mm.then_inc(y_ps, 1)

        @block.scalar
        def _(act):
            with act.Fori(0, CHUNKS) as c:
                for half in range(2):
                    act.wait_ge(g_ps, c * 2 + half + 1)
                    act.wait_ge(hid_ready, c * 2)
                    act.activation(act_g[:, half, :], ps_g[:, half, :], ACT.Silu).then_inc(g_sb, 1)

        @block.vector
        def _(dve):
            with dve.Fori(0, CHUNKS) as c:
                for half in range(2):
                    dve.wait_ge(g_sb, c * 2 + half + 1)
                    dve.wait_ge(u_ps, c * 2 + half + 1)
                    dve.wait_ge(y_ps, c)
                    dve.tensor_tensor(hid[:, half, :], act_g[:, half, :], ps_u[:, half, :],
                                      ALU.mult).then_inc(hid_ready, 1)
                dve.wait_ge(y_ps, c + 1)
                x_c = x_sb[:, bass.ds(c * CT, CT), :]
                dve.tensor_tensor(x_c, x_c, ps_y[0][:], ALU.add).then_inc(y_added, 1)
            dve.wait_ge(y_added, CHUNKS)


def l1_routed(nc, ident, sorted_x, sorted_y, wgu, wd, expert_of, n_tiles):
    with ExitStack() as st:
        a = Alloc(nc, st)
        rows = a.sb("x_rows", [P, 2, 2, E])
        rowsT = a.sb("x_rowsT", [P, 2, 2, P])
        act_g = a.sb("x_act_g", [P, 2, 2, I1])
        hid = a.sb("x_hid", [P, 2, 2, I1])
        hidT = a.sb("x_hidT", [P, 2, 2, 2, P])
        y = a.sb("x_y", [P, 2, 2, E])
        ps_t = a.ps("x_ps_t", [P, 2, P])
        ps_gu = [a.ps(f"x_ps_gu{i}", [P, 2, 2 * I1]) for i in range(2)]
        ps_h = a.ps("x_ps_h", [P, 2, 2, P])
        ps_y = a.ps("x_ps_y", [P, 2, E])
        sem = {n: a.sem("x_" + n) for n in (
            "loaded0 loaded1 rowsT_ps rowsT_sb gu_ps act_ready hid_ready hidT_ps hidT_sb y_ps y_sb stored").split()}
        block = st.enter_context(nc.Block())

        def first(i):
            return isinstance(i, int) and i == 0

        def pipeline(eng, enter, leave):
            count = eng.value_load(n_tiles[0:1, 0:1], min_val=NT, max_val=TILES)
            enter(0, 0)
            with eng.Fori(0, TP // 2 - 1) as j:
                for half in range(2):
                    i = j * 2 + half
                    with eng.If(count > (i + 1) * 2):
                        enter(i + 1, 1 - half)
                    with eng.If(count > i * 2):
                        leave(i, half)
            with eng.If(count > (TP - 1) * 2):
                enter(TP - 1, 1)
            with eng.If(count > (TP - 2) * 2):
                leave(TP - 2, 0)
            with eng.If(count > (TP - 1) * 2):
                leave(TP - 1, 1)

        @block.sync
        def _(sp):
            def load(i, half):
                if not first(i):
                    sp.wait_ge(sem["rowsT_ps"], i - 1)
                sp.dma_start(rows[:, half, :, :], sorted_x[bass.ds(i * 2 * P, 2 * P), :].rearrange(
                    "(t p) e -> p t e", p=P)).then_inc(sem[f"loaded{half}"], 16)

            def store(i, half):
                sp.wait_ge(sem["stored"], i * 16)
                sp.wait_ge(sem["y_sb"], i + 1)
                sp.dma_start(sorted_y[bass.ds(i * 2 * P, 2 * P), :].rearrange("(t p) e -> p t e", p=P),
                             y[:, half, :, :]).then_inc(sem["stored"], 16)
            pipeline(sp, load, store)

        @block.tensor
        def _(pe):
            def up(i, half):
                pe.wait_ge(sem[f"loaded{half}"], (i - half) * 8 + 16)
                if not first(i):
                    pe.wait_ge(sem["rowsT_sb"], i)
                for t in range(2):
                    mm = pe.transpose(ps_t[:, t, :], rows[:, half, t, :], ident[:])
                mm.then_inc(sem["rowsT_ps"], 1)
                pe.wait_ge(sem["rowsT_sb"], i + 1)
                if not first(i):
                    pe.wait_ge(sem["hid_ready"], i - 1)
                for t in range(2):
                    e = pe.value_load(expert_of[0:1, bass.ds(i * 2 + t, 1)], min_val=0, max_val=E1 - 1)
                    mm = pe.matmul(ps_gu[half][:, t, :], rowsT[:, half, t, :],
                                   wgu[:, bass.ds(e, 1), :].rearrange("p o c -> p (o c)"), start=True, stop=True)
                mm.then_inc(sem["gu_ps"], 1)

            def down(i, half):
                pe.wait_ge(sem["hid_ready"], i + 1)
                pe.wait_ge(sem["hidT_sb"], i)
                for t in range(2):
                    for k in range(2):
                        mm = pe.transpose(ps_h[:, t, k, :], hid[:, half, t, k * P:(k + 1) * P], ident[:])
                mm.then_inc(sem["hidT_ps"], 1)
                pe.wait_ge(sem["hidT_sb"], i + 1)
                pe.wait_ge(sem["y_sb"], i)
                for t in range(2):
                    e = pe.value_load(expert_of[0:1, bass.ds(i * 2 + t, 1)], min_val=0, max_val=E1 - 1)
                    for k in range(2):
                        mm = pe.matmul(ps_y[:, t, :], hidT[:, half, t, k, :],
                                       wd[:, bass.ds(e, 1), k, :].rearrange("p o c -> p (o c)"), start=(k == 0),
                                       stop=(k == 1))
                mm.then_inc(sem["y_ps"], 1)
            pipeline(pe, up, down)

        @block.scalar
        def _(act):
            def up(i, half):
                act.wait_ge(sem["gu_ps"], i + 1)
                if not first(i):
                    act.wait_ge(sem["hid_ready"], i - 1)
                act.activation(act_g[:, half, :, :], ps_gu[half][:, :, 0:I1], ACT.Silu).then_inc(sem["act_ready"], 1)

            def down(i, half):
                act.wait_ge(sem["hidT_ps"], i + 1)
                act.activation(hidT[:, half, :, :, :], ps_h[:], ACT.Copy).then_inc(sem["hidT_sb"], 1)
            pipeline(act, up, down)

        @block.vector
        def _(dve):
            def up(i, half):
                dve.wait_ge(sem["rowsT_ps"], i + 1)
                if not first(i):
                    dve.wait_ge(sem["gu_ps"], i - 1)
                dve.tensor_copy(rowsT[:, half, :, :], ps_t[:]).then_inc(sem["rowsT_sb"], 1)
                dve.wait_ge(sem["act_ready"], i + 1)
                if not first(i):
                    dve.wait_ge(sem["hidT_ps"], i - 1)
                dve.tensor_tensor(hid[:, half, :, :], act_g[:, half, :, :], ps_gu[half][:, :, I1:],
                                  ALU.mult).then_inc(sem["hid_ready"], 1)

            def down(i, half):
                dve.wait_ge(sem["y_ps"], i + 1)
                dve.wait_ge(sem["stored"], (i - half) * 16)
                dve.tensor_copy(y[:, half, :, :], ps_y[:]).then_inc(sem["y_sb"], 1)
            pipeline(dve, up, down)

        @block.gpsimd
        def _(pool):
            count = pool.value_load(n_tiles[0:1, 0:1], min_val=NT, max_val=TILES)
            pool.wait_ge(sem["stored"], (count + 1) // 2 * 16)


def l1_gather(nc, x_sb, got, position, sorted_y, out):
    with ExitStack() as st:
        a = Alloc(nc, st)
        fetched, added, stored = a.sem("o_fetched"), a.sem("o_added"), a.sem("o_stored")
        block = st.enter_context(nc.Block())

        @block.gpsimd
        def _(pool):
            for t in range(NT):
                pool.indirect_dma_start(got[:, t, :], None, sorted_y,
                                        bass.IndirectOffsetOnAxis(ap=position[:, t:t + 1], axis=0)).then_inc(fetched, 16)
            pool.wait_ge(fetched, 16 * NT)

        @block.vector
        def _(dve):
            dve.wait_ge(fetched, 16 * NT)
            for g in range(4):
                part = slice(g * NT // 4, (g + 1) * NT // 4)
                dve.tensor_tensor(x_sb[:, part, :], x_sb[:, part, :], got[:, part, :], ALU.add).then_inc(added, 1)

        @block.sync
        def _(sp):
            for g in range(4):
                sp.wait_ge(added, g + 1)
                part = slice(g * NT // 4, (g + 1) * NT // 4)
                sp.dma_start(out.rearrange("b (t p) e -> p (b t) e", p=P)[:, part, :],
                             x_sb[:, part, :]).then_inc(stored, 16)
            sp.wait_ge(stored, 64)


_IN = ["x", "ctx_1024", "mask_SxS2_ik0", "mask_BxS2_bk0", "L0_xattn_Wk", "L0_xattn_bk", "L0_xattn_Wq", "L0_xattn_bq",
       "L0_xattn_Wv", "L0_xattn_bv", "L0_xattn_Wp", "L0_xattn_bp", "L0_ffn_router_w", "L0_ffn_router_b", "L0_ffn_w1",
       "L0_ffn_b1", "L0_ffn_w2", "L0_ffn_b2", "L1_xattn_ln_x_g", "L1_xattn_ln_x_b", "L1_xattn_ln_l_g",
       "L1_xattn_ln_l_b", "L1_xattn_q_gamma", "L1_xattn_k_gamma", "L1_xattn_W_q", "L1_xattn_W_kv", "L1_xattn_W_out",
       "L1_xattn_b_out", "L1_ffn_gate_w", "L1_ffn_shared_gate_w", "L1_ffn_shared_up_w", "L1_ffn_shared_down_w",
       "L1_ffn_routed_gate_w", "L1_ffn_routed_up_w", "L1_ffn_routed_down_w"]


def scale_column(nc, column, factor):
    with ExitStack() as st:
        done = Alloc(nc, st).sem("column_scaled")
        block = st.enter_context(nc.Block())

        @block.vector
        def _(dve):
            dve.tensor_scalar(column, column, factor, None, ALU.mult).then_inc(done, 1)
            dve.wait_ge(done, 1)


def build_program(nc, d, out):
    flag_scratch = nc.dram_tensor("flag_scratch", (B, NW), I32, kind="Internal").ap()
    kT_scratch = nc.dram_tensor("kT_scratch", (B, NW, P, W), F32, kind="Internal").ap()
    v_scratch = nc.dram_tensor("v_scratch", (B, NW, P, W), F32, kind="Internal").ap()
    sorted_x = nc.dram_tensor("sorted_x", (SLOTS, E), F32, kind="Internal").ap()
    sorted_y = nc.dram_tensor("sorted_y", (SLOTS, E), F32, kind="Internal").ap()
    with ExitStack() as whole:
        keep = Alloc(nc, whole)
        x_sb = keep.sb("x_sb", [P, NT, E])
        xln = keep.sb("xln", [P, NT, E])
        ident = keep.sb("ident", [P, P])
        load_tokens(nc, d["x"], x_sb, ident)

        with ExitStack() as st:
            a = Alloc(nc, st)
            xlnT = a.sb("xlnT0", [P, NT * P])
            mneg = a.sb("mneg", [P, QT, NW, W])
            flags = a.sb("flags0", [1, NW], I32)
            wqT, wkT, wvT, wpT, bv, bp = (a.sb("a0" + n, [P, P]) for n in "wqT wkT wvT wpT bv bp".split())
            bq, bk = a.sb("a0bq", [P, 1]), a.sb("a0bk", [P, 1])
            turn_weights(nc, "w0", [(d["L0_xattn_Wq"], wqT[:]), (d["L0_xattn_Wk"], wkT[:]), (d["L0_xattn_Wv"], wvT[:]),
                                    (d["L0_xattn_Wp"], wpT[:])], ident,
                         columns=[(d["L0_xattn_bq"], bq[:]), (d["L0_xattn_bk"], bk[:])],
                         rows=[(d["L0_xattn_bv"], bv[:]), (d["L0_xattn_bp"], bp[:])])
            layer_norm(nc, "ln0", x_sb, xln, NT, xlnT, ident)
            l0_mask(nc, d["mask_SxS2_ik0"], mneg, flags, ident)
            l0_attention(nc, x_sb, xlnT, mneg, flags, ident, d["ctx_1024"], (wqT, wkT, wvT, wpT, bq, bk, bv, bp))

        with ExitStack() as st:
            a = Alloc(nc, st)
            xlnT = a.sb("xlnT1", [P, NT * P])
            rw, rb = a.sb("rw", [P, E0]), a.sb("rb", [P, E0])
            w1, w2 = a.sb("w1", [P, E0, I0]), a.sb("w2", [P, E0, 2, E])
            b1, b2 = a.sb("b1", [P, E0, 2]), a.sb("b2", [E0, E])
            weight = a.sb("weight", [P, NT, E0])
            with nc.allow_non_contiguous_dma(reason="biases by feature, 16 KB in all"):
                turn_weights(nc, "wf0", [], ident, rows=[(d["L0_ffn_router_b"], rb[:])], others=[
                    (d["L0_ffn_router_w"], rw[:]), (d["L0_ffn_b2"], b2[:]),
                    (d["L0_ffn_w1"].rearrange("e h i -> h e i"), w1[:]),
                    (d["L0_ffn_w2"].rearrange("e (t p) h -> p e t h", p=P), w2[:]),
                    (d["L0_ffn_b1"].rearrange("e (t p) -> p e t", p=P), b1[:])])
            layer_norm(nc, "ln1", x_sb, xln, NT, xlnT, ident)
            l0_router(nc, x_sb, xlnT, ident, rw, rb, b2, weight)
            l0_experts(nc, x_sb, xlnT, w1, b1, w2, weight)

        with ExitStack() as st:
            a = Alloc(nc, st)
            flags = a.sb("flags1", [1, B * NW], I32)
            ctx_gain, ctx_shift, lat_gain, lat_shift, gq, gk = (
                a.sb("a1" + n, [P, 1]) for n in "ctx_gain ctx_shift lat_gain lat_shift gq gk".split())
            wq, wkv, wout, bout = a.sb("wq", [P, E]), a.sb("wkv", [P, 2 * E]), a.sb("wout", [P, E]), a.sb("bout", [P, E])
            qT, klT, vl = a.sb("qT1", [P, NT * P]), a.sb("klT", [P, NT * P]), a.sb("vl", [P, NT, E])
            turn_weights(nc, "w1", [], ident, columns=[
                (d["L1_xattn_ln_x_g"], ctx_gain[:]), (d["L1_xattn_ln_x_b"], ctx_shift[:]),
                (d["L1_xattn_ln_l_g"], lat_gain[:]), (d["L1_xattn_ln_l_b"], lat_shift[:]),
                (d["L1_xattn_k_gamma"], gk[0:D1, :]), (d["L1_xattn_k_gamma"], gk[D1:, :]),
                (d["L1_xattn_q_gamma"], gq[0:D1, :]), (d["L1_xattn_q_gamma"], gq[D1:, :])],
                rows=[(d["L1_xattn_b_out"], bout[:])],
                others=[(d["L1_xattn_W_q"], wq[:]), (d["L1_xattn_W_kv"], wkv[:]), (d["L1_xattn_W_out"], wout[:])])
            scale_column(nc, gq[:], SCALE1)
            l1_flags(nc, d["mask_BxS2_bk0"], flag_scratch, flags)
            l1_project(nc, "c_", ident, ctx_gain, ctx_shift, wkv, gk,
                       context=(d["ctx_1024"], flags, kT_scratch, v_scratch))
            layer_norm(nc, "ln2", x_sb, xln, NT)
            l1_project(nc, "l_", ident, lat_gain, lat_shift, wkv, gk, latents=(xln, wq, gq, qT, klT, vl))
            l1_attention(nc, x_sb, ident, flags, d["mask_BxS2_bk0"], qT, klT, vl, kT_scratch, v_scratch, wout, bout)

        with ExitStack() as st:
            a = Alloc(nc, st)
            xlnT = a.sb("xlnT3", [P, NT * P])
            gate, shared_gu, shared_d = a.sb("gate", [P, E1]), a.sb("shared_gu", [P, 2 * I1]), a.sb("shared_d", [P, 2, E])
            wgu, wd = a.sb("wgu", [P, E1, 2 * I1]), a.sb("wd", [P, E1, 2, E])
            position = a.sb("position", [P, NT], U32)
            expert_of, n_tiles = a.sb("expert_of", [1, 2 * TP], I32), a.sb("n_tiles", [1, 1], I32)
            turn_weights(nc, "wf1", [], ident, others=[
                (d["L1_ffn_gate_w"], gate[:]), (d["L1_ffn_shared_gate_w"], shared_gu[:, 0:I1]),
                (d["L1_ffn_shared_up_w"], shared_gu[:, I1:]),
                (d["L1_ffn_shared_down_w"].rearrange("(t p) h -> p t h", p=P), shared_d[:]),
                (d["L1_ffn_routed_gate_w"].rearrange("e h i -> h e i"), wgu[:, :, 0:I1]),
                (d["L1_ffn_routed_up_w"].rearrange("e h i -> h e i"), wgu[:, :, I1:]),
                (d["L1_ffn_routed_down_w"].rearrange("e (t p) h -> p e t h", p=P), wd[:])])
            layer_norm(nc, "ln3", x_sb, xln, NT, xlnT, ident)
            l1_route(nc, xln, xlnT, gate, position, expert_of, n_tiles)
            l1_scatter(nc, xln, position, sorted_x, sorted_y)
            l1_shared(nc, x_sb, xlnT, shared_gu, shared_d)
            l1_routed(nc, ident, sorted_x, sorted_y, wgu, wd, expert_of, n_tiles)
            l1_gather(nc, x_sb, xln, position, sorted_y, out)


def kernel(**inputs):
    import numpy as _np
    import concourse.bacc as _bacc
    from concourse import mybir as _mybir
    from concourse.bass_utils import run_bass_kernel_spmd as _run

    nc = _bacc.Bacc("TRN2", target_bir_lowering=False, num_devices=1)
    arrays, tensors = {}, {}
    for name in _IN:
        a = _np.ascontiguousarray(inputs[name])
        arrays["in_" + name] = a
        tensors[name] = nc.dram_tensor("in_" + name, a.shape, _mybir.dt.from_np(a.dtype), kind="ExternalInput").ap()
    out = nc.dram_tensor("out_x", (B, S, E), F32, kind="ExternalOutput").ap()
    build_program(nc, tensors, out)
    result = _run(nc, [arrays], core_ids=[0])
    return result.results[0]["out_x"]
```

```python
from contextlib import ExitStack

import concourse.bass as bass
from concourse import mybir

F32 = mybir.dt.float32
BF16 = mybir.dt.bfloat16
I32 = mybir.dt.int32
U32 = mybir.dt.uint32
U8 = mybir.dt.uint8
ALU = mybir.AluOpType
ACT = mybir.ActivationFunctionType
AX = mybir.AxisListType.X

P = 128
B, S, E = 16, 256, 128
QT = S // P
NT = B * QT
KEYS = 1601
W = 512
NW = -(-KEYS // W)
KT = W // P
START = [max(KEYS - W * (NW - w), 0) for w in range(NW)]
FIRST_OWN = KEYS - W * (NW - 1)
MASKED = -float(2.0 ** 100)
DOUBLED = -float(2.0 ** 101)
NO_MAX = -float(2.0 ** 102)
EPS = 1e-5
ONE = 1


class Alloc:

    def __init__(self, nc, stack):
        self.nc, self.stack, self.sems = nc, stack, []
        stack.callback(self.clear)

    def start_at_one(self):
        for sem in self.sems:
            self.nc.gpsimd.sem_inc(sem, ONE)
        self.nc.all_engine_barrier()

    def clear(self):
        if self.sems:
            self.nc.clear_and_free_semaphores(self.sems)
            self.nc.all_engine_barrier()

    def sb(self, name, shape, dt=F32):
        return self.stack.enter_context(self.nc.sbuf_tensor(name, shape, dt))

    def ps(self, name, shape, dt=F32):
        return self.stack.enter_context(self.nc.psum_tensor(name, shape, dt))

    def sem(self, name):
        self.sems.append(self.nc.alloc_semaphore(name))
        return self.sems[-1]


class Awaited:

    def __init__(self, eng, sem, name, step=1):
        self.eng, self.sem, self.step = eng, sem, step
        self.value = eng.alloc_register(name)
        eng.reg_mov(self.value, ONE + step)

    def at(self):
        return self.eng.snap(self.value)

    def wait(self, at=None):
        self.eng.wait_ge(self.sem, self.at() if at is None else at)
        self.eng.reg_add(self.value, self.value, self.step)


class Steps:

    def __init__(self, eng, sem, base=0):
        self.eng, self.sem, self.base, self.n = eng, sem, base, 0

    def mark(self, ins):
        self.n += 1
        ins.then_inc(self.sem, 1)

    def settle(self):
        self.eng.wait_ge(self.sem, self.base + self.n)


def load_tokens(nc, x, x_sb, ident):
    with ExitStack() as st:
        a = Alloc(nc, st)
        loaded, zeroed, made = a.sem("x_loaded"), a.sem("ident_zeroed"), a.sem("ident_made")
        block = st.enter_context(nc.Block())

        @block.sync
        def _(sp):
            sp.dma_start(x_sb[:], x.rearrange("b (t p) e -> p (b t) e", p=P)).then_inc(loaded, 16)
            sp.wait_ge(loaded, 16)

        @block.gpsimd
        def _(pool):
            pool.memset(ident[:], 0.0).then_inc(zeroed, 1)
            pool.wait_ge(zeroed, 1)
            pool.affine_select(out=ident[:], in_=ident[:], compare_op=ALU.not_equal, fill=1.0, base=0,
                               pattern=[[-1, P]], channel_multiplier=1).then_inc(made, 1)
            pool.wait_ge(made, 1)


def layer_norm(nc, tag, src, dst, tiles, transposed=None, ident=None, affine=None):
    STEP = 8
    with ExitStack() as st:
        a = Alloc(nc, st)
        stats = a.sb(tag + "_stats", [P, tiles, 6])
        mv = a.sb(tag + "_mv", [P, tiles, 2])
        var = a.sb(tag + "_var", [P, tiles])
        rstd = a.sb(tag + "_rstd", [P, tiles])
        shift = a.sb(tag + "_shift", [P, tiles])
        expo = a.sb(tag + "_expo", [P, tiles])
        counted, merged, var_ready, root_ready = (a.sem(tag + n) for n in ("_counted", "_merged", "_varr", "_root"))
        expo_set = a.sem(tag + "_expo_set")
        scaled, normed, turned, moved = (a.sem(tag + n) for n in ("_scaled", "_normed", "_turned", "_moved"))
        if transposed is not None:
            pt = [a.ps(f"{tag}_pt{i}", [P, 4, P]) for i in range(2)]
        block = st.enter_context(nc.Block())

        @block.vector
        def _(dve):
            with dve.Fori(0, tiles // STEP) as g:
                for t in (g * STEP + i for i in range(STEP)):
                    dve.bn_stats(stats[:, bass.ds(t, 1), :].rearrange("p o s -> p (o s)"),
                                 src[:, bass.ds(t, 1), :].rearrange("p o e -> p (o e)")).then_inc(counted, 1)
            dve.wait_ge(counted, tiles)
            for t in range(tiles):
                dve.bn_aggr(mv[:, t, :], stats[:, t, :]).then_inc(merged, 1)
            dve.wait_ge(merged, tiles)
            dve.tensor_scalar(var[:], mv[:, :, 1], EPS, None, ALU.add).then_inc(var_ready, 1)
            dve.wait_ge(root_ready, 1)
            dve.scalar_tensor_tensor(shift[:], mv[:, :, 0], -1.0, rstd[:], ALU.mult, ALU.mult).then_inc(scaled, 1)
            dve.wait_ge(scaled, 1)
            with dve.Fori(0, tiles // STEP) as g:
                for t in (g * STEP + i for i in range(STEP)):
                    dve.tensor_scalar(dst[:, bass.ds(t, 1), :].rearrange("p o e -> p (o e)"),
                                      src[:, bass.ds(t, 1), :].rearrange("p o e -> p (o e)"),
                                      rstd[:, bass.ds(t, 1)], shift[:, bass.ds(t, 1)],
                                      ALU.mult, ALU.add).then_inc(normed, 1)
            dve.wait_ge(normed, tiles)

        @block.gpsimd
        def _(pool):
            pool.memset(expo[:], -0.5).then_inc(expo_set, 1)
            pool.wait_ge(expo_set, 1)
            pool.wait_ge(var_ready, 1)
            pool.tensor_tensor(rstd[:], var[:], expo[:], ALU.pow).then_inc(root_ready, 1)

        @block.scalar
        def _(act):
            if transposed is None:
                return
            for g in range(tiles // 4):
                act.wait_ge(turned, g + 1)
                out = transposed[:, g * 4 * P:(g + 1) * 4 * P]
                src_ps = pt[g % 2][:].rearrange("p t q -> p (t q)")
                if affine is None:
                    act.activation(out, src_ps, ACT.Copy).then_inc(moved, 1)
                else:
                    act.activation(out, src_ps, ACT.Identity, bias=affine[1], scale=affine[0]).then_inc(moved, 1)
            act.wait_ge(moved, tiles // 4)

        if transposed is not None:
            @block.tensor
            def _(pe):
                for g in range(tiles // 4):
                    pe.wait_ge(normed, 4 * (g + 1))
                    if g >= 2:
                        pe.wait_ge(moved, g - 1)
                    for t in range(4):
                        mm = pe.transpose(pt[g % 2][:, t, :], dst[:, 4 * g + t, :], ident[:])
                    mm.then_inc(turned, 1)


def start_loads(nc, loaded, columns=(), rows=(), others=()):
    with ExitStack() as st:
        block = st.enter_context(nc.Block())

        @block.sync
        def _(sp):
            for src, dst in columns:
                sp.dma_start(dst, src.rearrange("(p o) -> p o", o=1)).then_inc(loaded, 16)
            for src, dst in rows:
                sp.dma_start(dst, src.partition_broadcast(P)).then_inc(loaded, 16)
            for src, dst in others:
                sp.dma_start(dst, src).then_inc(loaded, 16)
    return len(columns) + len(rows) + len(others)


def await_loads(nc, loaded, count):
    with ExitStack() as st:
        block = st.enter_context(nc.Block())

        @block.sync
        def _(sp):
            sp.wait_ge(loaded, 16 * count)


def turn_weights(nc, tag, loads, ident, columns=(), rows=(), others=()):
    with ExitStack() as st:
        a = Alloc(nc, st)
        n = len(loads)
        raw = a.sb(tag + "_raw", [P, max(n, 1), P])
        pt = a.ps(tag + "_pt", [P, 4, P])
        loaded, turned, moved = a.sem(tag + "_loaded"), a.sem(tag + "_turned"), a.sem(tag + "_moved")
        block = st.enter_context(nc.Block())
        total = n + len(columns) + len(rows) + len(others)

        @block.sync
        def _(sp):
            for i, (src, _) in enumerate(loads):
                sp.dma_start(raw[:, i, :], src).then_inc(loaded, 16)
            for src, dst in columns:
                sp.dma_start(dst, src.rearrange("(p o) -> p o", o=1)).then_inc(loaded, 16)
            for src, dst in rows:
                sp.dma_start(dst, src.partition_broadcast(P)).then_inc(loaded, 16)
            for src, dst in others:
                sp.dma_start(dst, src).then_inc(loaded, 16)
            sp.wait_ge(loaded, 16 * total)

        if not n:
            return

        @block.tensor
        def _(pe):
            pe.wait_ge(loaded, 16 * total)
            for i in range(n):
                mm = pe.transpose(pt[:, i, :], raw[:, i, :], ident[:])
            mm.then_inc(turned, 1)

        @block.vector
        def _(dve):
            dve.wait_ge(turned, 1)
            for i, (_, dst) in enumerate(loads):
                dve.tensor_copy(dst, pt[:, i, :]).then_inc(moved, 1)
            dve.wait_ge(moved, n)


def l0_mask(nc, mask, mneg, flags, ident):
    with ExitStack() as st:
        a = Alloc(nc, st)
        raw = a.sb("m_raw", [P, QT, KEYS], I32)
        best = a.sb("m_best", [P, QT, NW])
        some = a.sb("m_some", [P, QT])
        need = a.sb("m_need", [P, QT, NW])
        row = a.sb("m_row", [QT * NW, 1])
        turned_sb = a.sb("m_turned_sb", [QT * NW, P])
        line = a.sb("m_line", [1, QT * NW])
        merged = a.sb("m_merged", [1, NW])
        firsts = a.sb("m_firsts", [1, NW])
        pt = a.ps("m_pt", [P, P])
        loaded, steps, turned, topped, line_ps = (a.sem(n) for n in ("m_loaded", "m_steps", "m_turn", "m_top", "m_line_ps"))
        block = st.enter_context(nc.Block())

        @block.sync
        def _(sp):
            sp.dma_start(raw[:], mask.rearrange("(t p) k -> p t k", p=P)).then_inc(loaded, 16)
            sp.wait_ge(loaded, 16)

        @block.vector
        def _(dve):
            s = Steps(dve, steps)
            s.mark(dve.memset(mneg[:, :, 0, FIRST_OWN:], DOUBLED))
            dve.wait_ge(loaded, 16)
            for w in range(NW):
                own = FIRST_OWN if w == 0 else W
                s.mark(dve.tensor_scalar(mneg[:, :, w, 0:own], raw[:, :, START[w]:START[w] + own], 0.0, MASKED,
                                         ALU.is_equal, ALU.mult))
            s.settle()
            s.mark(dve.tensor_reduce(best[:], mneg[:], AX, ALU.max))
            s.settle()
            s.mark(dve.tensor_reduce(some[:], best[:], AX, ALU.max))
            s.settle()
            s.mark(dve.tensor_scalar(some[:], some[:], 0.0, None, ALU.is_lt))
            s.mark(dve.tensor_scalar(best[:], best[:], 0.0, None, ALU.is_equal))
            s.settle()
            for t in range(QT):
                s.mark(dve.tensor_scalar(need[:, t, :], best[:, t, :], some[:, t:t + 1], None, ALU.max))
            s.settle()
            dve.engine_nop().then_inc(topped, 1)
            dve.wait_ge(turned, 1)
            s.mark(dve.tensor_reduce(row[:], pt[0:QT * NW, :], AX, ALU.max))
            s.settle()
            dve.engine_nop().then_inc(topped, 1)
            dve.wait_ge(line_ps, 1)
            s.mark(dve.tensor_copy(line[:], pt[0:1, 0:QT * NW]))
            s.settle()
            s.mark(dve.tensor_tensor(merged[:], line[:, 0:NW], line[:, NW:2 * NW], ALU.max))
            s.settle()
            s.mark(dve.tensor_copy(flags[:, 0:NW], merged[:]))
            s.mark(dve.tensor_copy(firsts[:], merged[:]))
            s.settle()
            for w in range(1, NW):
                s.mark(dve.tensor_tensor(firsts[:, w:w + 1], merged[:, w:w + 1], merged[:, w - 1:w], ALU.is_gt))
                s.mark(dve.tensor_tensor(merged[:, w:w + 1], merged[:, w:w + 1], merged[:, w - 1:w], ALU.max))
                s.settle()
            s.mark(dve.tensor_copy(flags[:, NW:2 * NW], firsts[:]))
            s.settle()

        @block.tensor
        def _(pe):
            pe.wait_ge(topped, 1)
            pe.transpose(pt[0:QT * NW, :], need[:].rearrange("p t w -> p (t w)"), ident[:]).then_inc(turned, 1)
            pe.wait_ge(topped, 2)
            pe.transpose(pt[0:1, 0:QT * NW], row[:], ident[0:QT * NW, 0:QT * NW]).then_inc(line_ps, 1)


H0, D0 = 16, 8
QUADS = H0 // 4
HQ = 4 * QT
SCALE0 = float(D0) ** -0.5


def l0_attention(nc, x_sb, xlnT, mneg, flags, ident, ctx, w):
    wqT, wkT, wvT, wpT, bq, bk, bv, bp = w
    ctx_rows = ctx.rearrange("b k e -> (b k) e")
    with ExitStack() as st:
        a = Alloc(nc, st)
        head_rows = a.sb("head_rows", [P, H0])
        qT = a.sb("qT", [P, NT * P])
        q_b = a.sb("q_b", [P, S])
        qbd = a.sb("qbd", [P, 2, H0, S])
        ctx_sb = a.sb("ctx_sb", [P, KT, E])
        ctxT = a.sb("ctxT", [P, W])
        kT = a.sb("kT", [P, W])
        v = a.sb("v", [P, KT, E])
        scores = a.sb("scores", [P, 2, HQ, W])
        probsT = a.sb("probsT", [P, 2, KT, 4, S])
        oT = a.sb("oT", [P, QUADS, S])
        m_old = a.sb("m_old", [P, H0 * QT])
        m_win = a.sb("m_win", [P, H0 * QT])
        m_new = a.sb("m_new", [P, H0 * QT])
        m_diff = a.sb("m_diff", [P, H0 * QT])
        alpha = a.sb("alpha", [P, H0 * QT])
        neg_m = a.sb("neg_m", [P, H0 * QT])
        l_win = a.sb("l_win", [P, H0 * QT])
        l_sum = a.sb("l_sum", [P, H0 * QT])
        acc = a.sb("acc", [P, QT, H0, D0])
        heads = a.sb("heads", [P, QT, E])
        headsT = a.sb("headsT", [P, S])
        ps_s = [a.ps(f"ps_s{i}", [P, W]) for i in range(2)]
        ps_t = [a.ps(f"ps_t{i}", [P, KT * P]) for i in range(2)]
        ps_o = a.ps("ps_o", [P, QUADS, S])
        ps_m = [a.ps(f"ps_m{i}", [P, 512]) for i in range(2)]

        sem = {n: a.sem("a0_" + n) for n in (
            "rows_zeroed rows_made q_ps q_sb q_b_ready qbd_ready flags_seen ctx_loaded ctxT_ps ctxT_sb kv_ps k_sb v_sb s_ps s_sb "
            "neg_m_ready p_sb t_ps t_act t_dve o_ps o_sb oT_ps acc_done alpha_ready heads_ready headsT_ps headsT_sb "
            "y_ps x_done dve_steps state_ready").split()}
        a.start_at_one()
        block = st.enter_context(nc.Block())

        def windows(eng):
            live, first = ([eng.value_load(flags[0:1, i:i + 1], min_val=0, max_val=1) for i in part]
                           for part in (range(NW), range(NW, 2 * NW)))
            n = eng.alloc_register("n_windows")
            eng.reg_mov(n, 0)
            return live, first, n

        @block.sync
        def _(sp):
            live, first, n = windows(sp)
            with sp.Fori(0, B) as b:
                for wi in range(NW):
                    with sp.If(live[wi] != 0):
                        done = sp.snap(n)
                        sp.wait_ge(sem["ctxT_ps"], ONE + done)
                        sp.dma_start(ctx_sb[:], ctx_rows[bass.ds(b * KEYS + START[wi], W), :].rearrange(
                            "(t p) e -> p t e", p=P)).then_inc(sem["ctx_loaded"], 16)
                        sp.reg_add(n, n, 1)

        @block.gpsimd
        def _(pool):
            pool.memset(head_rows[:], 1.0).then_inc(sem["rows_zeroed"], 1)
            pool.wait_ge(sem["rows_zeroed"], ONE + 1)
            pool.affine_select(out=head_rows[:], in_=head_rows[:], compare_op=ALU.is_ge, fill=0.0, base=0,
                               pattern=[[-D0, H0]], channel_multiplier=1).then_inc(sem["rows_made"], 1)
            pool.wait_ge(sem["rows_made"], ONE + 1)
            pool.affine_select(out=head_rows[:], in_=head_rows[:], compare_op=ALU.is_ge, fill=0.0, base=D0 - 1,
                               pattern=[[D0, H0]], channel_multiplier=-1).then_inc(sem["rows_made"], 1)
            pool.wait_ge(sem["rows_made"], ONE + 2)
            pool.wait_ge(sem["q_sb"], ONE + NT * P // 512)

            q_b_ready = Awaited(pool, sem["q_b_ready"], "a0_q_b_ready_at")

            def spread(b, half):
                pool.wait_ge(sem["qbd_ready"], ONE + b)
                pool.tensor_copy(q_b[:], qT[:, bass.ds(b * S, S)]).then_inc(sem["q_b_ready"], 1)
                q_b_ready.wait()
                for h in range(H0):
                    ins = pool.tensor_scalar(qbd[:, half, h, :], q_b[:], head_rows[:, h:h + 1], None, ALU.mult)
                ins.then_inc(sem["qbd_ready"], 1)

            spread(0, 0)
            spread(1, 1)
            with pool.Fori(1, B // 2) as i:
                for half in range(2):
                    pool.wait_ge(sem["headsT_ps"], ONE + i * 2 - 1 + half)
                    spread(i * 2 + half, half)

        @block.tensor
        def _(pe):
            for g in range(NT * P // 512):
                if g >= 2:
                    pe.wait_ge(sem["q_sb"], ONE + g - 1)
                pe.matmul(ps_m[g % 2][:], wqT[:], xlnT[:, g * 512:(g + 1) * 512], start=True,
                          stop=True).then_inc(sem["q_ps"], 1)
            live, first, n = windows(pe)
            pe.wait_ge(sem["q_sb"], ONE + NT * P // 512)
            pe.wait_ge(sem["state_ready"], ONE + 1)

            def one_score(u, quad, half, j):
                h, t = 4 * quad + j // QT, j % QT
                if not (quad == 0 and j < 2):
                    pe.wait_ge(sem["s_sb"], ONE + u * HQ + j - 1)
                pe.matmul(ps_s[j % 2][:], qbd[:, half, h, t * P:(t + 1) * P], kT[:], start=True,
                          stop=True).then_inc(sem["s_ps"], 1)

            def one_turn(u, quad, j):
                pe.wait_ge(sem["p_sb"], ONE + u * HQ + j + 1)
                if j % 2 == 0:
                    pe.wait_ge(sem["t_act"], ONE + u * HQ // 2 + j // 2)
                else:
                    pe.wait_ge(sem["t_dve"], ONE + u * HQ // 2 + j // 2)
                for k in range(KT):
                    mm = pe.transpose(ps_t[j % 2][:, k * P:(k + 1) * P], scores[:, quad % 2, j, k * P:(k + 1) * P], ident[:])
                mm.then_inc(sem["t_ps"], 1)

            def values(u, quad):
                pe.wait_ge(sem["t_act"], ONE + (u + 1) * HQ // 2)
                pe.wait_ge(sem["t_dve"], ONE + (u + 1) * HQ // 2)
                for k in range(KT):
                    for i in range(4):
                        h = 4 * quad + i
                        mm = pe.matmul(ps_o[32 * i:32 * i + D0, quad, :], v[:, k, D0 * h:D0 * (h + 1)],
                                       probsT[:, quad % 2, k, i, :], start=(k == 0), stop=(k == KT - 1),
                                       tile_position=(0, 32 * i))
                mm.then_inc(sem["o_ps"], 1)

            def merge_heads(done):
                pe.wait_ge(sem["o_sb"], ONE + done + 1)
                for t in range(QT):
                    for quad in range(QUADS):
                        mm = pe.transpose(ps_t[t][:, quad * P:(quad + 1) * P], oT[:, quad, t * P:(t + 1) * P], ident[:])
                    mm.then_inc(sem["oT_ps"], 1)

            def turn_heads(b):
                pe.wait_ge(sem["heads_ready"], ONE + b)
                for t in range(QT):
                    mm = pe.transpose(ps_m[0][:, t * P:(t + 1) * P], heads[:, t, :], ident[:])
                mm.then_inc(sem["headsT_ps"], 1)

            def project_heads(b):
                pe.wait_ge(sem["headsT_sb"], ONE + b)
                for t in range(QT):
                    mm = pe.matmul(ps_m[1][:, t * P:(t + 1) * P], headsT[:, t * P:(t + 1) * P], wpT[:], start=True,
                                   stop=True)
                mm.then_inc(sem["y_ps"], 1)

            def window(done, half, b, finish):
                pe.wait_ge(sem["ctx_loaded"], ONE + (done + 1) * 16)
                for k in range(KT):
                    mm = pe.transpose(ps_m[0][:, k * P:(k + 1) * P], ctx_sb[:, k, :], ident[:])
                mm.then_inc(sem["ctxT_ps"], 1)
                pe.wait_ge(sem["ctxT_sb"], ONE + done + 1)
                pe.matmul(ps_m[1][:], wkT[:], ctxT[:], start=True, stop=True).then_inc(sem["kv_ps"], 1)
                for k in range(KT):
                    mm = pe.matmul(ps_m[0][:, k * P:(k + 1) * P], ctxT[:, k * P:(k + 1) * P], wvT[:], start=True,
                                   stop=True)
                mm.then_inc(sem["kv_ps"], 1)
                merge_heads(done)
                pe.wait_ge(sem["k_sb"], ONE + done + 1)
                pe.wait_ge(sem["s_sb"], ONE + done * HQ * QUADS)
                for j in range(HQ):
                    one_score(done * QUADS, 0, half, j)
                pe.wait_ge(sem["v_sb"], ONE + done + 1)
                pe.wait_ge(sem["acc_done"], ONE + done + 1)
                for quad in range(QUADS):
                    u = done * QUADS + quad
                    for j in range(HQ):
                        if quad + 1 < QUADS:
                            one_score(u + 1, quad + 1, half, j)
                        one_turn(u, quad, j)
                    values(u, quad)
                    if quad == 0:
                        with pe.If(finish != 0):
                            turn_heads(b)
                    if quad == 1:
                        with pe.If(finish != 0):
                            project_heads(b)
                pe.wait_ge(sem["x_done"], ONE + b)

            def batch(b, half):
                pe.wait_ge(sem["qbd_ready"], ONE + b + 1)
                for wi in range(NW):
                    with pe.If(live[wi] != 0):
                        window(pe.snap(n), half, b, pe.snap(first[wi] * b))
                        pe.reg_add(n, n, 1)

            with pe.Fori(0, B // 2) as i:
                batch(i * 2, 0)
                batch(i * 2 + 1, 1)
            merge_heads(pe.snap(n))
            turn_heads(B)
            project_heads(B)

        @block.scalar
        def _(act):
            for g in range(NT * P // 512):
                act.wait_ge(sem["q_ps"], ONE + g + 1)
                act.activation(qT[:, g * 512:(g + 1) * 512], ps_m[g % 2][:], ACT.Identity,
                               bias=bq[:]).then_inc(sem["q_sb"], 1)
            live, first, n = windows(act)

            act.wait_ge(sem["state_ready"], ONE + 1)

            def merge_heads(done):
                act.wait_ge(sem["o_ps"], ONE + done * QUADS)
                act.wait_ge(sem["oT_ps"], ONE + done * QT)
                act.activation(oT[:], ps_o[:], ACT.Copy).then_inc(sem["o_sb"], 1)

            def turn_heads(b):
                act.wait_ge(sem["headsT_ps"], ONE + b)
                act.wait_ge(sem["y_ps"], ONE + b - 1)
                act.activation(headsT[:], ps_m[0][:, 0:S], ACT.Copy).then_inc(sem["headsT_sb"], 1)

            def window(done, b, finish):
                act.wait_ge(sem["ctxT_ps"], ONE + done + 1)
                act.wait_ge(sem["kv_ps"], ONE + done * 2)
                act.activation(ctxT[:], ps_m[0][:], ACT.Copy).then_inc(sem["ctxT_sb"], 1)
                merge_heads(done)
                act.wait_ge(sem["kv_ps"], ONE + done * 2 + 1)
                act.wait_ge(sem["s_ps"], ONE + done * HQ * QUADS)
                act.activation(kT[:], ps_m[1][:], ACT.Identity, bias=bk[:]).then_inc(sem["k_sb"], 1)
                for quad in range(QUADS):
                    u = done * QUADS + quad
                    act.wait_ge(sem["neg_m_ready"], ONE + u + 1)
                    c = quad * HQ
                    if quad == 0:
                        act.wait_ge(sem["acc_done"], ONE + done + 1)
                    act.activation(alpha[:, c:c + HQ], m_diff[:, c:c + HQ], ACT.Exp,
                                   scale=SCALE0).then_inc(sem["alpha_ready"], 1)

                    def move(j):
                        act.wait_ge(sem["t_ps"], ONE + u * HQ + j + 1)
                        i, t = j // QT, j % QT
                        if j == 0:
                            if quad >= 2:
                                act.wait_ge(sem["o_ps"], ONE + u - 1)
                            else:
                                act.wait_ge(sem["o_ps"], ONE + done * QUADS)
                        act.activation(probsT[:, quad % 2, :, i, t * P:(t + 1) * P],
                                       ps_t[0][:].rearrange("p (k q) -> p k q", k=KT),
                                       ACT.Copy).then_inc(sem["t_act"], 1)

                    for j in range(HQ):
                        act.activation(scores[:, quad % 2, j, :], scores[:, quad % 2, j, :], ACT.Exp,
                                       bias=neg_m[:, c + j:c + j + 1], scale=SCALE0,
                                       accum_out=l_win[:, c + j:c + j + 1]).then_inc(sem["p_sb"], 1)
                        if j % 2 == 1:
                            move(j - 1)
                        if quad == 1 and j == HQ // 2:
                            with act.If(finish != 0):
                                turn_heads(b)

            with act.Fori(0, B) as b:
                for wi in range(NW):
                    with act.If(live[wi] != 0):
                        window(act.snap(n), b, act.snap(first[wi] * b))
                        act.reg_add(n, n, 1)
            merge_heads(act.snap(n))
            turn_heads(B)

        @block.vector
        def _(dve):
            dve.memset(ps_o[:], 0.0).then_inc(sem["state_ready"], 1)
            s0 = Steps(dve, sem["dve_steps"], ONE)
            for state in (alpha, l_win, l_sum, acc):
                s0.mark(dve.memset(state[:], 0.0))
            s0.mark(dve.memset(m_old[:], NO_MAX))
            s0.settle()
            live, first, n = windows(dve)
            steps = dve.alloc_register("n_steps")
            dve.reg_mov(steps, ONE + s0.n)
            scores_in = Awaited(dve, sem["s_ps"], "a0_s_ps_at")

            def merge_heads(done, at):
                s = Steps(dve, sem["dve_steps"], at)
                dve.wait_ge(sem["alpha_ready"], ONE + done * QUADS)
                dve.wait_ge(sem["p_sb"], ONE + done * QUADS * HQ)
                s.mark(dve.tensor_tensor(l_sum[:], l_sum[:], alpha[:], ALU.mult))
                for t in range(QT):
                    by_head = alpha[:].rearrange("p (h t) -> p h t", t=QT)[:, :, t:t + 1].broadcast_to([P, H0, D0])
                    s.mark(dve.tensor_tensor(acc[:, t, :, :], acc[:, t, :, :], by_head, ALU.mult))
                s.settle()
                s.mark(dve.tensor_tensor(l_sum[:], l_sum[:], l_win[:], ALU.add))
                for t in range(QT):
                    dve.wait_ge(sem["oT_ps"], ONE + done * QT + t + 1)
                    got = ps_t[t][:].rearrange("p (h d) -> p h d", d=32)[:, :, 0:D0]
                    ins = dve.tensor_tensor(acc[:, t, :, :], acc[:, t, :, :], got, ALU.add)
                    if t + 1 < QT:
                        s.mark(ins)
                ins.then_inc(sem["acc_done"], 1)
                s.settle()
                dve.wait_ge(sem["acc_done"], ONE + done + 1)
                dve.reg_add(steps, steps, s.n)

            def give_heads(b):
                s = Steps(dve, sem["dve_steps"], dve.snap(steps))
                s.mark(dve.reciprocal(l_sum[:], l_sum[:]))
                s.settle()
                dve.wait_ge(sem["headsT_ps"], ONE + b - 1)
                for t in range(QT):
                    by_head = l_sum[:].rearrange("p (h t) -> p h t", t=QT)[:, :, t:t + 1].broadcast_to([P, H0, D0])
                    ins = dve.tensor_tensor(heads[:, t, :].rearrange("p (h d) -> p h d", d=D0), acc[:, t, :, :],
                                            by_head, ALU.mult)
                    if t + 1 < QT:
                        s.mark(ins)
                ins.then_inc(sem["heads_ready"], 1)
                s.settle()
                dve.wait_ge(sem["heads_ready"], ONE + b)
                s.mark(dve.memset(m_old[:], NO_MAX))
                s.mark(dve.memset(l_sum[:], 0.0))
                s.mark(dve.memset(acc[:], 0.0))
                s.settle()
                dve.reg_add(steps, steps, s.n)

            def add_to_x(b):
                s = Steps(dve, sem["dve_steps"], dve.snap(steps))
                dve.wait_ge(sem["y_ps"], ONE + b)
                at = (b - 1) * QT if isinstance(b, int) else nc.s_assert_within(
                    (b - 1) * QT, 0, (B - 2) * QT, skip_runtime_bounds_check_because="only taken where b > 0")
                x_b = x_sb[:, bass.ds(at, QT), :]
                s.mark(dve.tensor_tensor(x_b, x_b, ps_m[1][:, 0:S].rearrange("p (t e) -> p t e", t=QT), ALU.add))
                s.settle()
                dve.tensor_tensor(x_b, x_b, bp[:].unsqueeze(1).broadcast_to([P, QT, E]),
                                  ALU.add).then_inc(sem["x_done"], 1)
                dve.reg_add(steps, steps, s.n)

            def window(done, wi, b, finish):
                dve.wait_ge(sem["kv_ps"], ONE + done * 2 + 2)
                dve.wait_ge(sem["o_ps"], ONE + done * QUADS)
                dve.tensor_tensor(v[:], ps_m[0][:].rearrange("p (k e) -> p k e", k=KT),
                                  bv[:].unsqueeze(1).broadcast_to([P, KT, E]), ALU.add).then_inc(sem["v_sb"], 1)
                merge_heads(done, dve.snap(steps))
                with dve.If(finish != 0):
                    give_heads(b)

                def reduce_one(u, quad, j):
                    at = scores_in.at()
                    if j == 0:
                        if quad >= 2:
                            dve.wait_ge(sem["t_ps"], ONE + (u - 1) * HQ)
                        else:
                            dve.wait_ge(sem["t_ps"], ONE + done * QUADS * HQ)
                    scores_in.wait(at)
                    c = quad * HQ + j
                    dve.tensor_tensor_reduce(scores[:, quad % 2, j, :], ps_s[j % 2][:], mneg[:, j % QT, wi, :], 1.0,
                                             NO_MAX, ALU.add, ALU.max,
                                             m_win[:, c:c + 1]).then_inc(sem["s_sb"], 1)

                def shift(u, quad):
                    s = Steps(dve, sem["dve_steps"], dve.snap(steps))
                    c = slice(quad * HQ, (quad + 1) * HQ)
                    dve.wait_ge(sem["s_sb"], ONE + (u + 1) * HQ)
                    s.mark(dve.tensor_tensor(m_new[:, c], m_old[:, c], m_win[:, c], ALU.max))
                    s.settle()
                    s.mark(dve.tensor_tensor(m_diff[:, c], m_old[:, c], m_new[:, c], ALU.subtract))
                    s.settle()
                    s.mark(dve.tensor_copy(m_old[:, c], m_new[:, c]))
                    dve.tensor_scalar(neg_m[:, c], m_new[:, c], -SCALE0, None, ALU.mult).then_inc(sem["neg_m_ready"], 1)
                    s.settle()
                    dve.reg_add(steps, steps, s.n)

                for j in range(HQ):
                    reduce_one(done * QUADS, 0, j)
                shift(done * QUADS, 0)
                for quad in range(QUADS):
                    u = done * QUADS + quad
                    for j in range(HQ):
                        if quad + 1 < QUADS:
                            reduce_one(u + 1, quad + 1, j)
                        if j % 2:
                            dve.wait_ge(sem["t_ps"], ONE + u * HQ + j + 1)
                            if j == 1:
                                if quad >= 2:
                                    dve.wait_ge(sem["o_ps"], ONE + u - 1)
                                else:
                                    dve.wait_ge(sem["o_ps"], ONE + done * QUADS)
                            i, t = j // QT, j % QT
                            dve.tensor_copy(probsT[:, quad % 2, :, i, t * P:(t + 1) * P],
                                            ps_t[1][:].rearrange("p (k q) -> p k q", k=KT)).then_inc(sem["t_dve"], 1)
                    if quad + 1 < QUADS:
                        shift(u + 1, quad + 1)
                    if quad == 2:
                        with dve.If(finish != 0):
                            add_to_x(b)

            with dve.Fori(0, B) as b:
                for wi in range(NW):
                    with dve.If(live[wi] != 0):
                        window(dve.snap(n), wi, b, dve.snap(first[wi] * b))
                        dve.reg_add(n, n, 1)
            merge_heads(dve.snap(n), dve.snap(steps))
            give_heads(B)
            add_to_x(B)
            dve.wait_ge(sem["x_done"], ONE + B)


E0, K0, I0 = 16, 4, 256
CH = 512
CT = CH // P


def l0_router(nc, x_sb, xlnT, ident, rw, rb, b2, weight):
    with ExitStack() as st:
        a = Alloc(nc, st)
        logits = a.sb("r_logits", [P, NT, E0])
        e = a.sb("r_e", [P, NT, E0])
        sel = a.sb("r_sel", [P, NT, E0])
        eq = [a.sb(f"r_eq{i}", [P, NT, E0]) for i in range(2)]
        top = a.sb("r_top", [P, NT, 8])
        need = a.sb("r_need", [P, NT])
        total = a.sb("r_total", [P, NT])
        wT = a.sb("r_wT", [E0, 4, P])
        ps_l = a.ps("r_ps_l", [P, NT, E0])
        ps_w = a.ps("r_ps_w", [P, 4, P])
        ps_b = a.ps("r_ps_b", [P, 4, P])
        s_logit, s_steps, s_centred, s_exp, s_weight, s_turn, s_moved, s_bias, s_added = (
            a.sem("r_s" + n) for n in "logit steps centred exp weight turn moved bias added".split())
        block = st.enter_context(nc.Block())
        per_tile = lambda t: t[:].unsqueeze(2).broadcast_to([P, NT, E0])

        @block.tensor
        def _(pe):
            for t in range(NT):
                mm = pe.matmul(ps_l[:, t, :], xlnT[:, t * P:(t + 1) * P], rw[:], start=True, stop=True)
            mm.then_inc(s_logit, 1)
            pe.wait_ge(s_weight, 1)
            for g in range(NT // 4):
                pe.wait_ge(s_moved, g)
                for i in range(4):
                    mm = pe.transpose(ps_w[0:E0, i, :], weight[:, 4 * g + i, :], ident[:])
                mm.then_inc(s_turn, 1)
                pe.wait_ge(s_moved, g + 1)
                pe.wait_ge(s_added, g)
                for i in range(4):
                    mm = pe.matmul(ps_b[:, i, :], wT[:, i, :], b2[:], start=True, stop=True)
                mm.then_inc(s_bias, 1)

        @block.scalar
        def _(act):
            act.wait_ge(s_centred, 1)
            act.activation(e[:], logits[:], ACT.Exp).then_inc(s_exp, 1)
            for g in range(NT // 4):
                act.wait_ge(s_turn, g + 1)
                act.wait_ge(s_bias, g)
                act.activation(wT[:], ps_w[0:E0, :, :], ACT.Copy).then_inc(s_moved, 1)

        @block.vector
        def _(dve):
            s = Steps(dve, s_steps)
            dve.wait_ge(s_logit, 1)
            s.mark(dve.tensor_tensor(logits[:], ps_l[:], rb[:].unsqueeze(1).broadcast_to([P, NT, E0]), ALU.add))
            s.settle()
            for t in range(NT):
                s.mark(dve.max(top[:, t, :], logits[:, t, :]))
            s.settle()
            kth = top[:, :, K0 - 1:K0].broadcast_to([P, NT, E0])
            s.mark(dve.tensor_tensor(sel[:], logits[:], kth, ALU.is_gt))
            s.mark(dve.tensor_tensor(eq[0][:], logits[:], kth, ALU.is_equal))
            s.mark(dve.tensor_tensor(logits[:], logits[:], top[:, :, 0:1].broadcast_to([P, NT, E0]), ALU.subtract))
            s.settle()
            dve.engine_nop().then_inc(s_centred, 1)
            s.mark(dve.tensor_reduce(need[:], sel[:], AX, ALU.add))
            s.settle()
            s.mark(dve.tensor_scalar(need[:], need[:], -1.0, float(K0), ALU.mult, ALU.add))
            dve.wait_ge(s_exp, 1)
            s.mark(dve.tensor_copy(logits[:], eq[0][:]))
            s.settle()
            step, cur = 1, 0
            while step < E0:
                s.mark(dve.tensor_copy(eq[1 - cur][:, :, 0:step], eq[cur][:, :, 0:step]))
                s.mark(dve.tensor_tensor(eq[1 - cur][:, :, step:], eq[cur][:, :, step:], eq[cur][:, :, 0:E0 - step],
                                         ALU.add))
                s.settle()
                cur, step = 1 - cur, step * 2
            s.mark(dve.tensor_tensor(eq[cur][:], eq[cur][:], per_tile(need), ALU.is_le))
            s.settle()
            s.mark(dve.tensor_tensor(eq[cur][:], eq[cur][:], logits[:], ALU.mult))
            s.settle()
            s.mark(dve.tensor_tensor(sel[:], sel[:], eq[cur][:], ALU.add))
            s.settle()
            s.mark(dve.tensor_tensor(e[:], e[:], sel[:], ALU.mult))
            s.settle()
            s.mark(dve.tensor_reduce(total[:], e[:], AX, ALU.add))
            s.settle()
            s.mark(dve.reciprocal(total[:], total[:]))
            s.settle()
            dve.tensor_tensor(weight[:], e[:], per_tile(total), ALU.mult).then_inc(s_weight, 1)
            for g in range(NT // 4):
                dve.wait_ge(s_bias, g + 1)
                dve.tensor_tensor(x_sb[:, 4 * g:4 * g + 4, :], x_sb[:, 4 * g:4 * g + 4, :], ps_b[:],
                                  ALU.add).then_inc(s_added, 1)
            dve.wait_ge(s_added, NT // 4)


def l0_experts(nc, x_sb, xlnT, w1, b1, w2, weight):
    with ExitStack() as st:
        a = Alloc(nc, st)
        hid = a.sb("e_hid", [P, 2, 2, CH])
        ps_h = [a.ps(f"e_ps_h{i}", [P, 2, CH]) for i in range(2)]
        ps_y = [a.ps(f"e_ps_y{i}", [P, CT, E]) for i in range(2)]
        h_ps, h_sb, y_ps, y_added = (a.sem("e_" + n) for n in "h_ps h_sb y_ps y_added".split())
        a.start_at_one()
        block = st.enter_context(nc.Block())

        @block.tensor
        def _(pe):
            def up(u, c, e):
                if not (isinstance(u, int) and u < 2):
                    pe.wait_ge(h_sb, ONE + u * 2 - 2)
                for half in range(2):
                    mm = pe.matmul(ps_h[e % 2][:, half, :], w1[:, e, half * P:(half + 1) * P],
                                   xlnT[:, bass.ds(c * CH, CH)], start=True, stop=True)
                    mm.then_inc(h_ps, 1)

            def down(u, e):
                pe.wait_ge(h_sb, ONE + u * 2 + 2)
                if e >= 2:
                    pe.wait_ge(y_added, ONE + u * CT - CT)
                else:
                    pe.wait_ge(y_added, ONE + u * CT - CT * e)
                for t in range(CT):
                    for half in range(2):
                        mm = pe.matmul(ps_y[e % 2][:, t, :], hid[:, e % 2, half, t * P:(t + 1) * P], w2[:, e, half, :],
                                       start=(half == 0), stop=(half == 1))
                mm.then_inc(y_ps, 1)

            with pe.Fori(0, NT * P // CH) as c:
                u0 = c * E0
                for half in range(2):
                    pe.wait_ge(h_sb, ONE + u0 * 2)
                    pe.matmul(ps_h[0][:, half, :], w1[:, 0, half * P:(half + 1) * P], xlnT[:, bass.ds(c * CH, CH)],
                              start=True, stop=True).then_inc(h_ps, 1)
                for e in range(E0):
                    if e + 1 < E0:
                        if e == 0:
                            pe.wait_ge(h_sb, ONE + u0 * 2)
                            for half in range(2):
                                pe.matmul(ps_h[1][:, half, :], w1[:, 1, half * P:(half + 1) * P],
                                          xlnT[:, bass.ds(c * CH, CH)], start=True, stop=True).then_inc(h_ps, 1)
                        else:
                            up(u0 + e + 1, c, e + 1)
                    down(u0 + e, e)

        @block.scalar
        def _(act):
            with act.Fori(0, NT * P // CH) as c:
                for e in range(E0):
                    u = c * E0 + e
                    if e >= 2:
                        act.wait_ge(y_ps, ONE + u - 1)
                    else:
                        act.wait_ge(y_ps, ONE + u - e)
                    for half in range(2):
                        act.wait_ge(h_ps, ONE + u * 2 + half + 1)
                        act.activation(hid[:, e % 2, half, :], ps_h[e % 2][:, half, :], ACT.Gelu,
                                       bias=b1[:, e, half:half + 1]).then_inc(h_sb, 1)

        @block.vector
        def _(dve):
            with dve.Fori(0, NT * P // CH) as c:
                for e in range(E0):
                    u = c * E0 + e
                    dve.wait_ge(y_ps, ONE + u + 1)
                    if e:
                        dve.wait_ge(y_added, ONE + u * CT)
                    for t in range(CT):
                        x_t = x_sb[:, bass.ds(c * CT + t, 1), :].rearrange("p o e -> p (o e)")
                        w_t = weight[:, bass.ds(c * CT + t, 1), e:e + 1].rearrange("p o e -> p (o e)")
                        dve.scalar_tensor_tensor(x_t, ps_y[e % 2][:, t, :], w_t, x_t, ALU.mult,
                                                 ALU.add).then_inc(y_added, 1)
            dve.wait_ge(y_added, ONE + NT * P // CH * E0 * CT)


H1, D1 = 2, 64
PAIRS = H1 * QT
RMS_EPS = 1e-8
SCALE1 = float(D1) ** -0.5
GT = 4
LK = S // P


def l1_flags(nc, mask, scratch, flags):
    with ExitStack() as st:
        a = Alloc(nc, st)
        raw = a.sb("f_raw", [B, KEYS], U8)
        best = a.sb("f_best", [B, NW])
        seen = a.sb("f_seen", [B, NW], I32)
        loaded, steps, stored, done = a.sem("f_loaded"), a.sem("f_steps"), a.sem("f_stored"), a.sem("f_done")
        block = st.enter_context(nc.Block())

        @block.sync
        def _(sp):
            sp.dma_start(raw[:], mask).then_inc(loaded, 16)
            sp.wait_ge(steps, NW + 1)
            sp.dma_start(scratch, seen[:]).then_inc(stored, 16)
            sp.wait_ge(stored, 16)
            sp.dma_start(flags[:], scratch.rearrange("b w -> (b w)").unsqueeze(0)).then_inc(done, 16)
            sp.wait_ge(done, 16)

        @block.vector
        def _(dve):
            s = Steps(dve, steps)
            dve.wait_ge(loaded, 16)
            for w in range(NW):
                own = FIRST_OWN if w == 0 else W
                s.mark(dve.tensor_reduce(best[:, w:w + 1], raw[:, START[w]:START[w] + own], AX, ALU.max))
            s.settle()
            s.mark(dve.tensor_scalar(seen[:], best[:], 0.0, None, ALU.not_equal))


def l1_project(nc, tag, ident, gain, shift, wkv, gk, latents=None, context=None):
    NORMS = 2 if latents else 1
    with ExitStack() as st:
        a = Alloc(nc, st)
        rows = a.sb(tag + "rows", [P, GT, E]) if context else None
        stats = a.sb(tag + "stats", [P, GT, 6])
        mv = a.sb(tag + "mv", [P, GT, 2])
        var = a.sb(tag + "var", [P, GT])
        rstd = a.sb(tag + "rstd", [P, GT])
        off = a.sb(tag + "off", [P, GT])
        expo = a.sb(tag + "expo", [P, NORMS * GT * H1])
        xn = a.sb(tag + "xn", [P, GT, E])
        xnT = a.sb(tag + "xnT", [P, GT * P])
        sq = a.sb(tag + "sq", [P, NORMS, GT, E])
        ms = a.sb(tag + "ms", [P, NORMS * GT * H1])
        rms = a.sb(tag + "rms", [P, NORMS * GT * H1])
        normed_rows = a.sb(tag + "nr", [P, NORMS, GT, E])
        if context:
            kT_out = a.sb(tag + "kT_out", [P, GT * P])
            v_out = a.sb(tag + "v_out", [P, GT, E])
        ps_x = a.ps(tag + "ps_x", [P, GT, P])
        ps_k = a.ps(tag + "ps_k", [P, GT, E])
        ps_v = a.ps(tag + "ps_v", [P, GT, E])
        ps_q = a.ps(tag + "ps_q", [P, GT, E]) if latents else None
        ps_t = [a.ps(f"{tag}ps_t{i}", [P, GT, P]) for i in range(NORMS)]
        sem = {n: a.sem(tag + n) for n in (
            "loaded expo_set steps stats_ready var_ready rstd_ready xn_ready xnT_ps xnT_sb kv_ps sq_sb v_sb ms_ready rms_ready "
            "nr_ready nT_ps nT_sb k_stored v_stored").split()}
        a.start_at_one()
        block = st.enter_context(nc.Block())

        counts = {}

        def each(eng, body):
            if latents:
                with eng.Fori(0, NT // GT) as g:
                    body(g, g, 0)
                return
            _, flags = context[:2]
            n = counts[eng] = eng.alloc_register(tag + "n")
            eng.reg_mov(n, 0)
            with eng.Fori(0, B) as b:
                for w in range(NW):
                    live = eng.value_load(flags[0:1, bass.ds(b * NW + w, 1)], min_val=0, max_val=1)
                    with eng.If(live != 0):
                        body(eng.snap(n), b, w)
                        eng.reg_add(n, n, 1)

        @block.sync
        def _(sp):
            if latents:
                return
            ctx, _, kT_dram, v_dram = context
            ctx_rows = ctx.rearrange("b k e -> (b k) e")

            def body(done, b, w):
                sp.wait_ge(sem["xn_ready"], ONE + done)
                sp.dma_start(rows[:], ctx_rows[bass.ds(b * KEYS + START[w], W), :].rearrange(
                    "(t p) e -> p t e", p=P)).then_inc(sem["loaded"], 16)
            each(sp, body)

        @block.gpsimd
        def _(pool):
            pool.memset(expo[:], -0.5).then_inc(sem["expo_set"], 1)
            pool.wait_ge(sem["expo_set"], ONE + 1)

            def body(done, b, w):
                pool.wait_ge(sem["var_ready"], ONE + done + 1)
                pool.tensor_tensor(rstd[:], var[:], expo[:, 0:GT], ALU.pow).then_inc(sem["rstd_ready"], 1)
                pool.wait_ge(sem["ms_ready"], ONE + done + 1)
                pool.tensor_tensor(rms[:], ms[:], expo[:], ALU.pow).then_inc(sem["rms_ready"], 1)
            each(pool, body)
            if context:
                pool.wait_ge(sem["v_stored"], ONE + pool.snap(counts[pool]) * 16)
                pool.wait_ge(sem["k_stored"], ONE + pool.snap(counts[pool]) * 16)

        @block.tensor
        def _(pe):
            def body(done, b, w):
                pe.wait_ge(sem["xn_ready"], ONE + done + 1)
                for i in range(GT):
                    mm = pe.transpose(ps_x[:, i, :], xn[:, i, :], ident[:])
                mm.then_inc(sem["xnT_ps"], 1)
                pe.wait_ge(sem["xnT_sb"], ONE + done + 1)
                for bank, weights in ((ps_k, wkv[:, 0:E]), (ps_q, latents[1][:] if latents else None),
                                      (ps_v, wkv[:, E:])):
                    for i in range(GT):
                        if weights is not None:
                            mm = pe.matmul(bank[:, i, :], xnT[:, i * P:(i + 1) * P], weights, start=True, stop=True)
                mm.then_inc(sem["kv_ps"], 1)
                pe.wait_ge(sem["nr_ready"], ONE + done + 1)
                for c in range(NORMS):
                    for i in range(GT):
                        mm = pe.transpose(ps_t[c][:, i, :], normed_rows[:, c, i, :], ident[:])
                mm.then_inc(sem["nT_ps"], 1)
                pe.wait_ge(sem["nT_sb"], ONE + done + 1)
                pe.wait_ge(sem["v_sb"], ONE + done + 1)
            each(pe, body)

        @block.scalar
        def _(act):
            def body(done, b, w):
                act.wait_ge(sem["xnT_ps"], ONE + done + 1)
                act.activation(xnT[:], ps_x[:].rearrange("p t q -> p (t q)"), ACT.Identity, bias=shift[:],
                               scale=gain[:]).then_inc(sem["xnT_sb"], 1)
                act.wait_ge(sem["kv_ps"], ONE + done + 1)
                mm = act.activation(sq[:, 0, :, :], ps_k[:], ACT.Square)
                if latents:
                    mm = act.activation(sq[:, 1, :, :], ps_q[:], ACT.Square)
                mm.then_inc(sem["sq_sb"], 1)
                if context:
                    act.wait_ge(sem["v_stored"], ONE + done * 16)
                    v_to = v_out[:]
                else:
                    v_to = latents[5][:, bass.ds(b * GT, GT), :]
                act.activation(v_to, ps_v[:], ACT.Copy).then_inc(sem["v_sb"], 1)
                act.wait_ge(sem["nT_ps"], ONE + done + 1)
                if context:
                    act.wait_ge(sem["k_stored"], ONE + done * 16)
                    act.activation(kT_out[:], ps_t[0][:].rearrange("p t q -> p (t q)"), ACT.Copy,
                                   scale=gk[:]).then_inc(sem["nT_sb"], 1)
                    act.wait_ge(sem["v_sb"], ONE + done + 1)
                    act.dma_start(context[3][bass.ds(b, 1), w, :, :].rearrange("o p c -> (o p) c"),
                                  v_out[:].rearrange("p t e -> p (t e)")).then_inc(sem["v_stored"], 16)
                    act.wait_ge(sem["nT_sb"], ONE + done + 1)
                    act.dma_start(context[2][bass.ds(b, 1), w, :, :].rearrange("o p c -> (o p) c"),
                                  kT_out[:]).then_inc(sem["k_stored"], 16)
                else:
                    act.activation(latents[4][:, bass.ds(b * GT * P, GT * P)], ps_t[0][:].rearrange(
                        "p t q -> p (t q)"), ACT.Copy, scale=gk[:])
                    act.activation(latents[3][:, bass.ds(b * GT * P, GT * P)], ps_t[1][:].rearrange(
                        "p t q -> p (t q)"), ACT.Copy, scale=latents[2][:]).then_inc(sem["nT_sb"], 1)
            each(act, body)

        @block.vector
        def _(dve):
            total = dve.alloc_register(tag + "steps")
            dve.reg_mov(total, ONE)
            stats_in = Awaited(dve, sem["stats_ready"], tag + "stats_at")

            def body(done, b, w):
                s = Steps(dve, sem["steps"], dve.snap(total))
                if context:
                    dve.wait_ge(sem["loaded"], ONE + (done + 1) * 16)
                    row = lambda i: rows[:, i, :]
                else:
                    row = lambda i: latents[0][:, bass.ds(b * GT + i, 1), :].rearrange("p o e -> p (o e)")
                for i in range(GT):
                    ins = dve.bn_stats(stats[:, i, :], row(i))
                ins.then_inc(sem["stats_ready"], 1)
                stats_in.wait()
                for i in range(GT):
                    s.mark(dve.bn_aggr(mv[:, i, :], stats[:, i, :]))
                s.settle()
                dve.tensor_scalar(var[:], mv[:, :, 1], EPS, None, ALU.add).then_inc(sem["var_ready"], 1)
                dve.wait_ge(sem["rstd_ready"], ONE + done + 1)
                s.mark(dve.scalar_tensor_tensor(off[:], mv[:, :, 0], -1.0, rstd[:], ALU.mult, ALU.mult))
                s.settle()
                dve.wait_ge(sem["xnT_ps"], ONE + done)
                for i in range(GT):
                    ins = dve.tensor_scalar(xn[:, i, :], row(i), rstd[:, i:i + 1], off[:, i:i + 1], ALU.mult, ALU.add)
                ins.then_inc(sem["xn_ready"], 1)
                dve.wait_ge(sem["sq_sb"], ONE + done + 1)
                s.mark(dve.tensor_reduce(ms[:], sq[:].rearrange("p c t (h d) -> p (c t h) d", d=D1), AX, ALU.add))
                s.settle()
                dve.tensor_scalar(ms[:], ms[:], 1.0 / D1, RMS_EPS ** 2, ALU.mult, ALU.max).then_inc(sem["ms_ready"], 1)
                dve.wait_ge(sem["rms_ready"], ONE + done + 1)
                dve.wait_ge(sem["nT_ps"], ONE + done)
                for c in range(NORMS):
                    from_ps = ps_k[:] if c == 0 else ps_q[:]
                    by_head = rms[:, c * GT * H1:(c + 1) * GT * H1].rearrange("p (t h) -> p t h", h=H1).unsqueeze(
                        3).broadcast_to([P, GT, H1, D1])
                    ins = dve.tensor_tensor(normed_rows[:, c, :, :].rearrange("p t (h d) -> p t h d", d=D1),
                                            from_ps.rearrange("p t (h d) -> p t h d", d=D1), by_head, ALU.mult)
                ins.then_inc(sem["nr_ready"], 1)
                dve.reg_add(total, total, s.n)
            each(dve, body)


def l1_attention(nc, x_sb, ident, flags, mask, qT, klT, vl, kT_dram, v_dram, wout, bout):
    mask_flat = mask.rearrange("b k -> (b k)")
    with ExitStack() as st:
        a = Alloc(nc, st)
        qbd = a.sb("b_qbd", [P, 2, H1, S])
        kT = a.sb("b_kT", [P, W])
        v = a.sb("b_v", [P, KT, E])
        raw = a.sb("b_raw", [P, W], U8)
        neg = a.sb("b_neg", [P, W])
        none = a.sb("b_none", [P, S])
        scores = a.sb("b_scores", [P, PAIRS, W])
        probsT = a.sb("b_probsT", [P, PAIRS, KT, P])
        m_old, m_src, m_new, m_diff, alpha, neg_m, l_src, l_sum = (
            a.sb("b_" + n, [P, PAIRS]) for n in "m_old m_src m_new m_diff alpha neg_m l_src l_sum".split())
        acc = a.sb("b_acc", [P, QT, H1, D1])
        heads = a.sb("b_heads", [P, QT, E])
        headsT = a.sb("b_headsT", [P, S])
        ps_s = [a.ps(f"b_ps_s{i}", [P, W]) for i in range(2)]
        ps_t = [a.ps(f"b_ps_t{i}", [P, KT, P]) for i in range(2)]
        ps_o = a.ps("b_ps_o", [P, QT, H1, D1])
        ps_h = a.ps("b_ps_h", [P, S])
        ps_y = a.ps("b_ps_y", [P, QT, E])
        sem = {n: a.sem("b_" + n) for n in (
            "qbd_zeroed qbd_ready k_loaded v_loaded m_loaded s_ps s_sb neg_m_ready alpha_ready p_sb t_ps t_act t_dve "
            "o_ps acc_done heads_ready headsT_ps headsT_sb y_ps x_done steps src_done").split()}
        a.start_at_one()
        block = st.enter_context(nc.Block())

        def each_window(eng, n, m, b, body):
            for w in range(NW):
                live = eng.value_load(flags[0:1, bass.ds(b * NW + w, 1)], min_val=0, max_val=1)
                with eng.If(live != 0):
                    body(eng.snap(n), eng.snap(m), w)
                    eng.reg_add(n, n, 1)
                    eng.reg_add(m, m, 1)

        def counters(eng):
            n, m = eng.alloc_register("b_n_sources"), eng.alloc_register("b_n_windows")
            eng.reg_mov(n, 0)
            eng.reg_mov(m, 0)
            return n, m

        @block.sync
        def _(sp):
            n, m = counters(sp)
            with sp.Fori(0, B) as b:
                sp.reg_add(n, n, 1)

                def load(src, win, w):
                    sp.wait_ge(sem["o_ps"], ONE + src)
                    sp.dma_start(kT[:], kT_dram[bass.ds(b, 1), w, :, :].rearrange("o p c -> (o p) c")).then_inc(
                        sem["k_loaded"], 16)
                    sp.dma_start(raw[:], mask_flat[bass.ds(b * KEYS + START[w], W)].partition_broadcast(P)).then_inc(
                        sem["m_loaded"], 16)
                    sp.dma_start(v[:].rearrange("p t e -> p (t e)"), v_dram[bass.ds(b, 1), w, :, :].rearrange(
                        "o p c -> (o p) c")).then_inc(sem["v_loaded"], 16)
                each_window(sp, n, m, b, load)

        @block.gpsimd
        def _(pool):
            pool.memset(qbd[:], 0.0).then_inc(sem["qbd_zeroed"], 1)
            pool.wait_ge(sem["qbd_zeroed"], ONE + 1)

            def spread(b, half):
                pool.wait_ge(sem["headsT_ps"], ONE + b - half)
                for h in range(H1):
                    rows = slice(h * D1, (h + 1) * D1)
                    ins = pool.tensor_copy(qbd[rows, half, h, :], qT[rows, bass.ds(b * S, S)])
                    ins.then_inc(sem["qbd_ready"], 1)
            with pool.Fori(0, B // 2) as i:
                spread(i * 2, 0)
                spread(i * 2 + 1, 1)

        @block.tensor
        def _(pe):
            n, m = counters(pe)

            def source(src, half, tiles, key, value):
                for j in range(PAIRS):
                    h, t = j // QT, j % QT
                    pe.wait_ge(sem["s_sb"], ONE + src * PAIRS + max(j - 1, 0))
                    pe.matmul(ps_s[j % 2][:, 0:tiles * P], qbd[:, half, h, t * P:(t + 1) * P], key, start=True,
                              stop=True).then_inc(sem["s_ps"], 1)
                for j in range(PAIRS):
                    pe.wait_ge(sem["p_sb"], ONE + src * PAIRS + j + 1)
                    pe.wait_ge(sem["t_act" if j % 2 == 0 else "t_dve"], ONE + src * (PAIRS // 2) + j // 2)
                    for k in range(tiles):
                        mm = pe.transpose(ps_t[j % 2][:, k, :], scores[:, j, k * P:(k + 1) * P], ident[:])
                    mm.then_inc(sem["t_ps"], 1)
                pe.wait_ge(sem["acc_done"], ONE + src)
                for j in range(PAIRS):
                    h, t = j // QT, j % QT
                    pe.wait_ge(sem["t_act" if j % 2 == 0 else "t_dve"], ONE + src * (PAIRS // 2) + j // 2 + 1)
                    for k in range(tiles):
                        mm = pe.matmul(ps_o[:, t, h, :], probsT[:, j, k, :], value(k, h), start=(k == 0),
                                       stop=(k == tiles - 1))
                mm.then_inc(sem["o_ps"], 1)

            def batch(b, half):
                pe.wait_ge(sem["qbd_ready"], ONE + b * H1 + H1)
                source(pe.snap(n), half, LK, klT[:, bass.ds(b * S, S)],
                       lambda k, h: vl[:, bass.ds(b * LK + k, 1), h * D1:(h + 1) * D1].rearrange("p o d -> p (o d)"))
                pe.reg_add(n, n, 1)

                def window(src, win, w):
                    pe.wait_ge(sem["k_loaded"], ONE + (win + 1) * 16)
                    pe.wait_ge(sem["v_loaded"], ONE + (win + 1) * 16)
                    source(src, half, KT, kT[:], lambda k, h: v[:, k, h * D1:(h + 1) * D1])
                each_window(pe, n, m, b, window)
                pe.wait_ge(sem["heads_ready"], ONE + b + 1)
                for t in range(QT):
                    mm = pe.transpose(ps_h[:, t * P:(t + 1) * P], heads[:, t, :], ident[:])
                mm.then_inc(sem["headsT_ps"], 1)
                pe.wait_ge(sem["headsT_sb"], ONE + b + 1)
                pe.wait_ge(sem["x_done"], ONE + b)
                for t in range(QT):
                    mm = pe.matmul(ps_y[:, t, :], headsT[:, t * P:(t + 1) * P], wout[:], start=True, stop=True)
                mm.then_inc(sem["y_ps"], 1)

            with pe.Fori(0, B // 2) as i:
                batch(i * 2, 0)
                batch(i * 2 + 1, 1)

        @block.scalar
        def _(act):
            n, m = counters(act)

            def source(src, tiles):
                act.wait_ge(sem["neg_m_ready"], ONE + src + 1)
                act.wait_ge(sem["acc_done"], ONE + src)
                act.activation(alpha[:], m_diff[:], ACT.Exp).then_inc(sem["alpha_ready"], 1)
                for j in range(PAIRS):
                    act.activation(scores[:, j, 0:tiles * P], scores[:, j, 0:tiles * P], ACT.Exp,
                                   bias=neg_m[:, j:j + 1], accum_out=l_src[:, j:j + 1]).then_inc(sem["p_sb"], 1)
                    if j % 2:
                        act.wait_ge(sem["t_ps"], ONE + src * PAIRS + j)
                        act.wait_ge(sem["o_ps"], ONE + src)
                        act.activation(probsT[:, j - 1, 0:tiles, :], ps_t[0][:, 0:tiles, :],
                                       ACT.Copy).then_inc(sem["t_act"], 1)

            with act.Fori(0, B) as b:
                source(act.snap(n), LK)
                act.reg_add(n, n, 1)
                each_window(act, n, m, b, lambda src, win, w: source(src, KT))
                act.wait_ge(sem["headsT_ps"], ONE + b + 1)
                act.wait_ge(sem["y_ps"], ONE + b)
                act.activation(headsT[:], ps_h[:], ACT.Copy).then_inc(sem["headsT_sb"], 1)

        @block.vector
        def _(dve):
            n, m = counters(dve)
            total = dve.alloc_register("b_n_steps")
            dve.reg_mov(total, ONE)
            scores_in = Awaited(dve, sem["s_ps"], "b_s_ps_at")
            dve.memset(none[:], 0.0).then_inc(sem["steps"], 1)
            dve.reg_add(total, total, 1)

            def source(src, s, tiles, added):
                for j in range(PAIRS):
                    at = scores_in.at()
                    if j == 0:
                        dve.wait_ge(sem["t_ps"], ONE + src * PAIRS)
                    scores_in.wait(at)
                    dve.tensor_tensor_reduce(scores[:, j, 0:tiles * P], ps_s[j % 2][:, 0:tiles * P], added, 1.0,
                                             NO_MAX, ALU.add, ALU.max, m_src[:, j:j + 1]).then_inc(sem["s_sb"], 1)
                dve.wait_ge(sem["s_sb"], ONE + src * PAIRS + PAIRS)
                s.mark(dve.tensor_tensor(m_new[:], m_old[:], m_src[:], ALU.max))
                s.settle()
                s.mark(dve.tensor_tensor(m_diff[:], m_old[:], m_new[:], ALU.subtract))
                s.settle()
                s.mark(dve.tensor_copy(m_old[:], m_new[:]))
                dve.tensor_scalar(neg_m[:], m_new[:], -1.0, None, ALU.mult).then_inc(sem["neg_m_ready"], 1)
                for j in range(1, PAIRS, 2):
                    dve.wait_ge(sem["t_ps"], ONE + src * PAIRS + j + 1)
                    dve.wait_ge(sem["o_ps"], ONE + src)
                    dve.tensor_copy(probsT[:, j, 0:tiles, :], ps_t[1][:, 0:tiles, :]).then_inc(sem["t_dve"], 1)
                dve.wait_ge(sem["alpha_ready"], ONE + src + 1)
                dve.wait_ge(sem["p_sb"], ONE + src * PAIRS + PAIRS)
                by_head = alpha[:].rearrange("p (h t) -> p t h", t=QT).unsqueeze(3).broadcast_to([P, QT, H1, D1])
                dve.wait_ge(sem["acc_done"], ONE + src)
                s.mark(dve.tensor_tensor(l_sum[:], l_sum[:], alpha[:], ALU.mult))
                s.mark(dve.tensor_tensor(acc[:], acc[:], by_head, ALU.mult))
                s.settle()
                s.mark(dve.tensor_tensor(l_sum[:], l_sum[:], l_src[:], ALU.add))
                dve.wait_ge(sem["o_ps"], ONE + src + 1)
                dve.tensor_tensor(acc[:], acc[:], ps_o[:], ALU.add).then_inc(sem["acc_done"], 1)
                s.settle()

            with dve.Fori(0, B) as b:
                s = Steps(dve, sem["steps"], dve.snap(total))
                s.mark(dve.memset(m_old[:], NO_MAX))
                s.mark(dve.memset(l_sum[:], 0.0))
                s.mark(dve.memset(acc[:], 0.0))
                s.settle()
                source(dve.snap(n), s, LK, none[:])
                dve.reg_add(n, n, 1)
                dve.reg_add(total, total, s.n)

                def window(src, win, w):
                    s = Steps(dve, sem["steps"], dve.snap(total))
                    dve.wait_ge(sem["m_loaded"], ONE + (win + 1) * 16)
                    own = FIRST_OWN if w == 0 else W
                    s.mark(dve.tensor_scalar(neg[:, 0:own], raw[:, 0:own], 0.0, MASKED, ALU.is_equal, ALU.mult))
                    if own < W:
                        s.mark(dve.memset(neg[:, own:], DOUBLED))
                    s.settle()
                    source(src, s, KT, neg[:])
                    dve.reg_add(total, total, s.n)
                each_window(dve, n, m, b, window)
                s = Steps(dve, sem["steps"], dve.snap(total))
                dve.wait_ge(sem["acc_done"], ONE + dve.snap(n))
                s.mark(dve.reciprocal(l_sum[:], l_sum[:]))
                s.settle()
                by_head = l_sum[:].rearrange("p (h t) -> p t h", t=QT).unsqueeze(3).broadcast_to([P, QT, H1, D1])
                dve.wait_ge(sem["headsT_ps"], ONE + b)
                dve.tensor_tensor(heads[:].rearrange("p t (h d) -> p t h d", d=D1), acc[:], by_head,
                                  ALU.mult).then_inc(sem["heads_ready"], 1)
                dve.wait_ge(sem["y_ps"], ONE + b + 1)
                x_b = x_sb[:, bass.ds(b * QT, QT), :]
                s.mark(dve.tensor_tensor(x_b, x_b, ps_y[:], ALU.add))
                s.settle()
                dve.tensor_tensor(x_b, x_b, bout[:].unsqueeze(1).broadcast_to([P, QT, E]),
                                  ALU.add).then_inc(sem["x_done"], 1)
                dve.reg_add(total, total, s.n)
            dve.wait_ge(sem["x_done"], ONE + B)


E1, I1 = 32, 256
TILES = NT + E1 - 1
TP = -(-TILES // 2)
SLOTS = 2 * TP * P


def l1_route(nc, xln, xlnT, gate, position, expert_of, n_tiles):
    with ExitStack() as st:
        a = Alloc(nc, st)
        best = a.sb("g_best", [P, NT])
        score = a.sb("g_score", [P, NT])
        choice = a.sb("g_choice", [P, NT])
        num = a.sb("g_num", [P, E1], I32)
        num_f = a.sb("g_num_f", [P, E1])
        mark = a.sb("g_mark", [P, NT, E1])
        hot = a.sb("g_hot", [P, NT, E1], BF16)
        below = a.sb("g_below", [P, P], BF16)
        ones = a.sb("g_ones", [P, P], BF16)
        before = [a.sb(f"g_before{i}", [P, NT, E1]) for i in range(2)]
        size = a.sb("g_size", [P, E1])
        tiles_of = a.sb("g_tiles_of", [P, E1])
        end = [a.sb(f"g_end{i}", [P, E1]) for i in range(2)]
        slot = a.sb("g_slot", [P, NT])
        tile_num = a.sb("g_tile_num", [1, 2 * TP], I32)
        tile_num_f = a.sb("g_tile_num_f", [1, 2 * TP])
        past = a.sb("g_past", [1, 2 * TP, E1])
        tile_expert = a.sb("g_tile_expert", [1, 2 * TP])
        ps_l = a.ps("g_ps_l", [P, NT, E1])
        ps_r = a.ps("g_ps_r", [P, NT, E1])
        ps_c = a.ps("g_ps_c", [P, NT, E1])
        logits, consts, best_ready, scored, hot_ready, counted, steps = (
            a.sem("g_s_" + n) for n in "logits consts best scored hot counted steps".split())
        block = st.enter_context(nc.Block())
        HALF = NT // 2

        @block.gpsimd
        def _(pool):
            pool.iota(num[:], [[1, E1]], base=0, channel_multiplier=0).then_inc(consts, 1)
            pool.iota(tile_num[:], [[1, 2 * TP]], base=0, channel_multiplier=0).then_inc(consts, 1)
            pool.memset(ones[:], 1.0).then_inc(consts, 1)
            pool.memset(below[:], 1.0).then_inc(consts, 1)
            pool.wait_ge(consts, 4)
            pool.affine_select(out=below[:], in_=below[:], compare_op=ALU.is_gt, fill=0.0, base=0,
                               pattern=[[1, P]], channel_multiplier=-1).then_inc(consts, 1)

        @block.tensor
        def _(pe):
            for t in range(NT):
                mm = pe.matmul(ps_l[:, t, :], xlnT[:, t * P:(t + 1) * P], gate[:], start=True, stop=True)
            mm.then_inc(logits, 1)
            pe.wait_ge(hot_ready, 1)
            pe.wait_ge(consts, 5)
            for i in range(2):
                pe.matmul(ps_r[:, i * HALF:(i + 1) * HALF, :], below[:], hot[:, i * HALF:(i + 1) * HALF, :],
                          start=True, stop=True)
                mm = pe.matmul(ps_c[:, i * HALF:(i + 1) * HALF, :], ones[:], hot[:, i * HALF:(i + 1) * HALF, :],
                               start=True, stop=True)
            mm.then_inc(counted, 1)

        @block.scalar
        def _(act):
            act.wait_ge(best_ready, 1)
            act.activation(score[:], best[:], ACT.Sigmoid).then_inc(scored, 1)

        @block.vector
        def _(dve):
            s = Steps(dve, steps)
            full = [P, NT, E1]
            dve.wait_ge(logits, 1)
            dve.tensor_reduce(best[:], ps_l[:], AX, ALU.max).then_inc(best_ready, 1)
            dve.wait_ge(best_ready, 1)
            dve.wait_ge(consts, 5)
            s.mark(dve.tensor_copy(num_f[:], num[:]))
            s.mark(dve.tensor_copy(tile_num_f[:], tile_num[:]))
            s.mark(dve.tensor_tensor(mark[:], ps_l[:], best[:].unsqueeze(2).broadcast_to(full), ALU.is_equal))
            s.settle()
            s.mark(dve.tensor_scalar(size[:], num_f[:], -float(E1), None, ALU.add))
            s.settle()
            s.mark(dve.tensor_tensor(mark[:], mark[:], size[:].unsqueeze(1).broadcast_to(full), ALU.mult))
            s.settle()
            s.mark(dve.tensor_reduce(choice[:], mark[:], AX, ALU.min))
            s.settle()
            s.mark(dve.tensor_scalar(choice[:], choice[:], float(E1), None, ALU.add))
            s.settle()
            dve.tensor_tensor(hot[:], num_f[:].unsqueeze(1).broadcast_to(full),
                              choice[:].unsqueeze(2).broadcast_to(full), ALU.is_equal).then_inc(hot_ready, 1)
            dve.wait_ge(scored, 1)
            s.mark(dve.tensor_tensor(xln[:], xln[:], score[:].unsqueeze(2).broadcast_to([P, NT, E]), ALU.mult))
            dve.wait_ge(counted, 1)
            s.mark(dve.tensor_copy(before[0][:], ps_c[:]))
            s.settle()
            step, cur = 1, 0
            while step < NT:
                s.mark(dve.tensor_copy(before[1 - cur][:, 0:step, :], before[cur][:, 0:step, :]))
                s.mark(dve.tensor_tensor(before[1 - cur][:, step:, :], before[cur][:, step:, :],
                                         before[cur][:, 0:NT - step, :], ALU.add))
                s.settle()
                cur, step = 1 - cur, step * 2
            s.mark(dve.tensor_copy(size[:], before[cur][:, NT - 1, :]))
            s.settle()
            s.mark(dve.tensor_scalar(end[0][:], num_f[:], float(P), None, ALU.mult))
            s.settle()
            s.mark(dve.tensor_tensor(mark[:, 0:E1, :], size[:].unsqueeze(2).broadcast_to([P, E1, NT]),
                                     end[0][:].unsqueeze(1).broadcast_to([P, E1, NT]), ALU.is_gt))
            s.settle()
            s.mark(dve.tensor_reduce(tiles_of[:], mark[:], AX, ALU.add))
            s.settle()
            s.mark(dve.tensor_copy(end[0][:], tiles_of[:]))
            s.settle()
            step, at = 1, 0
            while step < E1:
                s.mark(dve.tensor_copy(end[1 - at][:, 0:step], end[at][:, 0:step]))
                s.mark(dve.tensor_tensor(end[1 - at][:, step:], end[at][:, step:], end[at][:, 0:E1 - step], ALU.add))
                s.settle()
                at, step = 1 - at, step * 2
            s.mark(dve.tensor_tensor(past[:], end[at][0:1, :].unsqueeze(1).broadcast_to([1, 2 * TP, E1]),
                                     tile_num_f[:].unsqueeze(2).broadcast_to([1, 2 * TP, E1]), ALU.is_le))
            s.mark(dve.tensor_copy(n_tiles[:], end[at][0:1, E1 - 1:E1]))
            s.mark(dve.tensor_tensor(size[:], end[at][:], tiles_of[:], ALU.subtract))
            s.settle()
            s.mark(dve.tensor_reduce(tile_expert[:], past[:], AX, ALU.add))
            s.mark(dve.tensor_scalar(size[:], size[:], float(P), None, ALU.mult))
            s.mark(dve.tensor_tensor(before[cur][:], before[cur][:], ps_c[:], ALU.subtract))
            s.settle()
            s.mark(dve.tensor_scalar(expert_of[:], tile_expert[:], float(E1 - 1), None, ALU.min))
            s.mark(dve.tensor_tensor(before[cur][:], before[cur][:], ps_r[:], ALU.add))
            s.settle()
            s.mark(dve.tensor_tensor(before[cur][:], before[cur][:], size[:].unsqueeze(1).broadcast_to(full), ALU.add))
            s.settle()
            s.mark(dve.tensor_tensor(before[cur][:], before[cur][:], hot[:], ALU.mult))
            s.settle()
            s.mark(dve.tensor_reduce(slot[:], before[cur][:], AX, ALU.add))
            s.settle()
            s.mark(dve.tensor_copy(position[:], slot[:]))
            s.settle()


def start_clearing(nc, zeros, tables, cleared):
    with ExitStack() as st:
        zero_ready = Alloc(nc, st).sem("z_ready")
        block = st.enter_context(nc.Block())
        parts = SLOTS // P // 8

        @block.vector
        def _(dve):
            dve.memset(zeros[:], 0.0).then_inc(zero_ready, 1)

        @block.sync
        def _(sp):
            sp.wait_ge(zero_ready, 1)
            for i in range(parts):
                for table in tables:
                    sp.dma_start(table[i * 8 * P:(i + 1) * 8 * P, :].rearrange("(p t) e -> p t e", p=P),
                                 zeros[:]).then_inc(cleared, 16)
    return parts * len(tables)


def l1_shared(nc, x_sb, xlnT, wgu, wd, xln, position, sorted_x, cleared, n_cleared):
    with ExitStack() as st:
        sent = Alloc(nc, st).sem("z_sent")
        a = Alloc(nc, st)
        act_g = a.sb("s_act_g", [P, 2, CH])
        hid = a.sb("s_hid", [P, 2, CH])
        ps_g = a.ps("s_ps_g", [P, 2, CH])
        ps_u = a.ps("s_ps_u", [P, 2, CH])
        ps_y = [a.ps(f"s_ps_y{i}", [P, CT, E]) for i in range(1)]
        g_ps, u_ps, g_sb, hid_ready, y_ps, y_added = (a.sem("s_" + n) for n in "g_ps u_ps g_sb hid y_ps y_added".split())
        a.start_at_one()
        block = st.enter_context(nc.Block())
        CHUNKS = NT * P // CH

        @block.gpsimd
        def _(pool):
            pool.wait_ge(cleared, 16 * n_cleared)
            for t in range(NT):
                pool.indirect_dma_start(sorted_x, bass.IndirectOffsetOnAxis(ap=position[:, t:t + 1], axis=0),
                                        xln[:, t, :], None).then_inc(sent, 16)
            pool.wait_ge(sent, 16 * NT)

        @block.tensor
        def _(pe):
            with pe.Fori(0, CHUNKS) as c:
                for bank, off, free, seen in ((ps_g, 0, g_sb, g_ps), (ps_u, I1, hid_ready, u_ps)):
                    pe.wait_ge(free, ONE + c * 2)
                    for half in range(2):
                        pe.matmul(bank[:, half, :], wgu[:, off + half * P:off + (half + 1) * P],
                                  xlnT[:, bass.ds(c * CH, CH)], start=True, stop=True).then_inc(seen, 1)
                pe.wait_ge(hid_ready, ONE + c * 2 + 2)
                pe.wait_ge(y_added, ONE + c)
                for t in range(CT):
                    for half in range(2):
                        mm = pe.matmul(ps_y[0][:, t, :], hid[:, half, t * P:(t + 1) * P], wd[:, half, :],
                                       start=(half == 0), stop=(half == 1))
                mm.then_inc(y_ps, 1)

        @block.scalar
        def _(act):
            with act.Fori(0, CHUNKS) as c:
                for half in range(2):
                    act.wait_ge(g_ps, ONE + c * 2 + half + 1)
                    act.wait_ge(hid_ready, ONE + c * 2)
                    act.activation(act_g[:, half, :], ps_g[:, half, :], ACT.Silu).then_inc(g_sb, 1)

        @block.vector
        def _(dve):
            with dve.Fori(0, CHUNKS) as c:
                for half in range(2):
                    dve.wait_ge(g_sb, ONE + c * 2 + half + 1)
                    dve.wait_ge(u_ps, ONE + c * 2 + half + 1)
                    dve.wait_ge(y_ps, ONE + c)
                    dve.tensor_tensor(hid[:, half, :], act_g[:, half, :], ps_u[:, half, :],
                                      ALU.mult).then_inc(hid_ready, 1)
                dve.wait_ge(y_ps, ONE + c + 1)
                x_c = x_sb[:, bass.ds(c * CT, CT), :]
                dve.tensor_tensor(x_c, x_c, ps_y[0][:], ALU.add).then_inc(y_added, 1)
            dve.wait_ge(y_added, ONE + CHUNKS)


def l1_routed(nc, ident, sorted_x, sorted_y, wgu, wd, expert_of, n_tiles):
    with ExitStack() as st:
        a = Alloc(nc, st)
        rows = a.sb("x_rows", [P, 2, 2, E])
        rowsT = a.sb("x_rowsT", [P, 2, 2, P])
        act_g = a.sb("x_act_g", [P, 2, 2, I1])
        hid = a.sb("x_hid", [P, 2, 2, I1])
        hidT = a.sb("x_hidT", [P, 2, 2, 2, P])
        y = a.sb("x_y", [P, 2, 2, E])
        ps_t = a.ps("x_ps_t", [P, 2, P])
        ps_gu = [a.ps(f"x_ps_gu{i}", [P, 2, 2 * I1]) for i in range(2)]
        ps_h = a.ps("x_ps_h", [P, 2, 2, P])
        ps_y = a.ps("x_ps_y", [P, 2, E])
        sem = {n: a.sem("x_" + n) for n in (
            "loaded0 loaded1 rowsT_ps rowsT_sb gu_ps act_ready hid_ready hidT_ps hidT_sb y_ps y_sb stored0 stored1").split()}
        a.start_at_one()
        block = st.enter_context(nc.Block())

        def first(i):
            return isinstance(i, int) and i == 0

        def pipeline(eng, enter, leave):
            count = eng.value_load(n_tiles[0:1, 0:1], min_val=NT, max_val=TILES)
            enter(0, 0)
            with eng.Fori(0, TP // 2 - 1) as j:
                for half in range(2):
                    i = j * 2 + half
                    with eng.If(count > (i + 1) * 2):
                        enter(i + 1, 1 - half)
                    with eng.If(count > i * 2):
                        leave(i, half)
            with eng.If(count > (TP - 1) * 2):
                enter(TP - 1, 1)
            with eng.If(count > (TP - 2) * 2):
                leave(TP - 2, 0)
            with eng.If(count > (TP - 1) * 2):
                leave(TP - 1, 1)

        @block.sync
        def _(sp):
            def load(i, half):
                row = i * 2 * P if isinstance(i, int) else sp.snap(i * 2 * P)
                if not first(i):
                    sp.wait_ge(sem["rowsT_ps"], ONE + i - 1)
                sp.dma_start(rows[:, half, :, :], sorted_x[bass.ds(row, 2 * P), :].rearrange(
                    "(t p) e -> p t e", p=P)).then_inc(sem[f"loaded{half}"], 16)

            def store(i, half):
                row, y_at = i * 2 * P, ONE + i + 1
                if not isinstance(i, int):
                    row, y_at = sp.snap(row), sp.snap(y_at)
                sp.wait_ge(sem["y_sb"], y_at)
                sp.dma_start(sorted_y[bass.ds(row, 2 * P), :].rearrange("(t p) e -> p t e", p=P),
                             y[:, half, :, :]).then_inc(sem[f"stored{half}"], 16)
            pipeline(sp, load, store)

        @block.tensor
        def _(pe):
            def up(i, half):
                pe.wait_ge(sem[f"loaded{half}"], ONE + (i - half) * 8 + 16)
                if not first(i):
                    pe.wait_ge(sem["rowsT_sb"], ONE + i)
                for t in range(2):
                    mm = pe.transpose(ps_t[:, t, :], rows[:, half, t, :], ident[:])
                mm.then_inc(sem["rowsT_ps"], 1)
                pe.wait_ge(sem["rowsT_sb"], ONE + i + 1)
                if not first(i):
                    pe.wait_ge(sem["hid_ready"], ONE + i - 1)
                for t in range(2):
                    e = pe.value_load(expert_of[0:1, bass.ds(i * 2 + t, 1)], min_val=0, max_val=E1 - 1)
                    mm = pe.matmul(ps_gu[half][:, t, :], rowsT[:, half, t, :],
                                   wgu[:, bass.ds(e, 1), :].rearrange("p o c -> p (o c)"), start=True, stop=True)
                mm.then_inc(sem["gu_ps"], 1)

            def down(i, half):
                pe.wait_ge(sem["hid_ready"], ONE + i + 1)
                pe.wait_ge(sem["hidT_sb"], ONE + i)
                for t in range(2):
                    for k in range(2):
                        mm = pe.transpose(ps_h[:, t, k, :], hid[:, half, t, k * P:(k + 1) * P], ident[:])
                mm.then_inc(sem["hidT_ps"], 1)
                pe.wait_ge(sem["hidT_sb"], ONE + i + 1)
                pe.wait_ge(sem["y_sb"], ONE + i)
                for t in range(2):
                    e = pe.value_load(expert_of[0:1, bass.ds(i * 2 + t, 1)], min_val=0, max_val=E1 - 1)
                    for k in range(2):
                        mm = pe.matmul(ps_y[:, t, :], hidT[:, half, t, k, :],
                                       wd[:, bass.ds(e, 1), k, :].rearrange("p o c -> p (o c)"), start=(k == 0),
                                       stop=(k == 1))
                mm.then_inc(sem["y_ps"], 1)
            pipeline(pe, up, down)

        @block.scalar
        def _(act):
            def up(i, half):
                act.wait_ge(sem["gu_ps"], ONE + i + 1)
                if not first(i):
                    act.wait_ge(sem["hid_ready"], ONE + i - 1)
                act.activation(act_g[:, half, :, :], ps_gu[half][:, :, 0:I1], ACT.Silu).then_inc(sem["act_ready"], 1)

            def down(i, half):
                act.wait_ge(sem["hidT_ps"], ONE + i + 1)
                act.activation(hidT[:, half, :, :, :], ps_h[:], ACT.Copy).then_inc(sem["hidT_sb"], 1)
            pipeline(act, up, down)

        @block.vector
        def _(dve):
            def up(i, half):
                dve.wait_ge(sem["rowsT_ps"], ONE + i + 1)
                if not first(i):
                    dve.wait_ge(sem["gu_ps"], ONE + i - 1)
                dve.tensor_copy(rowsT[:, half, :, :], ps_t[:]).then_inc(sem["rowsT_sb"], 1)
                dve.wait_ge(sem["act_ready"], ONE + i + 1)
                if not first(i):
                    dve.wait_ge(sem["hidT_ps"], ONE + i - 1)
                dve.tensor_tensor(hid[:, half, :, :], act_g[:, half, :, :], ps_gu[half][:, :, I1:],
                                  ALU.mult).then_inc(sem["hid_ready"], 1)

            def down(i, half):
                dve.wait_ge(sem["y_ps"], ONE + i + 1)
                dve.wait_ge(sem[f"stored{half}"], ONE + (i - half) * 8)
                dve.tensor_copy(y[:, half, :, :], ps_y[:]).then_inc(sem["y_sb"], 1)
            pipeline(dve, up, down)

        @block.gpsimd
        def _(pool):
            count = pool.value_load(n_tiles[0:1, 0:1], min_val=NT, max_val=TILES)
            pool.wait_ge(sem["stored0"], ONE + (count + 3) // 4 * 16)
            pool.wait_ge(sem["stored1"], ONE + (count + 1) // 4 * 16)


def l1_gather(nc, x_sb, got, position, sorted_y, out):
    with ExitStack() as st:
        a = Alloc(nc, st)
        GROUPS = 8
        per = NT // GROUPS
        fetched = [a.sem(f"o_fetched{g}") for g in range(GROUPS)]
        added, stored = a.sem("o_added"), a.sem("o_stored")
        block = st.enter_context(nc.Block())

        @block.gpsimd
        def _(pool):
            for t in range(NT):
                pool.indirect_dma_start(got[:, t, :], None, sorted_y, bass.IndirectOffsetOnAxis(
                    ap=position[:, t:t + 1], axis=0)).then_inc(fetched[t // per], 16)

        @block.vector
        def _(dve):
            for g in range(GROUPS):
                dve.wait_ge(fetched[g], 16 * per)
                part = slice(g * per, (g + 1) * per)
                dve.tensor_tensor(x_sb[:, part, :], x_sb[:, part, :], got[:, part, :], ALU.add).then_inc(added, 1)

        @block.sync
        def _(sp):
            for g in range(GROUPS):
                sp.wait_ge(added, g + 1)
                part = slice(g * per, (g + 1) * per)
                sp.dma_start(out.rearrange("b (t p) e -> p (b t) e", p=P)[:, part, :],
                             x_sb[:, part, :]).then_inc(stored, 16)
            sp.wait_ge(stored, 16 * GROUPS)


_IN = ["x", "ctx_1024", "mask_SxS2_ik0", "mask_BxS2_bk0", "L0_xattn_Wk", "L0_xattn_bk", "L0_xattn_Wq", "L0_xattn_bq",
       "L0_xattn_Wv", "L0_xattn_bv", "L0_xattn_Wp", "L0_xattn_bp", "L0_ffn_router_w", "L0_ffn_router_b", "L0_ffn_w1",
       "L0_ffn_b1", "L0_ffn_w2", "L0_ffn_b2", "L1_xattn_ln_x_g", "L1_xattn_ln_x_b", "L1_xattn_ln_l_g",
       "L1_xattn_ln_l_b", "L1_xattn_q_gamma", "L1_xattn_k_gamma", "L1_xattn_W_q", "L1_xattn_W_kv", "L1_xattn_W_out",
       "L1_xattn_b_out", "L1_ffn_gate_w", "L1_ffn_shared_gate_w", "L1_ffn_shared_up_w", "L1_ffn_shared_down_w",
       "L1_ffn_routed_gate_w", "L1_ffn_routed_up_w", "L1_ffn_routed_down_w"]


def scale_column(nc, column, factor):
    with ExitStack() as st:
        done = Alloc(nc, st).sem("column_scaled")
        block = st.enter_context(nc.Block())

        @block.vector
        def _(dve):
            dve.tensor_scalar(column, column, factor, None, ALU.mult).then_inc(done, 1)
            dve.wait_ge(done, 1)


def build_program(nc, d, out):
    flag_scratch = nc.dram_tensor("flag_scratch", (B, NW), I32, kind="Internal").ap()
    kT_scratch = nc.dram_tensor("kT_scratch", (B, NW, P, W), F32, kind="Internal").ap()
    v_scratch = nc.dram_tensor("v_scratch", (B, NW, P, W), F32, kind="Internal").ap()
    sorted_x = nc.dram_tensor("sorted_x", (SLOTS, E), F32, kind="Internal").ap()
    sorted_y = nc.dram_tensor("sorted_y", (SLOTS, E), F32, kind="Internal").ap()
    with ExitStack() as whole:
        keep = Alloc(nc, whole)
        x_sb = keep.sb("x_sb", [P, NT, E])
        xln = keep.sb("xln", [P, NT, E])
        ident = keep.sb("ident", [P, P])
        load_tokens(nc, d["x"], x_sb, ident)

        with ExitStack() as st:
            a = Alloc(nc, st)
            xlnT = a.sb("xlnT0", [P, NT * P])
            mneg = a.sb("mneg", [P, QT, NW, W])
            flags = a.sb("flags0", [1, 2 * NW], I32)
            wqT, wkT, wvT, wpT, bv, bp = (a.sb("a0" + n, [P, P]) for n in "wqT wkT wvT wpT bv bp".split())
            bq, bk = a.sb("a0bq", [P, 1]), a.sb("a0bk", [P, 1])
            turn_weights(nc, "w0", [(d["L0_xattn_Wq"], wqT[:]), (d["L0_xattn_Wk"], wkT[:]), (d["L0_xattn_Wv"], wvT[:]),
                                    (d["L0_xattn_Wp"], wpT[:])], ident,
                         columns=[(d["L0_xattn_bq"], bq[:]), (d["L0_xattn_bk"], bk[:])],
                         rows=[(d["L0_xattn_bv"], bv[:]), (d["L0_xattn_bp"], bp[:])])
            layer_norm(nc, "ln0", x_sb, xln, NT, xlnT, ident)
            l0_mask(nc, d["mask_SxS2_ik0"], mneg, flags, ident)
            l0_attention(nc, x_sb, xlnT, mneg, flags, ident, d["ctx_1024"], (wqT, wkT, wvT, wpT, bq, bk, bv, bp))

        small = Alloc(nc, whole)
        ctx_gain, ctx_shift, lat_gain, lat_shift, gq, gk = (
            small.sb("a1" + n, [P, 1]) for n in "ctx_gain ctx_shift lat_gain lat_shift gq gk".split())
        wq, wkv, wout, bout = (small.sb(n, [P, c]) for n, c in (("wq", E), ("wkv", 2 * E), ("wout", E), ("bout", E)))
        gate, shared_gu = small.sb("gate", [P, E1]), small.sb("shared_gu", [P, 2 * I1])
        shared_d = small.sb("shared_d", [P, 2, E])
        flags = small.sb("flags1", [1, B * NW], I32)
        small_loaded = small.sem("small_loaded")
        with ExitStack() as st:
            a = Alloc(nc, st)
            xlnT = a.sb("xlnT1", [P, NT * P])
            rw, rb = a.sb("rw", [P, E0]), a.sb("rb", [P, E0])
            w1, w2 = a.sb("w1", [P, E0, I0]), a.sb("w2", [P, E0, 2, E])
            b1, b2 = a.sb("b1", [P, E0, 2]), a.sb("b2", [E0, E])
            weight = a.sb("weight", [P, NT, E0])
            router_loaded, experts_loaded = a.sem("router_loaded"), a.sem("experts_loaded")
            n_router = start_loads(nc, router_loaded, rows=[(d["L0_ffn_router_b"], rb[:])], others=[
                (d["L0_ffn_router_w"], rw[:]), (d["L0_ffn_b2"], b2[:])])
            with nc.allow_non_contiguous_dma(reason="biases by feature, 16 KB in all"):
                n_experts = start_loads(nc, experts_loaded, others=[
                    (d["L0_ffn_w1"].rearrange("e h i -> h e i"), w1[:]),
                    (d["L0_ffn_w2"].rearrange("e (t p) h -> p e t h", p=P), w2[:]),
                    (d["L0_ffn_b1"].rearrange("e (t p) -> p e t", p=P), b1[:])])
                n_small = start_loads(nc, small_loaded, columns=[
                    (d["L1_xattn_ln_x_g"], ctx_gain[:]), (d["L1_xattn_ln_x_b"], ctx_shift[:]),
                    (d["L1_xattn_ln_l_g"], lat_gain[:]), (d["L1_xattn_ln_l_b"], lat_shift[:]),
                    (d["L1_xattn_k_gamma"], gk[0:D1, :]), (d["L1_xattn_k_gamma"], gk[D1:, :]),
                    (d["L1_xattn_q_gamma"], gq[0:D1, :]), (d["L1_xattn_q_gamma"], gq[D1:, :])],
                    rows=[(d["L1_xattn_b_out"], bout[:])],
                    others=[(d["L1_xattn_W_q"], wq[:]), (d["L1_xattn_W_kv"], wkv[:]), (d["L1_xattn_W_out"], wout[:]),
                            (d["L1_ffn_gate_w"], gate[:]), (d["L1_ffn_shared_gate_w"], shared_gu[:, 0:I1]),
                            (d["L1_ffn_shared_up_w"], shared_gu[:, I1:]),
                            (d["L1_ffn_shared_down_w"].rearrange("(t p) h -> p t h", p=P), shared_d[:])])
            layer_norm(nc, "ln1", x_sb, xln, NT, xlnT, ident)
            await_loads(nc, router_loaded, n_router)
            l0_router(nc, x_sb, xlnT, ident, rw, rb, b2, weight)
            await_loads(nc, experts_loaded, n_experts)
            l0_experts(nc, x_sb, xlnT, w1, b1, w2, weight)

        large = Alloc(nc, whole)
        wgu = large.sb("wgu", [P, E1, 2 * I1])
        zeros = large.sb("zeros", [P, 8, E])
        wgu_loaded, wd_loaded, cleared = (large.sem(n) for n in ("wgu_loaded", "wd_loaded", "cleared"))
        n_cleared = start_clearing(nc, zeros, (sorted_x, sorted_y), cleared)
        n_wgu = start_loads(nc, wgu_loaded, others=[
            (d["L1_ffn_routed_gate_w"].rearrange("e h i -> h e i"), wgu[:, :, 0:I1]),
            (d["L1_ffn_routed_up_w"].rearrange("e h i -> h e i"), wgu[:, :, I1:])])
        with ExitStack() as st:
            a = Alloc(nc, st)
            qT, klT, vl = a.sb("qT1", [P, NT * P]), a.sb("klT", [P, NT * P]), a.sb("vl", [P, NT, E])
            await_loads(nc, small_loaded, n_small)
            scale_column(nc, gq[:], SCALE1)
            l1_flags(nc, d["mask_BxS2_bk0"], flag_scratch, flags)
            l1_project(nc, "c_", ident, ctx_gain, ctx_shift, wkv, gk,
                       context=(d["ctx_1024"], flags, kT_scratch, v_scratch))
            layer_norm(nc, "ln2", x_sb, xln, NT)
            l1_project(nc, "l_", ident, lat_gain, lat_shift, wkv, gk, latents=(xln, wq, gq, qT, klT, vl))
            l1_attention(nc, x_sb, ident, flags, d["mask_BxS2_bk0"], qT, klT, vl, kT_scratch, v_scratch, wout, bout)

        with ExitStack() as st:
            a = Alloc(nc, st)
            xlnT = a.sb("xlnT3", [P, NT * P])
            wd = a.sb("wd", [P, E1, 2, E])
            position = a.sb("position", [P, NT], U32)
            expert_of, n_tiles = a.sb("expert_of", [1, 2 * TP], I32), a.sb("n_tiles", [1, 1], I32)
            n_wd = start_loads(nc, wd_loaded, others=[
                (d["L1_ffn_routed_down_w"].rearrange("e (t p) h -> p e t h", p=P), wd[:])])
            layer_norm(nc, "ln3", x_sb, xln, NT, xlnT, ident)
            l1_route(nc, xln, xlnT, gate, position, expert_of, n_tiles)
            l1_shared(nc, x_sb, xlnT, shared_gu, shared_d, xln, position, sorted_x, cleared, n_cleared)
            await_loads(nc, wgu_loaded, n_wgu)
            await_loads(nc, wd_loaded, n_wd)
            l1_routed(nc, ident, sorted_x, sorted_y, wgu, wd, expert_of, n_tiles)
            l1_gather(nc, x_sb, xln, position, sorted_y, out)


def kernel(**inputs):
    import numpy as _np
    import concourse.bacc as _bacc
    from concourse import mybir as _mybir
    from concourse.bass_utils import run_bass_kernel_spmd as _run

    nc = _bacc.Bacc("TRN2", target_bir_lowering=False, num_devices=1)
    arrays, tensors = {}, {}
    for name in _IN:
        a = _np.ascontiguousarray(inputs[name])
        arrays["in_" + name] = a
        tensors[name] = nc.dram_tensor("in_" + name, a.shape, _mybir.dt.from_np(a.dtype), kind="ExternalInput").ap()
    out = nc.dram_tensor("out_x", (B, S, E), F32, kind="ExternalOutput").ap()
    build_program(nc, tensors, out)
    result = _run(nc, [arrays], core_ids=[0])
    return result.results[0]["out_x"]
```

```python
from contextlib import ExitStack

import concourse.bass as bass
from concourse import mybir

F32 = mybir.dt.float32
BF16 = mybir.dt.bfloat16
I32 = mybir.dt.int32
U32 = mybir.dt.uint32
U8 = mybir.dt.uint8
ALU = mybir.AluOpType
ACT = mybir.ActivationFunctionType
AX = mybir.AxisListType.X

P = 128
B, S, E = 16, 256, 128
QT = S // P
NT = B * QT
KEYS = 1601
W = 512
NW = -(-KEYS // W)
KT = W // P
START = [max(KEYS - W * (NW - w), 0) for w in range(NW)]
FIRST_OWN = KEYS - W * (NW - 1)
MASKED = -float(2.0 ** 100)
DOUBLED = -float(2.0 ** 101)
NO_MAX = -float(2.0 ** 102)
EPS = 1e-5
ONE = 1


class Alloc:

    def __init__(self, nc, stack):
        self.nc, self.stack, self.sems = nc, stack, []
        stack.callback(self.clear)

    def start_at_one(self):
        for sem in self.sems:
            self.nc.gpsimd.sem_inc(sem, ONE)
        self.nc.all_engine_barrier()

    def clear(self):
        if self.sems:
            self.nc.clear_and_free_semaphores(self.sems)
            self.nc.all_engine_barrier()

    def sb(self, name, shape, dt=F32):
        return self.stack.enter_context(self.nc.sbuf_tensor(name, shape, dt))

    def ps(self, name, shape, dt=F32):
        return self.stack.enter_context(self.nc.psum_tensor(name, shape, dt))

    def sem(self, name):
        self.sems.append(self.nc.alloc_semaphore(name))
        return self.sems[-1]


class Awaited:

    def __init__(self, eng, sem, name, step=1):
        self.eng, self.sem, self.step = eng, sem, step
        self.value = eng.alloc_register(name)
        eng.reg_mov(self.value, ONE + step)

    def at(self):
        return self.eng.snap(self.value)

    def wait(self, at=None):
        self.eng.wait_ge(self.sem, self.at() if at is None else at)
        self.eng.reg_add(self.value, self.value, self.step)


class Steps:

    def __init__(self, eng, sem, base=0):
        self.eng, self.sem, self.base, self.n = eng, sem, base, 0

    def mark(self, ins):
        self.n += 1
        ins.then_inc(self.sem, 1)

    def settle(self):
        self.eng.wait_ge(self.sem, self.base + self.n)


def load_tokens(nc, x, x_sb, ident):
    with ExitStack() as st:
        a = Alloc(nc, st)
        loaded, zeroed, made = a.sem("x_loaded"), a.sem("ident_zeroed"), a.sem("ident_made")
        block = st.enter_context(nc.Block())

        @block.sync
        def _(sp):
            sp.dma_start(x_sb[:], x.rearrange("b (t p) e -> p (b t) e", p=P)).then_inc(loaded, 16)
            sp.wait_ge(loaded, 16)

        @block.gpsimd
        def _(pool):
            pool.memset(ident[:], 0.0).then_inc(zeroed, 1)
            pool.wait_ge(zeroed, 1)
            pool.affine_select(out=ident[:], in_=ident[:], compare_op=ALU.not_equal, fill=1.0, base=0,
                               pattern=[[-1, P]], channel_multiplier=1).then_inc(made, 1)
            pool.wait_ge(made, 1)


def layer_norm(nc, tag, src, dst, tiles, transposed=None, ident=None, affine=None):
    STEP = 8
    with ExitStack() as st:
        a = Alloc(nc, st)
        stats = a.sb(tag + "_stats", [P, tiles, 6])
        mv = a.sb(tag + "_mv", [P, tiles, 2])
        var = a.sb(tag + "_var", [P, tiles])
        rstd = a.sb(tag + "_rstd", [P, tiles])
        shift = a.sb(tag + "_shift", [P, tiles])
        expo = a.sb(tag + "_expo", [P, tiles])
        counted, merged, var_ready, root_ready = (a.sem(tag + n) for n in ("_counted", "_merged", "_varr", "_root"))
        expo_set = a.sem(tag + "_expo_set")
        scaled, normed, turned, moved = (a.sem(tag + n) for n in ("_scaled", "_normed", "_turned", "_moved"))
        if transposed is not None:
            pt = [a.ps(f"{tag}_pt{i}", [P, 4, P]) for i in range(2)]
        block = st.enter_context(nc.Block())

        @block.vector
        def _(dve):
            with dve.Fori(0, tiles // STEP) as g:
                for t in (g * STEP + i for i in range(STEP)):
                    dve.bn_stats(stats[:, bass.ds(t, 1), :].rearrange("p o s -> p (o s)"),
                                 src[:, bass.ds(t, 1), :].rearrange("p o e -> p (o e)")).then_inc(counted, 1)
            dve.wait_ge(counted, tiles)
            for t in range(tiles):
                dve.bn_aggr(mv[:, t, :], stats[:, t, :]).then_inc(merged, 1)
            dve.wait_ge(merged, tiles)
            dve.tensor_scalar(var[:], mv[:, :, 1], EPS, None, ALU.add).then_inc(var_ready, 1)
            dve.wait_ge(root_ready, 1)
            dve.scalar_tensor_tensor(shift[:], mv[:, :, 0], -1.0, rstd[:], ALU.mult, ALU.mult).then_inc(scaled, 1)
            dve.wait_ge(scaled, 1)
            with dve.Fori(0, tiles // STEP) as g:
                for t in (g * STEP + i for i in range(STEP)):
                    dve.tensor_scalar(dst[:, bass.ds(t, 1), :].rearrange("p o e -> p (o e)"),
                                      src[:, bass.ds(t, 1), :].rearrange("p o e -> p (o e)"),
                                      rstd[:, bass.ds(t, 1)], shift[:, bass.ds(t, 1)],
                                      ALU.mult, ALU.add).then_inc(normed, 1)
            dve.wait_ge(normed, tiles)

        @block.gpsimd
        def _(pool):
            pool.memset(expo[:], -0.5).then_inc(expo_set, 1)
            pool.wait_ge(expo_set, 1)
            pool.wait_ge(var_ready, 1)
            pool.tensor_tensor(rstd[:], var[:], expo[:], ALU.pow).then_inc(root_ready, 1)

        @block.scalar
        def _(act):
            if transposed is None:
                return
            for g in range(tiles // 4):
                act.wait_ge(turned, g + 1)
                out = transposed[:, g * 4 * P:(g + 1) * 4 * P]
                src_ps = pt[g % 2][:].rearrange("p t q -> p (t q)")
                if affine is None:
                    act.activation(out, src_ps, ACT.Copy).then_inc(moved, 1)
                else:
                    act.activation(out, src_ps, ACT.Identity, bias=affine[1], scale=affine[0]).then_inc(moved, 1)
            act.wait_ge(moved, tiles // 4)

        if transposed is not None:
            @block.tensor
            def _(pe):
                for g in range(tiles // 4):
                    pe.wait_ge(normed, 4 * (g + 1))
                    if g >= 2:
                        pe.wait_ge(moved, g - 1)
                    for t in range(4):
                        mm = pe.transpose(pt[g % 2][:, t, :], dst[:, 4 * g + t, :], ident[:])
                    mm.then_inc(turned, 1)


def start_loads(nc, loaded, columns=(), rows=(), others=()):
    with ExitStack() as st:
        block = st.enter_context(nc.Block())

        @block.sync
        def _(sp):
            for src, dst in columns:
                sp.dma_start(dst, src.rearrange("(p o) -> p o", o=1)).then_inc(loaded, 16)
            for src, dst in rows:
                sp.dma_start(dst, src.partition_broadcast(P)).then_inc(loaded, 16)
            for src, dst in others:
                sp.dma_start(dst, src).then_inc(loaded, 16)
    return len(columns) + len(rows) + len(others)


def await_loads(nc, loaded, count):
    with ExitStack() as st:
        block = st.enter_context(nc.Block())

        @block.sync
        def _(sp):
            sp.wait_ge(loaded, 16 * count)


def turn_weights(nc, tag, loads, ident, columns=(), rows=(), others=()):
    with ExitStack() as st:
        a = Alloc(nc, st)
        n = len(loads)
        raw = a.sb(tag + "_raw", [P, max(n, 1), P])
        pt = a.ps(tag + "_pt", [P, 4, P])
        loaded, turned, moved = a.sem(tag + "_loaded"), a.sem(tag + "_turned"), a.sem(tag + "_moved")
        block = st.enter_context(nc.Block())
        total = n + len(columns) + len(rows) + len(others)

        @block.sync
        def _(sp):
            for i, (src, _) in enumerate(loads):
                sp.dma_start(raw[:, i, :], src).then_inc(loaded, 16)
            for src, dst in columns:
                sp.dma_start(dst, src.rearrange("(p o) -> p o", o=1)).then_inc(loaded, 16)
            for src, dst in rows:
                sp.dma_start(dst, src.partition_broadcast(P)).then_inc(loaded, 16)
            for src, dst in others:
                sp.dma_start(dst, src).then_inc(loaded, 16)
            sp.wait_ge(loaded, 16 * total)

        if not n:
            return

        @block.tensor
        def _(pe):
            pe.wait_ge(loaded, 16 * total)
            for i in range(n):
                mm = pe.transpose(pt[:, i, :], raw[:, i, :], ident[:])
            mm.then_inc(turned, 1)

        @block.vector
        def _(dve):
            dve.wait_ge(turned, 1)
            for i, (_, dst) in enumerate(loads):
                dve.tensor_copy(dst, pt[:, i, :]).then_inc(moved, 1)
            dve.wait_ge(moved, n)


def l0_mask(nc, mask, mneg, flags, ident):
    with ExitStack() as st:
        a = Alloc(nc, st)
        raw = a.sb("m_raw", [P, QT, KEYS], I32)
        best = a.sb("m_best", [P, QT, NW])
        some = a.sb("m_some", [P, QT])
        need = a.sb("m_need", [P, QT, NW])
        row = a.sb("m_row", [QT * NW, 1])
        turned_sb = a.sb("m_turned_sb", [QT * NW, P])
        line = a.sb("m_line", [1, QT * NW])
        merged = a.sb("m_merged", [1, NW])
        firsts = a.sb("m_firsts", [1, NW])
        pt = a.ps("m_pt", [P, P])
        loaded, steps, turned, topped, line_ps = (a.sem(n) for n in ("m_loaded", "m_steps", "m_turn", "m_top", "m_line_ps"))
        block = st.enter_context(nc.Block())

        @block.sync
        def _(sp):
            sp.dma_start(raw[:], mask.rearrange("(t p) k -> p t k", p=P)).then_inc(loaded, 16)
            sp.wait_ge(loaded, 16)

        @block.vector
        def _(dve):
            s = Steps(dve, steps)
            s.mark(dve.memset(mneg[:, :, 0, FIRST_OWN:], DOUBLED))
            dve.wait_ge(loaded, 16)
            for w in range(NW):
                own = FIRST_OWN if w == 0 else W
                s.mark(dve.tensor_scalar(mneg[:, :, w, 0:own], raw[:, :, START[w]:START[w] + own], 0.0, MASKED,
                                         ALU.is_equal, ALU.mult))
            s.settle()
            s.mark(dve.tensor_reduce(best[:], mneg[:], AX, ALU.max))
            s.settle()
            s.mark(dve.tensor_reduce(some[:], best[:], AX, ALU.max))
            s.settle()
            s.mark(dve.tensor_scalar(some[:], some[:], 0.0, None, ALU.is_lt))
            s.mark(dve.tensor_scalar(best[:], best[:], 0.0, None, ALU.is_equal))
            s.settle()
            for t in range(QT):
                s.mark(dve.tensor_scalar(need[:, t, :], best[:, t, :], some[:, t:t + 1], None, ALU.max))
            s.settle()
            dve.engine_nop().then_inc(topped, 1)
            dve.wait_ge(turned, 1)
            s.mark(dve.tensor_reduce(row[:], pt[0:QT * NW, :], AX, ALU.max))
            s.settle()
            dve.engine_nop().then_inc(topped, 1)
            dve.wait_ge(line_ps, 1)
            s.mark(dve.tensor_copy(line[:], pt[0:1, 0:QT * NW]))
            s.settle()
            s.mark(dve.tensor_tensor(merged[:], line[:, 0:NW], line[:, NW:2 * NW], ALU.max))
            s.settle()
            s.mark(dve.tensor_copy(flags[:, 0:NW], merged[:]))
            s.mark(dve.tensor_copy(firsts[:], merged[:]))
            s.settle()
            for w in range(1, NW):
                s.mark(dve.tensor_tensor(firsts[:, w:w + 1], merged[:, w:w + 1], merged[:, w - 1:w], ALU.is_gt))
                s.mark(dve.tensor_tensor(merged[:, w:w + 1], merged[:, w:w + 1], merged[:, w - 1:w], ALU.max))
                s.settle()
            s.mark(dve.tensor_copy(flags[:, NW:2 * NW], firsts[:]))
            s.settle()

        @block.tensor
        def _(pe):
            pe.wait_ge(topped, 1)
            pe.transpose(pt[0:QT * NW, :], need[:].rearrange("p t w -> p (t w)"), ident[:]).then_inc(turned, 1)
            pe.wait_ge(topped, 2)
            pe.transpose(pt[0:1, 0:QT * NW], row[:], ident[0:QT * NW, 0:QT * NW]).then_inc(line_ps, 1)


H0, D0 = 16, 8
LEAD = 3
AHEAD = 2
EARLY = (3, 4, 6, 7, 8, 8, 8, 8)
QUADS = H0 // 4
HQ = 4 * QT
SCALE0 = float(D0) ** -0.5
SLOTS0 = [(q, k) for k in range(3) for q in range(3) if q + k < 4]
HP = H0 // 2


def l0_attention(nc, x_sb, xlnT, mneg, flags, ident, ctx, w, q_parts, k_parts):
    wqT, wkT, wvT, wpT, bq, bk, bv, bp = w
    ctx_rows = ctx.rearrange("b k e -> (b k) e")
    with ExitStack() as st:
        a = Alloc(nc, st)
        whole = a.sb("whole", [P, 2, W])
        rest = a.sb("rest", [P, W])
        parts = a.sb("parts", [P, 2, 3, W], BF16)
        q_st = a.sb("q_st", [P, 2, HP, 2, S], BF16)
        k_st = a.sb("k_st", [P, HP, W], BF16)
        ctx_sb = a.sb("ctx_sb", [P, KT, E])
        ctxT = a.sb("ctxT", [P, W])
        v = a.sb("v", [P, KT, E])
        scores = a.sb("scores", [P, 2, HQ, W])
        probsT = a.sb("probsT", [P, 2, KT, 4, S])
        oT = a.sb("oT", [P, QUADS, S])
        m_old = a.sb("m_old", [P, H0 * QT])
        m_win = a.sb("m_win", [P, H0 * QT])
        m_new = a.sb("m_new", [P, H0 * QT])
        m_diff = a.sb("m_diff", [P, H0 * QT])
        alpha = a.sb("alpha", [P, H0 * QT])
        neg_m = a.sb("neg_m", [P, H0 * QT])
        l_win = a.sb("l_win", [P, H0 * QT])
        l_sum = a.sb("l_sum", [P, H0 * QT])
        acc = a.sb("acc", [P, QT, H0, D0])
        heads = a.sb("heads", [P, QT, E])
        headsT = a.sb("headsT", [P, S])
        ps_s = [a.ps(f"ps_s{i}", [P, W]) for i in range(2)]
        ps_t = [a.ps(f"ps_t{i}", [P, KT * P]) for i in range(2)]
        ps_o = a.ps("ps_o", [P, QUADS, S])
        ps_m = [a.ps(f"ps_m{i}", [P, 512]) for i in range(2)]

        sem = {n: a.sem("a0_" + n) for n in (
            "q_st_zeroed q_ps q_sb q_split q_stored0 q_stored1 q_stacked0 q_stacked1 k_split k_stored k_stacked ctx_loaded ctxT_ps ctxT_sb kv_ps k_sb v_sb s_ps s_sb "
            "neg_m_ready p_sb t_ps t_act t_dve o_ps o_sb oT_ps acc_done alpha_ready heads_ready headsT_ps headsT_sb "
            "y_ps x_done dve_steps state_ready").split()}
        a.start_at_one()
        block = st.enter_context(nc.Block())

        def windows(eng):
            live, first = ([eng.value_load(flags[0:1, i:i + 1], min_val=0, max_val=1) for i in part]
                           for part in (range(NW), range(NW, 2 * NW)))
            n = eng.alloc_register("n_windows")
            eng.reg_mov(n, 0)
            return live, first, n

        def split(dve, s, src, to):
            s.mark(dve.tensor_copy(to[:, 0, :], src))
            s.settle()
            s.mark(dve.tensor_tensor(rest[:], src, to[:, 0, :], ALU.subtract))
            s.settle()
            s.mark(dve.tensor_copy(to[:, 1, :], rest[:]))
            s.settle()
            return dve.tensor_tensor(to[:, 2, :], rest[:], to[:, 1, :], ALU.subtract)

        def stack(sp, which, source, target, seen):
            for c in range(2):
                for slot, pick in enumerate(SLOTS0):
                    at = (c * len(SLOTS0) + slot) * D0
                    sp.dma_start(target(c)[at:at + D0], source(pick[which]).rearrange(
                        "(p c d) k -> c d p k", c=2, d=D0)[c]).then_inc(seen, 16)
        STACK = 2 * len(SLOTS0) * 16

        @block.sync
        def _(sp):
            for g in range(NT * P // W):
                sp.wait_ge(sem["q_split"], ONE + g + 1)
                sp.dma_start(q_parts[:, :, g * W:(g + 1) * W].rearrange("c p k -> p c k"),
                             parts[:, g % 2, :, :]).then_inc(sem[f"q_stored{g % 2}"], 16)
            for half in range(2):
                sp.wait_ge(sem[f"q_stored{half}"], ONE + NT * P // W // 2 * 16)
            sp.wait_ge(sem["q_st_zeroed"], ONE + 1)
            live, first, n = windows(sp)

            def batch(b, half):
                for wi in range(NW):
                    with sp.If(live[wi] != 0):
                        done = sp.snap(n)
                        at = sp.snap(b * KEYS + START[wi])
                        sp.wait_ge(sem["ctxT_ps"], ONE + done)
                        sp.dma_start(ctx_sb[:], ctx_rows[bass.ds(at, W), :].rearrange(
                            "(t p) e -> p t e", p=P)).then_inc(sem["ctx_loaded"], 16)
                        with sp.If(first[wi] != 0):
                            stack(sp, 0, lambda part: q_parts[part, :, bass.ds(b * S, S)],
                                  lambda c: q_st[:, half, :, c, :], sem[f"q_stacked{half}"])
                        sp.wait_ge(sem["k_split"], ONE + done + 1)
                        sp.dma_start(k_parts.rearrange("c p k -> p c k"), parts[:, 0, :, :]).then_inc(
                            sem["k_stored"], 16)
                        sp.wait_ge(sem["s_ps"], ONE + done * HQ * QUADS)
                        sp.wait_ge(sem["k_stored"], ONE + (done + 1) * 16)
                        stack(sp, 1, lambda part: k_parts[part], lambda c: k_st[:], sem["k_stacked"])
                        sp.reg_add(n, n, 1)

            with sp.Fori(0, B // 2) as i:
                batch(i * 2, 0)
                batch(i * 2 + 1, 1)
            sp.wait_ge(sem["ctxT_ps"], ONE + sp.snap(n))
            sp.dma_start(ctx_sb[:], ctx_rows[START[-1]:START[-1] + W, :].rearrange(
                "(t p) e -> p t e", p=P)).then_inc(sem["ctx_loaded"], 16)

        @block.gpsimd
        def _(pool):
            pool.memset(q_st[:], 0.0).then_inc(sem["q_st_zeroed"], 1)

        @block.tensor
        def _(pe):
            for g in range(NT * P // 512):
                if g >= 2:
                    pe.wait_ge(sem["q_sb"], ONE + g - 1)
                pe.matmul(ps_m[g % 2][:], wqT[:], xlnT[:, g * 512:(g + 1) * 512], start=True,
                          stop=True).then_inc(sem["q_ps"], 1)
            live, first, n = windows(pe)
            pe.wait_ge(sem["q_sb"], ONE + NT * P // 512)
            pe.wait_ge(sem["state_ready"], ONE + 1)

            def one_score(u, quad, half, j):
                h, t = 4 * quad + j // QT, j % QT
                if not (quad == 0 and j < 2):
                    pe.wait_ge(sem["s_sb"], ONE + u * HQ + j - 1)
                pe.matmul(ps_s[j % 2][:], q_st[:, half, h // 2, h % 2, t * P:(t + 1) * P], k_st[:, h // 2, :],
                          start=True, stop=True).then_inc(sem["s_ps"], 1)

            def one_turn(u, quad, j):
                pe.wait_ge(sem["p_sb"], ONE + u * HQ + j + 1)
                if j % 2 == 0:
                    pe.wait_ge(sem["t_act"], ONE + u * HQ // 2 + j // 2)
                else:
                    pe.wait_ge(sem["t_dve"], ONE + u * HQ // 2 + j // 2)
                for k in range(KT):
                    mm = pe.transpose(ps_t[j % 2][:, k * P:(k + 1) * P], scores[:, quad % 2, j, k * P:(k + 1) * P], ident[:])
                mm.then_inc(sem["t_ps"], 1)

            def values(u, quad, tiles):
                if tiles[0] == 0:
                    pe.wait_ge(sem["t_act"], ONE + (u + 1) * HQ // 2)
                    pe.wait_ge(sem["t_dve"], ONE + (u + 1) * HQ // 2)
                for k in tiles:
                    for i in range(4):
                        h = 4 * quad + i
                        mm = pe.matmul(ps_o[32 * i:32 * i + D0, quad, :], v[:, k, D0 * h:D0 * (h + 1)],
                                       probsT[:, quad % 2, k, i, :], start=(k == 0), stop=(k == KT - 1),
                                       tile_position=(0, 32 * i))
                if tiles[-1] == KT - 1:
                    mm.then_inc(sem["o_ps"], 1)

            def merge_heads(done):
                pe.wait_ge(sem["o_sb"], ONE + done + 1)
                for t in range(QT):
                    for quad in range(QUADS):
                        mm = pe.transpose(ps_t[t][:, quad * P:(quad + 1) * P], oT[:, quad, t * P:(t + 1) * P], ident[:])
                    mm.then_inc(sem["oT_ps"], 1)

            def turn_heads(b):
                pe.wait_ge(sem["heads_ready"], ONE + b)
                for t in range(QT):
                    mm = pe.transpose(ps_m[0][:, t * P:(t + 1) * P], heads[:, t, :], ident[:])
                mm.then_inc(sem["headsT_ps"], 1)

            def project_heads(b):
                pe.wait_ge(sem["headsT_sb"], ONE + b)
                for t in range(QT):
                    mm = pe.matmul(ps_m[0][:, S + t * P:S + (t + 1) * P], headsT[:, t * P:(t + 1) * P], wpT[:], start=True,
                                   stop=True)
                mm.then_inc(sem["y_ps"], 1)

            def turn_context(win):
                pe.wait_ge(sem["ctx_loaded"], ONE + (win + 1) * 16)
                for k in range(KT):
                    mm = pe.transpose(ps_m[1][:, k * P:(k + 1) * P], ctx_sb[:, k, :], ident[:])
                mm.then_inc(sem["ctxT_ps"], 1)

            def project_keys(win):
                pe.wait_ge(sem["ctxT_sb"], ONE + win + 1)
                pe.matmul(ps_m[1][:], wkT[:], ctxT[:], start=True, stop=True).then_inc(sem["kv_ps"], 1)

            def project_values():
                for k in range(KT):
                    mm = pe.matmul(ps_m[0][:, k * P:(k + 1) * P], ctxT[:, k * P:(k + 1) * P], wvT[:], start=True,
                                   stop=True)
                mm.then_inc(sem["kv_ps"], 1)

            def window(done, half, b, finish):
                pe.wait_ge(sem["k_stacked"], ONE + (done + 1) * STACK)
                pe.wait_ge(sem["s_sb"], ONE + done * HQ * QUADS)
                for j in range(HQ):
                    one_score(done * QUADS, 0, half, j)
                    if j == 1:
                        project_values()
                        merge_heads(done)
                for ahead in range(AHEAD):
                    one_score(done * QUADS + 1, 1, half, ahead)
                pe.wait_ge(sem["v_sb"], ONE + done + 1)
                pe.wait_ge(sem["acc_done"], ONE + done + 1)
                for quad in range(QUADS):
                    u = done * QUADS + quad
                    for j in range(HQ):
                        if quad and j == 0:
                            values(u - 1, quad - 1, range(KT // 2))
                        if quad + 1 < QUADS:
                            for ahead in range(EARLY[j - 1] if j else AHEAD, EARLY[j]):
                                one_score(u + 1, quad + 1, half, ahead)
                        one_turn(u, quad, j)
                        if quad and j == 1:
                            values(u - 1, quad - 1, range(KT // 2, KT))
                        if quad == 1 and j == 1:
                            with pe.If(finish != 0):
                                turn_heads(b)
                            pe.wait_ge(sem["k_sb"], ONE + done + 1)
                            turn_context(done + 1)
                        if quad == 1 and j == HQ // 2 + 1:
                            project_keys(done + 1)
                        if quad == 2 and j == 1:
                            with pe.If(finish != 0):
                                project_heads(b)
                    if quad + 2 < QUADS:
                        for ahead in range(AHEAD):
                            one_score(u + 2, quad + 2, half, ahead)
                values(done * QUADS + QUADS - 1, QUADS - 1, range(KT))
                pe.wait_ge(sem["x_done"], ONE + b)

            def batch(b, half):
                pe.wait_ge(sem[f"q_stacked{half}"], ONE + (b - half) * (STACK // 2) + STACK)
                for wi in range(NW):
                    with pe.If(live[wi] != 0):
                        window(pe.snap(n), half, b, pe.snap(first[wi] * b))
                        pe.reg_add(n, n, 1)

            turn_context(0)
            project_keys(0)
            with pe.Fori(0, B // 2) as i:
                batch(i * 2, 0)
                batch(i * 2 + 1, 1)
            merge_heads(pe.snap(n))
            turn_heads(B)
            project_heads(B)

        @block.scalar
        def _(act):
            for g in range(NT * P // 512):
                act.wait_ge(sem["q_ps"], ONE + g + 1)
                if g >= 2:
                    act.wait_ge(sem["q_split"], ONE + g - 1)
                act.activation(whole[:, g % 2, :], ps_m[g % 2][:], ACT.Identity, bias=bq[:]).then_inc(sem["q_sb"], 1)
            act.wait_ge(sem["q_split"], ONE + NT * P // 512)
            live, first, n = windows(act)

            act.wait_ge(sem["state_ready"], ONE + 1)

            def merge_heads(done):
                act.wait_ge(sem["o_ps"], ONE + done * QUADS)
                act.wait_ge(sem["oT_ps"], ONE + done * QT)
                act.activation(oT[:], ps_o[:], ACT.Copy).then_inc(sem["o_sb"], 1)

            def turn_heads(b):
                act.wait_ge(sem["headsT_ps"], ONE + b)
                act.wait_ge(sem["y_ps"], ONE + b - 1)
                act.activation(headsT[:], ps_m[0][:, 0:S], ACT.Copy).then_inc(sem["headsT_sb"], 1)

            def move_context(win):
                act.wait_ge(sem["ctxT_ps"], ONE + win + 1)
                act.wait_ge(sem["kv_ps"], ONE + win * 2)
                act.activation(ctxT[:], ps_m[1][:], ACT.Copy).then_inc(sem["ctxT_sb"], 1)

            def move_keys(win):
                act.wait_ge(sem["kv_ps"], ONE + win * 2 + 1)
                act.wait_ge(sem["k_split"], ONE + win)
                act.activation(whole[:, 0, :], ps_m[1][:], ACT.Identity, bias=bk[:]).then_inc(sem["k_sb"], 1)

            def window(done, b, finish):
                merge_heads(done)
                for quad in range(QUADS):
                    u = done * QUADS + quad
                    act.wait_ge(sem["neg_m_ready"], ONE + u + 1)
                    c = quad * HQ
                    if quad == 0:
                        act.wait_ge(sem["acc_done"], ONE + done + 1)
                    act.activation(alpha[:, c:c + HQ], m_diff[:, c:c + HQ], ACT.Exp,
                                   scale=SCALE0).then_inc(sem["alpha_ready"], 1)

                    def move(j):
                        act.wait_ge(sem["t_ps"], ONE + u * HQ + j + 1)
                        i, t = j // QT, j % QT
                        if j == 0:
                            if quad >= 2:
                                act.wait_ge(sem["o_ps"], ONE + u - 1)
                            else:
                                act.wait_ge(sem["o_ps"], ONE + done * QUADS)
                        act.activation(probsT[:, quad % 2, :, i, t * P:(t + 1) * P],
                                       ps_t[0][:].rearrange("p (k q) -> p k q", k=KT),
                                       ACT.Copy).then_inc(sem["t_act"], 1)

                    for j in range(HQ):
                        act.activation(scores[:, quad % 2, j, :], scores[:, quad % 2, j, :], ACT.Exp,
                                       bias=neg_m[:, c + j:c + j + 1], scale=SCALE0,
                                       accum_out=l_win[:, c + j:c + j + 1]).then_inc(sem["p_sb"], 1)
                        if j % 2 == 1 and j >= LEAD:
                            move(j - LEAD)
                            if j == HQ - 1:
                                for left in range(HQ + 1 - LEAD, HQ, 2):
                                    move(left)
                        if quad == 1 and j == 3:
                            move_context(done + 1)
                        if quad == 2 and j == 1:
                            move_keys(done + 1)
                        if quad == 1 and j == HQ // 2:
                            with act.If(finish != 0):
                                turn_heads(b)

            move_context(0)
            move_keys(0)
            with act.Fori(0, B) as b:
                for wi in range(NW):
                    with act.If(live[wi] != 0):
                        window(act.snap(n), b, act.snap(first[wi] * b))
                        act.reg_add(n, n, 1)
            merge_heads(act.snap(n))
            turn_heads(B)

        @block.vector
        def _(dve):
            dve.memset(ps_o[:], 0.0).then_inc(sem["state_ready"], 1)
            s0 = Steps(dve, sem["dve_steps"], ONE)
            for state in (alpha, l_win, l_sum, acc):
                s0.mark(dve.memset(state[:], 0.0))
            s0.mark(dve.memset(m_old[:], NO_MAX))
            s0.settle()
            for g in range(NT * P // 512):
                dve.wait_ge(sem["q_sb"], ONE + g + 1)
                if g >= 2:
                    dve.wait_ge(sem[f"q_stored{g % 2}"], ONE + g // 2 * 16)
                split(dve, s0, whole[:, g % 2, :], parts[:, g % 2, :, :]).then_inc(sem["q_split"], 1)
            for half in range(2):
                dve.wait_ge(sem[f"q_stored{half}"], ONE + NT * P // 512 // 2 * 16)
            live, first, n = windows(dve)
            steps = dve.alloc_register("n_steps")
            dve.reg_mov(steps, ONE + s0.n)
            scores_in = Awaited(dve, sem["s_ps"], "a0_s_ps_at")

            def rescale(done, s):
                dve.wait_ge(sem["alpha_ready"], ONE + done * QUADS)
                dve.wait_ge(sem["p_sb"], ONE + done * QUADS * HQ)
                s.mark(dve.tensor_tensor(l_sum[:], l_sum[:], alpha[:], ALU.mult))
                for t in range(QT):
                    by_head = alpha[:].rearrange("p (h t) -> p h t", t=QT)[:, :, t:t + 1].broadcast_to([P, H0, D0])
                    s.mark(dve.tensor_tensor(acc[:, t, :, :], acc[:, t, :, :], by_head, ALU.mult))
                s.settle()
                s.mark(dve.tensor_tensor(l_sum[:], l_sum[:], l_win[:], ALU.add))

            def merge_heads(done, s):
                for t in range(QT):
                    dve.wait_ge(sem["oT_ps"], ONE + done * QT + t + 1)
                    got = ps_t[t][:].rearrange("p (h d) -> p h d", d=32)[:, :, 0:D0]
                    ins = dve.tensor_tensor(acc[:, t, :, :], acc[:, t, :, :], got, ALU.add)
                    if t + 1 < QT:
                        s.mark(ins)
                ins.then_inc(sem["acc_done"], 1)
                s.settle()
                dve.wait_ge(sem["acc_done"], ONE + done + 1)
                dve.reg_add(steps, steps, s.n)

            def give_heads(b):
                s = Steps(dve, sem["dve_steps"], dve.snap(steps))
                s.mark(dve.reciprocal(l_sum[:], l_sum[:]))
                s.settle()
                dve.wait_ge(sem["headsT_ps"], ONE + b - 1)
                for t in range(QT):
                    by_head = l_sum[:].rearrange("p (h t) -> p h t", t=QT)[:, :, t:t + 1].broadcast_to([P, H0, D0])
                    ins = dve.tensor_tensor(heads[:, t, :].rearrange("p (h d) -> p h d", d=D0), acc[:, t, :, :],
                                            by_head, ALU.mult)
                    if t + 1 < QT:
                        s.mark(ins)
                ins.then_inc(sem["heads_ready"], 1)
                s.settle()
                dve.wait_ge(sem["heads_ready"], ONE + b)
                s.mark(dve.memset(m_old[:], NO_MAX))
                s.mark(dve.memset(l_sum[:], 0.0))
                s.mark(dve.memset(acc[:], 0.0))
                s.settle()
                dve.reg_add(steps, steps, s.n)

            def add_to_x(b):
                s = Steps(dve, sem["dve_steps"], dve.snap(steps))
                dve.wait_ge(sem["y_ps"], ONE + b)
                at = (b - 1) * QT if isinstance(b, int) else nc.s_assert_within(
                    (b - 1) * QT, 0, (B - 2) * QT, skip_runtime_bounds_check_because="only taken where b > 0")
                x_b = x_sb[:, bass.ds(at, QT), :]
                s.mark(dve.tensor_tensor(x_b, x_b, ps_m[0][:, S:2 * S].rearrange("p (t e) -> p t e", t=QT), ALU.add))
                s.settle()
                dve.tensor_tensor(x_b, x_b, bp[:].unsqueeze(1).broadcast_to([P, QT, E]),
                                  ALU.add).then_inc(sem["x_done"], 1)
                dve.reg_add(steps, steps, s.n)

            def split_keys(win, at):
                s = Steps(dve, sem["dve_steps"], at)
                dve.wait_ge(sem["k_sb"], ONE + win + 1)
                dve.wait_ge(sem["k_stored"], ONE + win * 16)
                split(dve, s, whole[:, 0, :], parts[:, 0, :, :]).then_inc(sem["k_split"], 1)
                dve.reg_add(steps, steps, s.n)

            def window(done, wi, b, finish):
                def move_values():
                    dve.wait_ge(sem["kv_ps"], ONE + done * 2 + 2)
                    dve.wait_ge(sem["o_ps"], ONE + done * QUADS)
                    dve.tensor_tensor(v[:], ps_m[0][:].rearrange("p (k e) -> p k e", k=KT),
                                      bv[:].unsqueeze(1).broadcast_to([P, KT, E]), ALU.add).then_inc(sem["v_sb"], 1)

                def reduce_one(u, quad, j):
                    at = scores_in.at()
                    if j == 0:
                        if quad >= 2:
                            dve.wait_ge(sem["t_ps"], ONE + (u - 1) * HQ)
                        else:
                            dve.wait_ge(sem["t_ps"], ONE + done * QUADS * HQ)
                    scores_in.wait(at)
                    c = quad * HQ + j
                    dve.tensor_tensor_reduce(scores[:, quad % 2, j, :], ps_s[j % 2][:], mneg[:, j % QT, wi, :], 1.0,
                                             NO_MAX, ALU.add, ALU.max,
                                             m_win[:, c:c + 1]).then_inc(sem["s_sb"], 1)

                def shift(u, quad):
                    s = Steps(dve, sem["dve_steps"], dve.snap(steps))
                    c = slice(quad * HQ, (quad + 1) * HQ)
                    dve.wait_ge(sem["s_sb"], ONE + (u + 1) * HQ)
                    s.mark(dve.tensor_tensor(m_new[:, c], m_old[:, c], m_win[:, c], ALU.max))
                    s.settle()
                    s.mark(dve.tensor_tensor(m_diff[:, c], m_old[:, c], m_new[:, c], ALU.subtract))
                    s.settle()
                    s.mark(dve.tensor_copy(m_old[:, c], m_new[:, c]))
                    dve.tensor_scalar(neg_m[:, c], m_new[:, c], -SCALE0, None, ALU.mult).then_inc(sem["neg_m_ready"], 1)
                    s.settle()
                    dve.reg_add(steps, steps, s.n)

                s = Steps(dve, sem["dve_steps"], dve.snap(steps))
                for j in range(HQ):
                    reduce_one(done * QUADS, 0, j)
                    if j == 0:
                        rescale(done, s)
                    if j == 1:
                        move_values()
                    if j == 2:
                        merge_heads(done, s)
                    if j == 3:
                        with dve.If(finish != 0):
                            give_heads(b)
                shift(done * QUADS, 0)
                for ahead in range(AHEAD):
                    reduce_one(done * QUADS + 1, 1, ahead)
                for quad in range(QUADS):
                    u = done * QUADS + quad
                    for j in range(HQ):
                        if quad + 1 < QUADS:
                            for ahead in range(EARLY[j - 1] if j else AHEAD, EARLY[j]):
                                reduce_one(u + 1, quad + 1, ahead)
                        if j % 2:
                            dve.wait_ge(sem["t_ps"], ONE + u * HQ + j + 1)
                            if j == 1:
                                if quad >= 2:
                                    dve.wait_ge(sem["o_ps"], ONE + u - 1)
                                else:
                                    dve.wait_ge(sem["o_ps"], ONE + done * QUADS)
                            i, t = j // QT, j % QT
                            dve.tensor_copy(probsT[:, quad % 2, :, i, t * P:(t + 1) * P],
                                            ps_t[1][:].rearrange("p (k q) -> p k q", k=KT)).then_inc(sem["t_dve"], 1)
                        if quad + 1 < QUADS and j == EARLY.index(HQ):
                            shift(u + 1, quad + 1)
                        if quad == 2 and j == 1:
                            split_keys(done + 1, dve.snap(steps))
                        if quad == 2 and j == HQ // 2 + 1:
                            with dve.If(finish != 0):
                                add_to_x(b)
                    if quad + 2 < QUADS:
                        for ahead in range(AHEAD):
                            reduce_one(u + 2, quad + 2, ahead)

            split_keys(0, dve.snap(steps))
            with dve.Fori(0, B) as b:
                for wi in range(NW):
                    with dve.If(live[wi] != 0):
                        window(dve.snap(n), wi, b, dve.snap(first[wi] * b))
                        dve.reg_add(n, n, 1)
            s1 = Steps(dve, sem["dve_steps"], dve.snap(steps))
            rescale(dve.snap(n), s1)
            merge_heads(dve.snap(n), s1)
            give_heads(B)
            add_to_x(B)
            dve.wait_ge(sem["x_done"], ONE + B)


E0, K0, I0 = 16, 4, 256
CH = 512
CT = CH // P


def l0_router(nc, x_sb, xlnT, ident, rw, rb, b2, weight):
    with ExitStack() as st:
        a = Alloc(nc, st)
        logits = a.sb("r_logits", [P, NT, E0])
        e = a.sb("r_e", [P, NT, E0])
        sel = a.sb("r_sel", [P, NT, E0])
        eq = [a.sb(f"r_eq{i}", [P, NT, E0]) for i in range(2)]
        top = a.sb("r_top", [P, NT, 8])
        need = a.sb("r_need", [P, NT])
        total = a.sb("r_total", [P, NT])
        wT = a.sb("r_wT", [E0, 4, P])
        ps_l = a.ps("r_ps_l", [P, NT, E0])
        ps_w = a.ps("r_ps_w", [P, 4, P])
        ps_b = a.ps("r_ps_b", [P, 4, P])
        s_logit, s_steps, s_centred, s_exp, s_weight, s_turn, s_moved, s_bias, s_added = (
            a.sem("r_s" + n) for n in "logit steps centred exp weight turn moved bias added".split())
        block = st.enter_context(nc.Block())
        per_tile = lambda t: t[:].unsqueeze(2).broadcast_to([P, NT, E0])

        @block.tensor
        def _(pe):
            for t in range(NT):
                mm = pe.matmul(ps_l[:, t, :], xlnT[:, t * P:(t + 1) * P], rw[:], start=True, stop=True)
            mm.then_inc(s_logit, 1)
            pe.wait_ge(s_weight, 1)
            for g in range(NT // 4):
                pe.wait_ge(s_moved, g)
                for i in range(4):
                    mm = pe.transpose(ps_w[0:E0, i, :], weight[:, 4 * g + i, :], ident[:])
                mm.then_inc(s_turn, 1)
                pe.wait_ge(s_moved, g + 1)
                pe.wait_ge(s_added, g)
                for i in range(4):
                    mm = pe.matmul(ps_b[:, i, :], wT[:, i, :], b2[:], start=True, stop=True)
                mm.then_inc(s_bias, 1)

        @block.scalar
        def _(act):
            act.wait_ge(s_centred, 1)
            act.activation(e[:], logits[:], ACT.Exp).then_inc(s_exp, 1)
            for g in range(NT // 4):
                act.wait_ge(s_turn, g + 1)
                act.wait_ge(s_bias, g)
                act.activation(wT[:], ps_w[0:E0, :, :], ACT.Copy).then_inc(s_moved, 1)

        @block.vector
        def _(dve):
            s = Steps(dve, s_steps)
            dve.wait_ge(s_logit, 1)
            s.mark(dve.tensor_tensor(logits[:], ps_l[:], rb[:].unsqueeze(1).broadcast_to([P, NT, E0]), ALU.add))
            s.settle()
            for t in range(NT):
                s.mark(dve.max(top[:, t, :], logits[:, t, :]))
            s.settle()
            kth = top[:, :, K0 - 1:K0].broadcast_to([P, NT, E0])
            s.mark(dve.tensor_tensor(sel[:], logits[:], kth, ALU.is_gt))
            s.mark(dve.tensor_tensor(eq[0][:], logits[:], kth, ALU.is_equal))
            s.mark(dve.tensor_tensor(logits[:], logits[:], top[:, :, 0:1].broadcast_to([P, NT, E0]), ALU.subtract))
            s.settle()
            dve.engine_nop().then_inc(s_centred, 1)
            s.mark(dve.tensor_reduce(need[:], sel[:], AX, ALU.add))
            s.settle()
            s.mark(dve.tensor_scalar(need[:], need[:], -1.0, float(K0), ALU.mult, ALU.add))
            dve.wait_ge(s_exp, 1)
            s.mark(dve.tensor_copy(logits[:], eq[0][:]))
            s.settle()
            step, cur = 1, 0
            while step < E0:
                s.mark(dve.tensor_copy(eq[1 - cur][:, :, 0:step], eq[cur][:, :, 0:step]))
                s.mark(dve.tensor_tensor(eq[1 - cur][:, :, step:], eq[cur][:, :, step:], eq[cur][:, :, 0:E0 - step],
                                         ALU.add))
                s.settle()
                cur, step = 1 - cur, step * 2
            s.mark(dve.tensor_tensor(eq[cur][:], eq[cur][:], per_tile(need), ALU.is_le))
            s.settle()
            s.mark(dve.tensor_tensor(eq[cur][:], eq[cur][:], logits[:], ALU.mult))
            s.settle()
            s.mark(dve.tensor_tensor(sel[:], sel[:], eq[cur][:], ALU.add))
            s.settle()
            s.mark(dve.tensor_tensor(e[:], e[:], sel[:], ALU.mult))
            s.settle()
            s.mark(dve.tensor_reduce(total[:], e[:], AX, ALU.add))
            s.settle()
            s.mark(dve.reciprocal(total[:], total[:]))
            s.settle()
            dve.tensor_tensor(weight[:], e[:], per_tile(total), ALU.mult).then_inc(s_weight, 1)
            for g in range(NT // 4):
                dve.wait_ge(s_bias, g + 1)
                dve.tensor_tensor(x_sb[:, 4 * g:4 * g + 4, :], x_sb[:, 4 * g:4 * g + 4, :], ps_b[:],
                                  ALU.add).then_inc(s_added, 1)
            dve.wait_ge(s_added, NT // 4)


def l0_experts(nc, x_sb, xlnT, w1, b1, w2, weight):
    with ExitStack() as st:
        a = Alloc(nc, st)
        hid = a.sb("e_hid", [P, 2, 2, CH])
        ps_h = [a.ps(f"e_ps_h{i}", [P, 2, CH]) for i in range(2)]
        ps_y = [a.ps(f"e_ps_y{i}", [P, CT, E]) for i in range(2)]
        h_ps, h_sb, y_ps, y_added = (a.sem("e_" + n) for n in "h_ps h_sb y_ps y_added".split())
        a.start_at_one()
        block = st.enter_context(nc.Block())

        @block.tensor
        def _(pe):
            def up(u, c, e):
                if not (isinstance(u, int) and u < 2):
                    pe.wait_ge(h_sb, ONE + u * 2 - 2)
                for half in range(2):
                    mm = pe.matmul(ps_h[e % 2][:, half, :], w1[:, e, half * P:(half + 1) * P],
                                   xlnT[:, bass.ds(c * CH, CH)], start=True, stop=True)
                    mm.then_inc(h_ps, 1)

            def down(u, e):
                pe.wait_ge(h_sb, ONE + u * 2 + 2)
                if e >= 2:
                    pe.wait_ge(y_added, ONE + u * CT - CT)
                else:
                    pe.wait_ge(y_added, ONE + u * CT - CT * e)
                for t in range(CT):
                    for half in range(2):
                        mm = pe.matmul(ps_y[e % 2][:, t, :], hid[:, e % 2, half, t * P:(t + 1) * P], w2[:, e, half, :],
                                       start=(half == 0), stop=(half == 1))
                mm.then_inc(y_ps, 1)

            with pe.Fori(0, NT * P // CH) as c:
                u0 = c * E0
                for half in range(2):
                    pe.wait_ge(h_sb, ONE + u0 * 2)
                    pe.matmul(ps_h[0][:, half, :], w1[:, 0, half * P:(half + 1) * P], xlnT[:, bass.ds(c * CH, CH)],
                              start=True, stop=True).then_inc(h_ps, 1)
                for e in range(E0):
                    if e + 1 < E0:
                        if e == 0:
                            pe.wait_ge(h_sb, ONE + u0 * 2)
                            for half in range(2):
                                pe.matmul(ps_h[1][:, half, :], w1[:, 1, half * P:(half + 1) * P],
                                          xlnT[:, bass.ds(c * CH, CH)], start=True, stop=True).then_inc(h_ps, 1)
                        else:
                            up(u0 + e + 1, c, e + 1)
                    down(u0 + e, e)

        @block.scalar
        def _(act):
            with act.Fori(0, NT * P // CH) as c:
                for e in range(E0):
                    u = c * E0 + e
                    if e >= 2:
                        act.wait_ge(y_ps, ONE + u - 1)
                    else:
                        act.wait_ge(y_ps, ONE + u - e)
                    for half in range(2):
                        act.wait_ge(h_ps, ONE + u * 2 + half + 1)
                        act.activation(hid[:, e % 2, half, :], ps_h[e % 2][:, half, :], ACT.Gelu,
                                       bias=b1[:, e, half:half + 1]).then_inc(h_sb, 1)

        @block.vector
        def _(dve):
            with dve.Fori(0, NT * P // CH) as c:
                for e in range(E0):
                    u = c * E0 + e
                    dve.wait_ge(y_ps, ONE + u + 1)
                    if e:
                        dve.wait_ge(y_added, ONE + u * CT)
                    for t in range(CT):
                        x_t = x_sb[:, bass.ds(c * CT + t, 1), :].rearrange("p o e -> p (o e)")
                        w_t = weight[:, bass.ds(c * CT + t, 1), e:e + 1].rearrange("p o e -> p (o e)")
                        dve.scalar_tensor_tensor(x_t, ps_y[e % 2][:, t, :], w_t, x_t, ALU.mult,
                                                 ALU.add).then_inc(y_added, 1)
            dve.wait_ge(y_added, ONE + NT * P // CH * E0 * CT)


H1, D1 = 2, 64
PAIRS = H1 * QT
RMS_EPS = 1e-8
SCALE1 = float(D1) ** -0.5
GT = 4
LK = S // P


def l1_flags(nc, mask, scratch, flags):
    with ExitStack() as st:
        a = Alloc(nc, st)
        raw = a.sb("f_raw", [B, KEYS], U8)
        best = a.sb("f_best", [B, NW])
        seen = a.sb("f_seen", [B, NW])
        line = a.sb("f_line", [1, B * NW])
        bits = a.sb("f_bits", [1, B // 2, NW])
        word = a.sb("f_word", [1, B // 2])
        loaded, steps, stored, done = a.sem("f_loaded"), a.sem("f_steps"), a.sem("f_stored"), a.sem("f_done")
        block = st.enter_context(nc.Block())

        @block.sync
        def _(sp):
            sp.dma_start(raw[:], mask).then_inc(loaded, 16)
            sp.wait_ge(steps, 2 * NW)
            sp.dma_start(scratch, seen[:]).then_inc(stored, 16)
            sp.wait_ge(stored, 16)
            sp.dma_start(line[:], scratch.rearrange("b w -> (b w)").unsqueeze(0)).then_inc(done, 16)
            sp.wait_ge(done, 16)

        @block.vector
        def _(dve):
            s = Steps(dve, steps)
            dve.wait_ge(loaded, 16)
            for w in range(NW):
                own = FIRST_OWN if w == 0 else W
                s.mark(dve.tensor_reduce(best[:, w:w + 1], raw[:, START[w]:START[w] + own], AX, ALU.max))
            s.settle()
            for w in range(NW):
                s.mark(dve.tensor_scalar(seen[:, w:w + 1], best[:, w:w + 1], 0.0, float(2 ** w), ALU.not_equal,
                                         ALU.mult))
            dve.wait_ge(done, 16)
            s.mark(dve.tensor_reduce(bits[:], line[:].rearrange("o (g b w) -> o g w b", b=2, w=NW), AX, ALU.max))
            s.settle()
            s.mark(dve.tensor_reduce(word[:], bits[:], AX, ALU.add))
            s.settle()
            s.mark(dve.tensor_copy(flags[:], word[:]))
            s.settle()


def each_live_window(eng, flags, g, body):
    word = eng.value_load(flags[0:1, bass.ds(g, 1)], min_val=0, max_val=2 ** NW - 1)
    for w in range(NW):
        with eng.If((word & 2 ** w) != 0):
            body(w)


def l1_project(nc, tag, ident, gain, shift, wkv, gk, latents=None, context=None):
    NORMS = 2 if latents else 1
    HALVES = range(2)
    with ExitStack() as st:
        a = Alloc(nc, st)
        rows = a.sb(tag + "rows", [P, 2, GT, E]) if context else None
        stats = a.sb(tag + "stats", [P, 2, GT, 6])
        mv = a.sb(tag + "mv", [P, 2, GT, 2])
        var = a.sb(tag + "var", [P, 2, GT])
        rstd = a.sb(tag + "rstd", [P, 2, GT])
        off = a.sb(tag + "off", [P, 2, GT])
        expo = a.sb(tag + "expo", [P, NORMS * GT * H1])
        xn = a.sb(tag + "xn", [P, 2, GT, E])
        xnT = a.sb(tag + "xnT", [P, 2, GT * P])
        sq = a.sb(tag + "sq", [P, 2, NORMS, GT, E])
        ms = a.sb(tag + "ms", [P, 2, NORMS * GT * H1])
        rms = a.sb(tag + "rms", [P, 2, NORMS * GT * H1])
        normed_rows = a.sb(tag + "nr", [P, 2, NORMS, GT, E])
        if context:
            kT_out = a.sb(tag + "kT_out", [P, 2, GT * P])
            v_out = a.sb(tag + "v_out", [P, 2, GT, E])
        ps_x, ps_k, ps_v = ([a.ps(f"{tag}ps_{n}{h}", [P, GT, P]) for h in HALVES] for n in "xkv")
        ps_q = [a.ps(f"{tag}ps_q{h}", [P, GT, P]) for h in HALVES] if latents else None
        ps_kq = [ps_k, ps_q]
        sem = [{n: a.sem(f"{tag}{n}{h}") for n in (
            "loaded stats_ready var_ready rstd_ready xn_ready xnT_ps xnT_sb kv_ps sq_sb v_sb ms_ready rms_ready "
            "nr_ready nT_ps nT_sb k_stored v_stored").split()} for h in HALVES]
        expo_set, steps = a.sem(tag + "expo_set"), a.sem(tag + "steps")
        a.start_at_one()
        block = st.enter_context(nc.Block())

        counts = {}

        def each(eng, body):
            if latents:
                with eng.Fori(0, NT // GT // 2) as g:
                    body(g, g, 0)
                return
            n = counts[eng] = eng.alloc_register(tag + "n")
            eng.reg_mov(n, 0)

            def window(g, w):
                body(eng.snap(n), g, w)
                eng.reg_add(n, n, 1)
            with eng.Fori(0, B // 2) as g:
                each_live_window(eng, context[1], g, lambda w: window(g, w))

        @block.sync
        def _(sp):
            if latents:
                return
            ctx_rows = context[0].rearrange("b k e -> (b k) e")

            def body(done, g, w):
                for h in HALVES:
                    at = sp.snap((g * 2 + h) * KEYS + START[w])
                    sp.wait_ge(sem[h]["xn_ready"], ONE + done)
                    sp.dma_start(rows[:, h, :, :], ctx_rows[bass.ds(at, W), :].rearrange(
                        "(t p) e -> p t e", p=P)).then_inc(sem[h]["loaded"], 16)
            each(sp, body)

        @block.gpsimd
        def _(pool):
            pool.memset(expo[:], -0.5).then_inc(expo_set, 1)
            pool.wait_ge(expo_set, ONE + 1)

            def body(done, g, w):
                for h in HALVES:
                    pool.wait_ge(sem[h]["var_ready"], ONE + done + 1)
                    pool.tensor_tensor(rstd[:, h, :], var[:, h, :], expo[:, 0:GT],
                                       ALU.pow).then_inc(sem[h]["rstd_ready"], 1)
                for h in HALVES:
                    pool.wait_ge(sem[h]["ms_ready"], ONE + done + 1)
                    pool.tensor_tensor(rms[:, h, :], ms[:, h, :], expo[:], ALU.pow).then_inc(sem[h]["rms_ready"], 1)
            each(pool, body)
            if context:
                for h in HALVES:
                    pool.wait_ge(sem[h]["v_stored"], ONE + pool.snap(counts[pool]) * 16)
                    pool.wait_ge(sem[h]["k_stored"], ONE + pool.snap(counts[pool]) * 16)

        @block.tensor
        def _(pe):
            def body(done, g, w):
                for h in HALVES:
                    pe.wait_ge(sem[h]["xn_ready"], ONE + done + 1)
                    for i in range(GT):
                        mm = pe.transpose(ps_x[h][:, i, :], xn[:, h, i, :], ident[:])
                    mm.then_inc(sem[h]["xnT_ps"], 1)
                for h in HALVES:
                    pe.wait_ge(sem[h]["xnT_sb"], ONE + done + 1)
                    pe.wait_ge(sem[h]["nT_sb"], ONE + done)
                    pe.wait_ge(sem[h]["v_sb"], ONE + done)
                    for bank, weights in ((ps_k[h], wkv[:, 0:E]), (ps_q[h] if latents else None,
                                          latents[1][:] if latents else None), (ps_v[h], wkv[:, E:])):
                        for i in range(GT):
                            if weights is not None:
                                mm = pe.matmul(bank[:, i, :], xnT[:, h, i * P:(i + 1) * P], weights, start=True,
                                               stop=True)
                    mm.then_inc(sem[h]["kv_ps"], 1)
                for h in HALVES:
                    pe.wait_ge(sem[h]["nr_ready"], ONE + done + 1)
                    for c in range(NORMS):
                        for i in range(GT):
                            mm = pe.transpose(ps_kq[c][h][:, i, :], normed_rows[:, h, c, i, :], ident[:])
                    mm.then_inc(sem[h]["nT_ps"], 1)
            each(pe, body)

        @block.scalar
        def _(act):
            def body(done, g, w):
                for h in HALVES:
                    act.wait_ge(sem[h]["xnT_ps"], ONE + done + 1)
                    act.activation(xnT[:, h, :], ps_x[h][:].rearrange("p t q -> p (t q)"), ACT.Identity,
                                   bias=shift[:], scale=gain[:]).then_inc(sem[h]["xnT_sb"], 1)
                for h in HALVES:
                    act.wait_ge(sem[h]["kv_ps"], ONE + done + 1)
                    mm = act.activation(sq[:, h, 0, :, :], ps_k[h][:], ACT.Square)
                    if latents:
                        mm = act.activation(sq[:, h, 1, :, :], ps_q[h][:], ACT.Square)
                    mm.then_inc(sem[h]["sq_sb"], 1)
                for h in HALVES:
                    if context:
                        act.wait_ge(sem[h]["v_stored"], ONE + done * 16)
                        v_to = v_out[:, h, :, :]
                    else:
                        v_to = latents[5][:, bass.ds((g * 2 + h) * GT, GT), :]
                    act.activation(v_to, ps_v[h][:], ACT.Copy).then_inc(sem[h]["v_sb"], 1)
                for h in HALVES:
                    if context:
                        at = act.snap(g * 2 + h)
                        act.wait_ge(sem[h]["nT_ps"], ONE + done + 1)
                        act.wait_ge(sem[h]["k_stored"], ONE + done * 16)
                        act.activation(kT_out[:, h, :], ps_k[h][:].rearrange("p t q -> p (t q)"), ACT.Copy,
                                       scale=gk[:]).then_inc(sem[h]["nT_sb"], 1)
                        act.wait_ge(sem[h]["v_sb"], ONE + done + 1)
                        act.dma_start(context[3][bass.ds(at, 1), w, :, :].rearrange("o p c -> (o p) c"),
                                      v_out[:, h, :, :].rearrange("p t e -> p (t e)")).then_inc(sem[h]["v_stored"], 16)
                        act.wait_ge(sem[h]["nT_sb"], ONE + done + 1)
                        act.dma_start(context[2][bass.ds(at, 1), w, :, :].rearrange("o p c -> (o p) c"),
                                      kT_out[:, h, :]).then_inc(sem[h]["k_stored"], 16)
                    else:
                        act.wait_ge(sem[h]["nT_ps"], ONE + done + 1)
                        to = bass.ds((g * 2 + h) * GT * P, GT * P)
                        act.activation(latents[4][:, to], ps_k[h][:].rearrange("p t q -> p (t q)"), ACT.Copy,
                                       scale=gk[:])
                        act.activation(latents[3][:, to], ps_q[h][:].rearrange("p t q -> p (t q)"), ACT.Copy,
                                       scale=latents[2][:]).then_inc(sem[h]["nT_sb"], 1)
            each(act, body)

        @block.vector
        def _(dve):
            total = dve.alloc_register(tag + "steps")
            dve.reg_mov(total, ONE)
            stats_in = [Awaited(dve, sem[h]["stats_ready"], f"{tag}stats_at{h}") for h in HALVES]

            def body(done, g, w):
                s = Steps(dve, steps, dve.snap(total))

                def row(h, i):
                    if context:
                        return rows[:, h, i, :]
                    return latents[0][:, bass.ds((g * 2 + h) * GT + i, 1), :].rearrange("p o e -> p (o e)")
                for h in HALVES:
                    at = stats_in[h].at()
                    if context:
                        dve.wait_ge(sem[h]["loaded"], ONE + (done + 1) * 16)
                    for i in range(GT):
                        ins = dve.bn_stats(stats[:, h, i, :], row(h, i))
                    ins.then_inc(sem[h]["stats_ready"], 1)
                    stats_in[h].wait(at)
                    for i in range(GT):
                        s.mark(dve.bn_aggr(mv[:, h, i, :], stats[:, h, i, :]))
                    s.settle()
                    dve.tensor_scalar(var[:, h, :], mv[:, h, :, 1], EPS, None,
                                      ALU.add).then_inc(sem[h]["var_ready"], 1)
                for h in HALVES:
                    dve.wait_ge(sem[h]["rstd_ready"], ONE + done + 1)
                    s.mark(dve.scalar_tensor_tensor(off[:, h, :], mv[:, h, :, 0], -1.0, rstd[:, h, :], ALU.mult,
                                                    ALU.mult))
                    s.settle()
                    dve.wait_ge(sem[h]["xnT_ps"], ONE + done)
                    for i in range(GT):
                        ins = dve.tensor_scalar(xn[:, h, i, :], row(h, i), rstd[:, h, i:i + 1], off[:, h, i:i + 1],
                                                ALU.mult, ALU.add)
                    ins.then_inc(sem[h]["xn_ready"], 1)
                for h in HALVES:
                    dve.wait_ge(sem[h]["sq_sb"], ONE + done + 1)
                    s.mark(dve.tensor_reduce(ms[:, h, :], sq[:, h, :, :, :].rearrange("p c t (h d) -> p (c t h) d", d=D1),
                                             AX, ALU.add))
                    s.settle()
                    dve.tensor_scalar(ms[:, h, :], ms[:, h, :], 1.0 / D1, RMS_EPS ** 2, ALU.mult,
                                      ALU.max).then_inc(sem[h]["ms_ready"], 1)
                for h in HALVES:
                    dve.wait_ge(sem[h]["rms_ready"], ONE + done + 1)
                    dve.wait_ge(sem[h]["nT_ps"], ONE + done)
                    for c in range(NORMS):
                        by_head = rms[:, h, c * GT * H1:(c + 1) * GT * H1].rearrange(
                            "p (t h) -> p t h", h=H1).unsqueeze(3).broadcast_to([P, GT, H1, D1])
                        ins = dve.tensor_tensor(normed_rows[:, h, c, :, :].rearrange("p t (h d) -> p t h d", d=D1),
                                                ps_kq[c][h][:].rearrange("p t (h d) -> p t h d", d=D1), by_head,
                                                ALU.mult)
                    ins.then_inc(sem[h]["nr_ready"], 1)
                dve.reg_add(total, total, s.n)
            each(dve, body)


def l1_attention(nc, x_sb, ident, flags, mask, qT, klT, vl, kT_dram, v_dram, wout, bout, probsT):
    mask_flat = mask.rearrange("b k -> (b k)")
    PT = 2 * QT
    SH = (P, 2, PAIRS)
    with ExitStack() as st:
        a = Alloc(nc, st)
        qbd = a.sb("b_qbd", [P, 2, 2, H1, S])
        kT = a.sb("b_kT", [P, 2, W])
        v = a.sb("b_v", [P, 2, KT, E])
        raw = a.sb("b_raw", [P, 2, W], U8)
        neg = a.sb("b_neg", [P, 2, W])
        none = a.sb("b_none", [P, S])
        scores = a.sb("b_scores", [P, 2, PAIRS, W])
        m_old, m_src, m_new, m_diff, alpha, neg_m, l_src, l_sum = (
            a.sb("b_" + n, list(SH)) for n in "m_old m_src m_new m_diff alpha neg_m l_src l_sum".split())
        acc = a.sb("b_acc", [P, 2, QT, H1, D1])
        heads = a.sb("b_heads", [P, 2, QT, E])
        headsT = a.sb("b_headsT", [P, 2 * S])
        ps_s = [a.ps(f"b_ps_s{i}", [P, W]) for i in range(2)]
        ps_t = [a.ps(f"b_ps_t{i}", [P, KT, P]) for i in range(2)]
        ps_o = [a.ps(f"b_ps_o{i}", [P, QT, H1, D1]) for i in range(2)]
        ps_h = a.ps("b_ps_h", [P, 2 * S])
        ps_y = a.ps("b_ps_y", [P, PT, E])
        sem = {n: a.sem("b_" + n) for n in (
            "qbd_zeroed qbd_ready k_loaded v_loaded m_loaded s_ps s_sb neg_m_ready alpha_ready p_sb t_ps t_act t_dve "
            "o_ps0 o_ps1 acc_done0 acc_done1 heads_ready headsT_ps headsT_sb y_ps x_done steps").split()}
        a.start_at_one()
        block = st.enter_context(nc.Block())

        def by_head(t, c):
            return t[:, c, :].rearrange("p (h t) -> p t h", t=QT).unsqueeze(3).broadcast_to([P, QT, H1, D1])

        def sources(eng, name):
            n = eng.alloc_register(name)
            eng.reg_mov(n, 0)
            return n

        @block.sync
        def _(sp):
            n, m, used = sources(sp, "b_n"), sources(sp, "b_m"), sources(sp, "b_used")
            with sp.Fori(0, B // 2) as g:
                sp.reg_add(n, n, 1)

                def load(w):
                    pair = [sp.snap(g * 2 + c) for c in range(2)]
                    mask_at = [sp.snap((g * 2 + c) * KEYS + START[w]) for c in range(2)]
                    sp.wait_ge(sem["o_ps1"], ONE + sp.snap(used))
                    for c in range(2):
                        sp.dma_start(raw[:, c, :], mask_flat[bass.ds(mask_at[c], W)].partition_broadcast(P)).then_inc(
                            sem["m_loaded"], 16)
                    for c in range(2):
                        sp.dma_start(kT[:, c, :], kT_dram[bass.ds(pair[c], 1), w, :, :].rearrange(
                            "o p c -> (o p) c")).then_inc(sem["k_loaded"], 16)
                    for c in range(2):
                        sp.dma_start(v[:, c, :, :].rearrange("p t e -> p (t e)"), v_dram[
                            bass.ds(pair[c], 1), w, :, :].rearrange("o p c -> (o p) c")).then_inc(sem["v_loaded"], 16)
                    sp.reg_add(n, n, 1)
                    sp.reg_mov(used, n)
                each_live_window(sp, flags, g, load)

        @block.gpsimd
        def _(pool):
            pool.memset(qbd[:], 0.0).then_inc(sem["qbd_zeroed"], 1)
            pool.wait_ge(sem["qbd_zeroed"], ONE + 1)

            def spread(g, half):
                for h in range(H1):
                    rows = slice(h * D1, (h + 1) * D1)
                    pool.tensor_copy(qbd[rows, half, :, h, :], qT[rows, bass.ds(g * 2 * S, 2 * S)].rearrange(
                        "p (c s) -> p c s", c=2)).then_inc(sem["qbd_ready"], 1)
            spread(0, 0)
            spread(1, 1)
            with pool.Fori(1, B // 4) as i:
                for half in range(2):
                    pool.wait_ge(sem["headsT_ps"], ONE + i * 2 - 1 + half)
                    spread(i * 2 + half, half)

        @block.tensor
        def _(pe):
            n, m = sources(pe, "b_n"), sources(pe, "b_m")

            def source(src, half, tiles, key, value, between=None, after=None):
                def one_score(c, j):
                    h, t = j // QT, j % QT
                    pe.wait_ge(sem["s_sb"], ONE + src * 2 * PAIRS + max(c * PAIRS + j - 1, 0))
                    pe.matmul(ps_s[j % 2][:, 0:tiles * P], qbd[:, half, c, h, t * P:(t + 1) * P], key(c), start=True,
                              stop=True).then_inc(sem["s_ps"], 1)
                for j in range(PAIRS):
                    one_score(0, j)
                for c in range(2):
                    u = src * 2 + c
                    for j in range(PAIRS):
                        if c == 0:
                            one_score(1, j)
                        pe.wait_ge(sem["p_sb"], ONE + u * PAIRS + j + 1)
                        pe.wait_ge(sem["t_act" if j % 2 == 0 else "t_dve"], ONE + u * (PAIRS // 2) + j // 2)
                        for k in range(tiles):
                            mm = pe.transpose(ps_t[j % 2][:, k, :], scores[:, c, j, k * P:(k + 1) * P], ident[:])
                        mm.then_inc(sem["t_ps"], 1)
                    pe.wait_ge(sem[f"acc_done{c}"], ONE + src)
                    for j in range(PAIRS):
                        h, t = j // QT, j % QT
                        pe.wait_ge(sem["t_act" if j % 2 == 0 else "t_dve"], ONE + u * (PAIRS // 2) + j // 2 + 1)
                        for k in range(tiles):
                            mm = pe.matmul(ps_o[c][:, t, h, :], probsT[:, c, j, k, :], value(c, k, h), start=(k == 0),
                                           stop=(k == tiles - 1))
                    mm.then_inc(sem[f"o_ps{c}"], 1)
                    if c == 0 and between:
                        between()
                if after:
                    after()

            def turn_heads(g):
                pe.wait_ge(sem["heads_ready"], ONE + g)
                for t in range(PT):
                    mm = pe.transpose(ps_h[:, t * P:(t + 1) * P], heads[:, t // QT, t % QT, :], ident[:])
                mm.then_inc(sem["headsT_ps"], 1)

            def project_heads(g):
                pe.wait_ge(sem["headsT_sb"], ONE + g)
                pe.wait_ge(sem["x_done"], ONE + g - 1)
                for t in range(PT):
                    mm = pe.matmul(ps_y[:, t, :], headsT[:, t * P:(t + 1) * P], wout[:], start=True, stop=True)
                mm.then_inc(sem["y_ps"], 1)

            def pair(g, half):
                def unless_first(step):
                    with pe.If(g > 0):
                        step(g)
                pe.wait_ge(sem["qbd_ready"], ONE + g * H1 + H1)
                source(pe.snap(n), half, LK, lambda c: klT[:, bass.ds((g * 2 + c) * S, S)],
                       lambda c, k, h: vl[:, bass.ds((g * 2 + c) * LK + k, 1), h * D1:(h + 1) * D1].rearrange(
                           "p o d -> p (o d)"),
                       lambda: unless_first(turn_heads), lambda: unless_first(project_heads))
                pe.reg_add(n, n, 1)

                def window(w):
                    win = pe.snap(m)
                    pe.wait_ge(sem["k_loaded"], ONE + (win + 1) * 32)
                    pe.wait_ge(sem["v_loaded"], ONE + (win + 1) * 32)
                    source(pe.snap(n), half, KT, lambda c: kT[:, c, :], lambda c, k, h: v[:, c, k, h * D1:(h + 1) * D1])
                    pe.reg_add(n, n, 1)
                    pe.reg_add(m, m, 1)
                each_live_window(pe, flags, g, window)

            with pe.Fori(0, B // 4) as i:
                pair(i * 2, 0)
                pair(i * 2 + 1, 1)
            turn_heads(B // 2)
            project_heads(B // 2)

        @block.scalar
        def _(act):
            n = sources(act, "b_n")

            def turn_heads(g):
                act.wait_ge(sem["headsT_ps"], ONE + g)
                act.wait_ge(sem["y_ps"], ONE + g - 1)
                act.activation(headsT[:], ps_h[:], ACT.Copy).then_inc(sem["headsT_sb"], 1)

            def source(src, tiles, between=None):
                for c in range(2):
                    u = src * 2 + c
                    act.wait_ge(sem["neg_m_ready"], ONE + u + 1)
                    act.wait_ge(sem[f"acc_done{c}"], ONE + src)
                    act.activation(alpha[:, c, :], m_diff[:, c, :], ACT.Exp).then_inc(sem["alpha_ready"], 1)
                    for j in range(PAIRS):
                        act.activation(scores[:, c, j, 0:tiles * P], scores[:, c, j, 0:tiles * P], ACT.Exp,
                                       bias=neg_m[:, c, j:j + 1],
                                       accum_out=l_src[:, c, j:j + 1]).then_inc(sem["p_sb"], 1)
                        if j % 2:
                            act.wait_ge(sem["t_ps"], ONE + u * PAIRS + j)
                            act.wait_ge(sem[f"o_ps{c}"], ONE + src)
                            act.activation(probsT[:, c, j - 1, 0:tiles, :], ps_t[0][:, 0:tiles, :],
                                           ACT.Copy).then_inc(sem["t_act"], 1)
                        if between and c == 1 and j == 1:
                            between()

            def window(w):
                source(act.snap(n), KT)
                act.reg_add(n, n, 1)

            with act.Fori(0, B // 2) as g:
                def unless_first():
                    with act.If(g > 0):
                        turn_heads(g)
                source(act.snap(n), LK, unless_first)
                act.reg_add(n, n, 1)
                each_live_window(act, flags, g, window)
            turn_heads(B // 2)

        @block.vector
        def _(dve):
            n, m = sources(dve, "b_n"), sources(dve, "b_m")
            total = dve.alloc_register("b_n_steps")
            scores_in = Awaited(dve, sem["s_ps"], "b_s_ps_at")
            s0 = Steps(dve, sem["steps"], ONE)
            for state in (none, l_sum, acc):
                s0.mark(dve.memset(state[:], 0.0))
            s0.mark(dve.memset(m_old[:], NO_MAX))
            s0.settle()
            dve.reg_mov(total, ONE + s0.n)

            def source(src, s, tiles, added):
                def reduce_one(c, j):
                    at = scores_in.at()
                    if c == 0 and j == 0:
                        dve.wait_ge(sem["t_ps"], ONE + src * 2 * PAIRS)
                    scores_in.wait(at)
                    dve.tensor_tensor_reduce(scores[:, c, j, 0:tiles * P], ps_s[j % 2][:, 0:tiles * P], added(c), 1.0,
                                             NO_MAX, ALU.add, ALU.max, m_src[:, c, j:j + 1]).then_inc(sem["s_sb"], 1)

                def shift(c):
                    dve.wait_ge(sem["s_sb"], ONE + (src * 2 + c + 1) * PAIRS)
                    s.mark(dve.tensor_tensor(m_new[:, c, :], m_old[:, c, :], m_src[:, c, :], ALU.max))
                    s.settle()
                    s.mark(dve.tensor_tensor(m_diff[:, c, :], m_old[:, c, :], m_new[:, c, :], ALU.subtract))
                    s.settle()
                    s.mark(dve.tensor_copy(m_old[:, c, :], m_new[:, c, :]))
                    dve.tensor_scalar(neg_m[:, c, :], m_new[:, c, :], -1.0, None,
                                      ALU.mult).then_inc(sem["neg_m_ready"], 1)

                def move(c, j):
                    dve.wait_ge(sem["t_ps"], ONE + (src * 2 + c) * PAIRS + j + 1)
                    dve.wait_ge(sem[f"o_ps{c}"], ONE + src)
                    dve.tensor_copy(probsT[:, c, j, 0:tiles, :], ps_t[1][:, 0:tiles, :]).then_inc(sem["t_dve"], 1)

                def rescale(c):
                    dve.wait_ge(sem["alpha_ready"], ONE + src * 2 + c + 1)
                    dve.wait_ge(sem["p_sb"], ONE + (src * 2 + c + 1) * PAIRS)
                    s.mark(dve.tensor_tensor(l_sum[:, c, :], l_sum[:, c, :], alpha[:, c, :], ALU.mult))
                    s.mark(dve.tensor_tensor(acc[:, c], acc[:, c], by_head(alpha, c), ALU.mult))
                    s.settle()
                    s.mark(dve.tensor_tensor(l_sum[:, c, :], l_sum[:, c, :], l_src[:, c, :], ALU.add))

                def add_heads(c):
                    dve.wait_ge(sem[f"o_ps{c}"], ONE + src + 1)
                    dve.tensor_tensor(acc[:, c], acc[:, c], ps_o[c][:], ALU.add).then_inc(sem[f"acc_done{c}"], 1)

                for j in range(PAIRS):
                    reduce_one(0, j)
                shift(0)
                for j in range(PAIRS):
                    reduce_one(1, j)
                    if j % 2:
                        move(0, j)
                shift(1)
                rescale(0)
                move(1, 1)
                add_heads(0)
                move(1, 3)
                rescale(1)
                add_heads(1)
                s.settle()

            def give_heads(g):
                s = Steps(dve, sem["steps"], dve.snap(total))
                for c in range(2):
                    dve.wait_ge(sem[f"acc_done{c}"], ONE + dve.snap(n))
                s.mark(dve.reciprocal(l_sum[:], l_sum[:]))
                s.settle()
                dve.wait_ge(sem["headsT_ps"], ONE + g - 1)
                for c in range(2):
                    ins = dve.tensor_tensor(heads[:, c, :, :].rearrange("p t (h d) -> p t h d", d=D1), acc[:, c],
                                            by_head(l_sum, c), ALU.mult)
                    if c == 0:
                        s.mark(ins)
                ins.then_inc(sem["heads_ready"], 1)
                s.settle()
                dve.wait_ge(sem["heads_ready"], ONE + g)
                s.mark(dve.memset(m_old[:], NO_MAX))
                s.mark(dve.memset(l_sum[:], 0.0))
                s.mark(dve.memset(acc[:], 0.0))
                s.settle()
                dve.reg_add(total, total, s.n)

            def add_to_x(g):
                s = Steps(dve, sem["steps"], dve.snap(total))
                dve.wait_ge(sem["y_ps"], ONE + g)
                at = (g - 1) * PT if isinstance(g, int) else nc.s_assert_within(
                    (g - 1) * PT, 0, (B // 2 - 2) * PT, skip_runtime_bounds_check_because="only taken where g > 0")
                x_g = x_sb[:, bass.ds(at, PT), :]
                s.mark(dve.tensor_tensor(x_g, x_g, ps_y[:], ALU.add))
                s.settle()
                dve.tensor_tensor(x_g, x_g, bout[:].unsqueeze(1).broadcast_to([P, PT, E]),
                                  ALU.add).then_inc(sem["x_done"], 1)
                dve.reg_add(total, total, s.n)

            def window(w):
                s = Steps(dve, sem["steps"], dve.snap(total))
                dve.wait_ge(sem["m_loaded"], ONE + (dve.snap(m) + 1) * 32)
                own = FIRST_OWN if w == 0 else W
                s.mark(dve.tensor_scalar(neg[:, :, 0:own], raw[:, :, 0:own], 0.0, MASKED, ALU.is_equal, ALU.mult))
                if own < W:
                    s.mark(dve.memset(neg[:, :, own:], DOUBLED))
                s.settle()
                source(dve.snap(n), s, KT, lambda c: neg[:, c, :])
                dve.reg_add(total, total, s.n)
                dve.reg_add(n, n, 1)
                dve.reg_add(m, m, 1)

            with dve.Fori(0, B // 2) as g:
                with dve.If(g > 0):
                    give_heads(g)
                s = Steps(dve, sem["steps"], dve.snap(total))
                source(dve.snap(n), s, LK, lambda c: none[:])
                dve.reg_add(n, n, 1)
                dve.reg_add(total, total, s.n)
                with dve.If(g > 0):
                    add_to_x(g)
                each_live_window(dve, flags, g, window)
            give_heads(B // 2)
            add_to_x(B // 2)
            dve.wait_ge(sem["x_done"], ONE + B // 2)


E1, I1 = 32, 256
TILES = NT + E1 - 1
TP = -(-TILES // 2)
SLOTS = 2 * TP * P


def l1_route(nc, xln, xlnT, gate, position, expert_of, n_tiles):
    with ExitStack() as st:
        a = Alloc(nc, st)
        best = a.sb("g_best", [P, NT])
        score = a.sb("g_score", [P, NT])
        choice = a.sb("g_choice", [P, NT])
        num = a.sb("g_num", [P, E1], I32)
        num_f = a.sb("g_num_f", [P, E1])
        mark = a.sb("g_mark", [P, NT, E1])
        hot = a.sb("g_hot", [P, NT, E1], BF16)
        below = a.sb("g_below", [P, P], BF16)
        ones = a.sb("g_ones", [P, P], BF16)
        before = [a.sb(f"g_before{i}", [P, NT, E1]) for i in range(2)]
        size = a.sb("g_size", [P, E1])
        tiles_of = a.sb("g_tiles_of", [P, E1])
        end = [a.sb(f"g_end{i}", [P, E1]) for i in range(2)]
        slot = a.sb("g_slot", [P, NT])
        tile_num = a.sb("g_tile_num", [1, 2 * TP], I32)
        tile_num_f = a.sb("g_tile_num_f", [1, 2 * TP])
        past = a.sb("g_past", [1, 2 * TP, E1])
        tile_expert = a.sb("g_tile_expert", [1, 2 * TP])
        ps_l = a.ps("g_ps_l", [P, NT, E1])
        ps_r = a.ps("g_ps_r", [P, NT, E1])
        ps_c = a.ps("g_ps_c", [P, NT, E1])
        logits, consts, best_ready, scored, hot_ready, counted, steps = (
            a.sem("g_s_" + n) for n in "logits consts best scored hot counted steps".split())
        block = st.enter_context(nc.Block())
        HALF = NT // 2

        @block.gpsimd
        def _(pool):
            pool.iota(num[:], [[1, E1]], base=0, channel_multiplier=0).then_inc(consts, 1)
            pool.iota(tile_num[:], [[1, 2 * TP]], base=0, channel_multiplier=0).then_inc(consts, 1)
            pool.memset(ones[:], 1.0).then_inc(consts, 1)
            pool.memset(below[:], 1.0).then_inc(consts, 1)
            pool.wait_ge(consts, 4)
            pool.affine_select(out=below[:], in_=below[:], compare_op=ALU.is_gt, fill=0.0, base=0,
                               pattern=[[1, P]], channel_multiplier=-1).then_inc(consts, 1)

        @block.tensor
        def _(pe):
            for t in range(NT):
                mm = pe.matmul(ps_l[:, t, :], xlnT[:, t * P:(t + 1) * P], gate[:], start=True, stop=True)
            mm.then_inc(logits, 1)
            pe.wait_ge(hot_ready, 1)
            pe.wait_ge(consts, 5)
            for i in range(2):
                pe.matmul(ps_r[:, i * HALF:(i + 1) * HALF, :], below[:], hot[:, i * HALF:(i + 1) * HALF, :],
                          start=True, stop=True)
                mm = pe.matmul(ps_c[:, i * HALF:(i + 1) * HALF, :], ones[:], hot[:, i * HALF:(i + 1) * HALF, :],
                               start=True, stop=True)
            mm.then_inc(counted, 1)

        @block.scalar
        def _(act):
            act.wait_ge(best_ready, 1)
            act.activation(score[:], best[:], ACT.Sigmoid).then_inc(scored, 1)

        @block.vector
        def _(dve):
            s = Steps(dve, steps)
            full = [P, NT, E1]
            dve.wait_ge(logits, 1)
            dve.tensor_reduce(best[:], ps_l[:], AX, ALU.max).then_inc(best_ready, 1)
            dve.wait_ge(best_ready, 1)
            dve.wait_ge(consts, 5)
            s.mark(dve.tensor_copy(num_f[:], num[:]))
            s.mark(dve.tensor_copy(tile_num_f[:], tile_num[:]))
            s.mark(dve.tensor_tensor(mark[:], ps_l[:], best[:].unsqueeze(2).broadcast_to(full), ALU.is_equal))
            s.settle()
            s.mark(dve.tensor_scalar(size[:], num_f[:], -float(E1), None, ALU.add))
            s.settle()
            s.mark(dve.tensor_tensor(mark[:], mark[:], size[:].unsqueeze(1).broadcast_to(full), ALU.mult))
            s.settle()
            s.mark(dve.tensor_reduce(choice[:], mark[:], AX, ALU.min))
            s.settle()
            s.mark(dve.tensor_scalar(choice[:], choice[:], float(E1), None, ALU.add))
            s.settle()
            dve.tensor_tensor(hot[:], num_f[:].unsqueeze(1).broadcast_to(full),
                              choice[:].unsqueeze(2).broadcast_to(full), ALU.is_equal).then_inc(hot_ready, 1)
            dve.wait_ge(scored, 1)
            s.mark(dve.tensor_tensor(xln[:], xln[:], score[:].unsqueeze(2).broadcast_to([P, NT, E]), ALU.mult))
            dve.wait_ge(counted, 1)
            s.mark(dve.tensor_copy(before[0][:], ps_c[:]))
            s.settle()
            step, cur = 1, 0
            while step < NT:
                s.mark(dve.tensor_copy(before[1 - cur][:, 0:step, :], before[cur][:, 0:step, :]))
                s.mark(dve.tensor_tensor(before[1 - cur][:, step:, :], before[cur][:, step:, :],
                                         before[cur][:, 0:NT - step, :], ALU.add))
                s.settle()
                cur, step = 1 - cur, step * 2
            s.mark(dve.tensor_copy(size[:], before[cur][:, NT - 1, :]))
            s.settle()
            s.mark(dve.tensor_scalar(end[0][:], num_f[:], float(P), None, ALU.mult))
            s.settle()
            s.mark(dve.tensor_tensor(mark[:, 0:E1, :], size[:].unsqueeze(2).broadcast_to([P, E1, NT]),
                                     end[0][:].unsqueeze(1).broadcast_to([P, E1, NT]), ALU.is_gt))
            s.settle()
            s.mark(dve.tensor_reduce(tiles_of[:], mark[:], AX, ALU.add))
            s.settle()
            s.mark(dve.tensor_copy(end[0][:], tiles_of[:]))
            s.settle()
            step, at = 1, 0
            while step < E1:
                s.mark(dve.tensor_copy(end[1 - at][:, 0:step], end[at][:, 0:step]))
                s.mark(dve.tensor_tensor(end[1 - at][:, step:], end[at][:, step:], end[at][:, 0:E1 - step], ALU.add))
                s.settle()
                at, step = 1 - at, step * 2
            s.mark(dve.tensor_tensor(past[:], end[at][0:1, :].unsqueeze(1).broadcast_to([1, 2 * TP, E1]),
                                     tile_num_f[:].unsqueeze(2).broadcast_to([1, 2 * TP, E1]), ALU.is_le))
            s.mark(dve.tensor_copy(n_tiles[:], end[at][0:1, E1 - 1:E1]))
            s.mark(dve.tensor_tensor(size[:], end[at][:], tiles_of[:], ALU.subtract))
            s.settle()
            s.mark(dve.tensor_reduce(tile_expert[:], past[:], AX, ALU.add))
            s.mark(dve.tensor_scalar(size[:], size[:], float(P), None, ALU.mult))
            s.mark(dve.tensor_tensor(before[cur][:], before[cur][:], ps_c[:], ALU.subtract))
            s.settle()
            s.mark(dve.tensor_scalar(expert_of[:], tile_expert[:], float(E1 - 1), None, ALU.min))
            s.mark(dve.tensor_tensor(before[cur][:], before[cur][:], ps_r[:], ALU.add))
            s.settle()
            s.mark(dve.tensor_tensor(before[cur][:], before[cur][:], size[:].unsqueeze(1).broadcast_to(full), ALU.add))
            s.settle()
            s.mark(dve.tensor_tensor(before[cur][:], before[cur][:], hot[:], ALU.mult))
            s.settle()
            s.mark(dve.tensor_reduce(slot[:], before[cur][:], AX, ALU.add))
            s.settle()
            s.mark(dve.tensor_copy(position[:], slot[:]))
            s.settle()


def start_clearing(nc, zeros, tables, cleared):
    with ExitStack() as st:
        zero_ready = Alloc(nc, st).sem("z_ready")
        block = st.enter_context(nc.Block())
        parts = SLOTS // P // 8

        @block.vector
        def _(dve):
            dve.memset(zeros[:], 0.0).then_inc(zero_ready, 1)

        @block.sync
        def _(sp):
            sp.wait_ge(zero_ready, 1)
            for i in range(parts):
                for table in tables:
                    sp.dma_start(table[i * 8 * P:(i + 1) * 8 * P, :].rearrange("(p t) e -> p t e", p=P),
                                 zeros[:]).then_inc(cleared, 16)
    return parts * len(tables)


def l1_shared(nc, x_sb, xlnT, wgu, wd, xln, position, sorted_x, cleared, n_cleared):
    with ExitStack() as st:
        sent = Alloc(nc, st).sem("z_sent")
        a = Alloc(nc, st)
        act_g = a.sb("s_act_g", [P, 2, CH])
        hid = a.sb("s_hid", [P, 2, CH])
        ps_g = a.ps("s_ps_g", [P, 2, CH])
        ps_u = a.ps("s_ps_u", [P, 2, CH])
        ps_y = [a.ps(f"s_ps_y{i}", [P, CT, E]) for i in range(1)]
        g_ps, u_ps, g_sb, hid_ready, y_ps, y_added = (a.sem("s_" + n) for n in "g_ps u_ps g_sb hid y_ps y_added".split())
        a.start_at_one()
        block = st.enter_context(nc.Block())
        CHUNKS = NT * P // CH

        @block.gpsimd
        def _(pool):
            pool.wait_ge(cleared, 16 * n_cleared)
            for t in range(NT):
                pool.indirect_dma_start(sorted_x, bass.IndirectOffsetOnAxis(ap=position[:, t:t + 1], axis=0),
                                        xln[:, t, :], None).then_inc(sent, 16)
            pool.wait_ge(sent, 16 * NT)

        @block.tensor
        def _(pe):
            with pe.Fori(0, CHUNKS) as c:
                for bank, off, free, seen in ((ps_g, 0, g_sb, g_ps), (ps_u, I1, hid_ready, u_ps)):
                    pe.wait_ge(free, ONE + c * 2)
                    for half in range(2):
                        pe.matmul(bank[:, half, :], wgu[:, off + half * P:off + (half + 1) * P],
                                  xlnT[:, bass.ds(c * CH, CH)], start=True, stop=True).then_inc(seen, 1)
                pe.wait_ge(hid_ready, ONE + c * 2 + 2)
                pe.wait_ge(y_added, ONE + c)
                for t in range(CT):
                    for half in range(2):
                        mm = pe.matmul(ps_y[0][:, t, :], hid[:, half, t * P:(t + 1) * P], wd[:, half, :],
                                       start=(half == 0), stop=(half == 1))
                mm.then_inc(y_ps, 1)

        @block.scalar
        def _(act):
            with act.Fori(0, CHUNKS) as c:
                for half in range(2):
                    act.wait_ge(g_ps, ONE + c * 2 + half + 1)
                    act.wait_ge(hid_ready, ONE + c * 2)
                    act.activation(act_g[:, half, :], ps_g[:, half, :], ACT.Silu).then_inc(g_sb, 1)

        @block.vector
        def _(dve):
            with dve.Fori(0, CHUNKS) as c:
                for half in range(2):
                    dve.wait_ge(g_sb, ONE + c * 2 + half + 1)
                    dve.wait_ge(u_ps, ONE + c * 2 + half + 1)
                    dve.wait_ge(y_ps, ONE + c)
                    dve.tensor_tensor(hid[:, half, :], act_g[:, half, :], ps_u[:, half, :],
                                      ALU.mult).then_inc(hid_ready, 1)
                dve.wait_ge(y_ps, ONE + c + 1)
                x_c = x_sb[:, bass.ds(c * CT, CT), :]
                dve.tensor_tensor(x_c, x_c, ps_y[0][:], ALU.add).then_inc(y_added, 1)
            dve.wait_ge(y_added, ONE + CHUNKS)


def l1_routed(nc, ident, sorted_x, sorted_y, wgu, wd, expert_of, n_tiles):
    with ExitStack() as st:
        a = Alloc(nc, st)
        rows = a.sb("x_rows", [P, 2, 2, E])
        rowsT = a.sb("x_rowsT", [P, 2, 2, P])
        act_g = a.sb("x_act_g", [P, 2, 2, I1])
        hid = a.sb("x_hid", [P, 2, 2, I1])
        hidT = a.sb("x_hidT", [P, 2, 2, 2, P])
        y = a.sb("x_y", [P, 2, 2, E])
        ps_t = a.ps("x_ps_t", [P, 2, P])
        ps_gu = [a.ps(f"x_ps_gu{i}", [P, 2, 2 * I1]) for i in range(2)]
        ps_h = a.ps("x_ps_h", [P, 2, 2, P])
        ps_y = a.ps("x_ps_y", [P, 2, E])
        sem = {n: a.sem("x_" + n) for n in (
            "loaded0 loaded1 rowsT_ps rowsT_sb gu_ps act_ready hid_ready hidT_ps hidT_sb y_ps y_sb stored0 stored1").split()}
        a.start_at_one()
        block = st.enter_context(nc.Block())

        def first(i):
            return isinstance(i, int) and i == 0

        def pipeline(eng, *stages):
            count = eng.value_load(n_tiles[0:1, 0:1], min_val=NT, max_val=TILES)
            for lead, step in sorted(stages, key=lambda stage: -stage[0]):
                for i in range(lead):
                    step(i, i % 2)
            with eng.Fori(0, TP // 2 - 2) as j:
                for half in range(2):
                    for lead, step in stages:
                        i = j * 2 + half + lead
                        with eng.If(count > i * 2):
                            step(i, (half + lead) % 2)
            for last in range(TP - 4, TP):
                for lead, step in stages:
                    if last + lead < TP:
                        with eng.If(count > (last + lead) * 2):
                            step(last + lead, (last + lead) % 2)

        @block.sync
        def _(sp):
            def load(i, half):
                row = i * 2 * P if isinstance(i, int) else sp.snap(i * 2 * P)
                if not first(i):
                    sp.wait_ge(sem["rowsT_ps"], ONE + i - 1)
                sp.dma_start(rows[:, half, :, :], sorted_x[bass.ds(row, 2 * P), :].rearrange(
                    "(t p) e -> p t e", p=P)).then_inc(sem[f"loaded{half}"], 16)

            def store(i, half):
                row, y_at = i * 2 * P, ONE + i + 1
                if not isinstance(i, int):
                    row, y_at = sp.snap(row), sp.snap(y_at)
                sp.wait_ge(sem["y_sb"], y_at)
                sp.dma_start(sorted_y[bass.ds(row, 2 * P), :].rearrange("(t p) e -> p t e", p=P),
                             y[:, half, :, :]).then_inc(sem[f"stored{half}"], 16)
            pipeline(sp, (3, load), (0, store))

        @block.tensor
        def _(pe):
            experts = [[pe.alloc_register(f"x_expert{half}{t}") for t in range(2)] for half in range(2)]

            for registers in experts:
                for register in registers:
                    pe.reg_mov(register, 0)

            def turn(i, half):
                pe.wait_ge(sem[f"loaded{half}"], ONE + (i - half) * 8 + 16)
                if not first(i):
                    pe.wait_ge(sem["rowsT_sb"], ONE + i)
                for t in range(2):
                    mm = pe.transpose(ps_t[:, t, :], rows[:, half, t, :], ident[:])
                mm.then_inc(sem["rowsT_ps"], 1)

            def expert(half, t):
                return nc.s_assert_within(pe.snap(experts[half][t]), 0, E1 - 1, skip_runtime_bounds_check_because=(
                    "loaded with these bounds"))

            def up(i, half):
                for t in range(2):
                    pe.reg_mov(experts[half][t], pe.value_load(expert_of[0:1, bass.ds(i * 2 + t, 1)], min_val=0,
                                                               max_val=E1 - 1))
                e = [expert(half, t) for t in range(2)]
                pe.wait_ge(sem["rowsT_sb"], ONE + i + 1)
                if not first(i):
                    pe.wait_ge(sem["hid_ready"], ONE + i - 1)
                for t in range(2):
                    mm = pe.matmul(ps_gu[half][:, t, :], rowsT[:, half, t, :],
                                   wgu[:, bass.ds(e[t], 1), :].rearrange("p o c -> p (o c)"), start=True, stop=True)
                mm.then_inc(sem["gu_ps"], 1)

            def turn_hidden(i, half):
                pe.wait_ge(sem["hid_ready"], ONE + i + 1)
                pe.wait_ge(sem["hidT_sb"], ONE + i)
                for t in range(2):
                    for k in range(2):
                        mm = pe.transpose(ps_h[:, t, k, :], hid[:, half, t, k * P:(k + 1) * P], ident[:])
                mm.then_inc(sem["hidT_ps"], 1)

            def down(i, half):
                e = [expert(half, t) for t in range(2)]
                pe.wait_ge(sem["hidT_sb"], ONE + i + 1)
                pe.wait_ge(sem["y_sb"], ONE + i)
                for t in range(2):
                    for k in range(2):
                        mm = pe.matmul(ps_y[:, t, :], hidT[:, half, t, k, :],
                                       wd[:, bass.ds(e[t], 1), k, :].rearrange("p o c -> p (o c)"), start=(k == 0),
                                       stop=(k == 1))
                mm.then_inc(sem["y_ps"], 1)
            pipeline(pe, (0, turn_hidden), (1, up), (2, turn), (0, down))

        @block.scalar
        def _(act):
            def up(i, half):
                act.wait_ge(sem["gu_ps"], ONE + i + 1)
                if not first(i):
                    act.wait_ge(sem["hid_ready"], ONE + i - 1)
                act.activation(act_g[:, half, :, :], ps_gu[half][:, :, 0:I1], ACT.Silu).then_inc(sem["act_ready"], 1)

            def down(i, half):
                act.wait_ge(sem["hidT_ps"], ONE + i + 1)
                act.activation(hidT[:, half, :, :, :], ps_h[:], ACT.Copy).then_inc(sem["hidT_sb"], 1)
            pipeline(act, (0, down), (1, up))

        @block.vector
        def _(dve):
            def turn(i, half):
                dve.wait_ge(sem["rowsT_ps"], ONE + i + 1)
                if not first(i):
                    dve.wait_ge(sem["gu_ps"], ONE + i - 1)
                dve.tensor_copy(rowsT[:, half, :, :], ps_t[:]).then_inc(sem["rowsT_sb"], 1)

            def up(i, half):
                dve.wait_ge(sem["act_ready"], ONE + i + 1)
                if not first(i):
                    dve.wait_ge(sem["hidT_ps"], ONE + i - 1)
                dve.tensor_tensor(hid[:, half, :, :], act_g[:, half, :, :], ps_gu[half][:, :, I1:],
                                  ALU.mult).then_inc(sem["hid_ready"], 1)

            def down(i, half):
                dve.wait_ge(sem["y_ps"], ONE + i + 1)
                dve.wait_ge(sem[f"stored{half}"], ONE + (i - half) * 8)
                dve.tensor_copy(y[:, half, :, :], ps_y[:]).then_inc(sem["y_sb"], 1)
            pipeline(dve, (2, turn), (1, up), (0, down))

        @block.gpsimd
        def _(pool):
            count = pool.value_load(n_tiles[0:1, 0:1], min_val=NT, max_val=TILES)
            pool.wait_ge(sem["stored0"], ONE + (count + 3) // 4 * 16)
            pool.wait_ge(sem["stored1"], ONE + (count + 1) // 4 * 16)


def l1_gather(nc, x_sb, got, position, sorted_y, out):
    with ExitStack() as st:
        a = Alloc(nc, st)
        GROUPS = 8
        per = NT // GROUPS
        fetched = [a.sem(f"o_fetched{g}") for g in range(GROUPS)]
        added, stored = a.sem("o_added"), a.sem("o_stored")
        block = st.enter_context(nc.Block())

        @block.gpsimd
        def _(pool):
            for t in range(NT):
                pool.indirect_dma_start(got[:, t, :], None, sorted_y, bass.IndirectOffsetOnAxis(
                    ap=position[:, t:t + 1], axis=0)).then_inc(fetched[t // per], 16)

        @block.vector
        def _(dve):
            for g in range(GROUPS):
                dve.wait_ge(fetched[g], 16 * per)
                part = slice(g * per, (g + 1) * per)
                dve.tensor_tensor(x_sb[:, part, :], x_sb[:, part, :], got[:, part, :], ALU.add).then_inc(added, 1)

        @block.sync
        def _(sp):
            for g in range(GROUPS):
                sp.wait_ge(added, g + 1)
                part = slice(g * per, (g + 1) * per)
                sp.dma_start(out.rearrange("b (t p) e -> p (b t) e", p=P)[:, part, :],
                             x_sb[:, part, :]).then_inc(stored, 16)
            sp.wait_ge(stored, 16 * GROUPS)


_IN = ["x", "ctx_1024", "mask_SxS2_ik0", "mask_BxS2_bk0", "L0_xattn_Wk", "L0_xattn_bk", "L0_xattn_Wq", "L0_xattn_bq",
       "L0_xattn_Wv", "L0_xattn_bv", "L0_xattn_Wp", "L0_xattn_bp", "L0_ffn_router_w", "L0_ffn_router_b", "L0_ffn_w1",
       "L0_ffn_b1", "L0_ffn_w2", "L0_ffn_b2", "L1_xattn_ln_x_g", "L1_xattn_ln_x_b", "L1_xattn_ln_l_g",
       "L1_xattn_ln_l_b", "L1_xattn_q_gamma", "L1_xattn_k_gamma", "L1_xattn_W_q", "L1_xattn_W_kv", "L1_xattn_W_out",
       "L1_xattn_b_out", "L1_ffn_gate_w", "L1_ffn_shared_gate_w", "L1_ffn_shared_up_w", "L1_ffn_shared_down_w",
       "L1_ffn_routed_gate_w", "L1_ffn_routed_up_w", "L1_ffn_routed_down_w"]


def scale_column(nc, column, factor):
    with ExitStack() as st:
        done = Alloc(nc, st).sem("column_scaled")
        block = st.enter_context(nc.Block())

        @block.vector
        def _(dve):
            dve.tensor_scalar(column, column, factor, None, ALU.mult).then_inc(done, 1)
            dve.wait_ge(done, 1)


def build_program(nc, d, out):
    flag_scratch = nc.dram_tensor("flag_scratch", (B, NW), F32, kind="Internal").ap()
    kT_scratch = nc.dram_tensor("kT_scratch", (B, NW, P, W), F32, kind="Internal").ap()
    v_scratch = nc.dram_tensor("v_scratch", (B, NW, P, W), F32, kind="Internal").ap()
    sorted_x = nc.dram_tensor("sorted_x", (SLOTS, E), F32, kind="Internal").ap()
    sorted_y = nc.dram_tensor("sorted_y", (SLOTS, E), F32, kind="Internal").ap()
    q_parts = nc.dram_tensor("q_parts", (3, P, NT * P), BF16, kind="Internal").ap()
    k_parts = nc.dram_tensor("k_parts", (3, P, W), BF16, kind="Internal").ap()
    with ExitStack() as whole:
        keep = Alloc(nc, whole)
        x_sb = keep.sb("x_sb", [P, NT, E])
        xln = keep.sb("xln", [P, NT, E])
        ident = keep.sb("ident", [P, P])
        load_tokens(nc, d["x"], x_sb, ident)

        with ExitStack() as st:
            a = Alloc(nc, st)
            xlnT = a.sb("xlnT0", [P, NT * P])
            mneg = a.sb("mneg", [P, QT, NW, W])
            flags = a.sb("flags0", [1, 2 * NW], I32)
            wqT, wkT, wvT, wpT, bv, bp = (a.sb("a0" + n, [P, P]) for n in "wqT wkT wvT wpT bv bp".split())
            bq, bk = a.sb("a0bq", [P, 1]), a.sb("a0bk", [P, 1])
            turn_weights(nc, "w0", [(d["L0_xattn_Wq"], wqT[:]), (d["L0_xattn_Wk"], wkT[:]), (d["L0_xattn_Wv"], wvT[:]),
                                    (d["L0_xattn_Wp"], wpT[:])], ident,
                         columns=[(d["L0_xattn_bq"], bq[:]), (d["L0_xattn_bk"], bk[:])],
                         rows=[(d["L0_xattn_bv"], bv[:]), (d["L0_xattn_bp"], bp[:])])
            layer_norm(nc, "ln0", x_sb, xln, NT, xlnT, ident)
            l0_mask(nc, d["mask_SxS2_ik0"], mneg, flags, ident)
            l0_attention(nc, x_sb, xlnT, mneg, flags, ident, d["ctx_1024"], (wqT, wkT, wvT, wpT, bq, bk, bv, bp),
                         q_parts, k_parts)

        small = Alloc(nc, whole)
        ctx_gain, ctx_shift, lat_gain, lat_shift, gq, gk = (
            small.sb("a1" + n, [P, 1]) for n in "ctx_gain ctx_shift lat_gain lat_shift gq gk".split())
        wq, wkv, wout, bout = (small.sb(n, [P, c]) for n, c in (("wq", E), ("wkv", 2 * E), ("wout", E), ("bout", E)))
        gate, shared_gu = small.sb("gate", [P, E1]), small.sb("shared_gu", [P, 2 * I1])
        shared_d = small.sb("shared_d", [P, 2, E])
        flags = small.sb("flags1", [1, B // 2], I32)
        small_loaded = small.sem("small_loaded")
        with ExitStack() as st:
            a = Alloc(nc, st)
            xlnT = a.sb("xlnT1", [P, NT * P])
            rw, rb = a.sb("rw", [P, E0]), a.sb("rb", [P, E0])
            w1, w2 = a.sb("w1", [P, E0, I0]), a.sb("w2", [P, E0, 2, E])
            b1, b2 = a.sb("b1", [P, E0, 2]), a.sb("b2", [E0, E])
            weight = a.sb("weight", [P, NT, E0])
            router_loaded, experts_loaded = a.sem("router_loaded"), a.sem("experts_loaded")
            n_router = start_loads(nc, router_loaded, rows=[(d["L0_ffn_router_b"], rb[:])], others=[
                (d["L0_ffn_router_w"], rw[:]), (d["L0_ffn_b2"], b2[:])])
            with nc.allow_non_contiguous_dma(reason="biases by feature, 16 KB in all"):
                n_experts = start_loads(nc, experts_loaded, others=[
                    (d["L0_ffn_w1"].rearrange("e h i -> h e i"), w1[:]),
                    (d["L0_ffn_w2"].rearrange("e (t p) h -> p e t h", p=P), w2[:]),
                    (d["L0_ffn_b1"].rearrange("e (t p) -> p e t", p=P), b1[:])])
                n_small = start_loads(nc, small_loaded, columns=[
                    (d["L1_xattn_ln_x_g"], ctx_gain[:]), (d["L1_xattn_ln_x_b"], ctx_shift[:]),
                    (d["L1_xattn_ln_l_g"], lat_gain[:]), (d["L1_xattn_ln_l_b"], lat_shift[:]),
                    (d["L1_xattn_k_gamma"], gk[0:D1, :]), (d["L1_xattn_k_gamma"], gk[D1:, :]),
                    (d["L1_xattn_q_gamma"], gq[0:D1, :]), (d["L1_xattn_q_gamma"], gq[D1:, :])],
                    rows=[(d["L1_xattn_b_out"], bout[:])],
                    others=[(d["L1_xattn_W_q"], wq[:]), (d["L1_xattn_W_kv"], wkv[:]), (d["L1_xattn_W_out"], wout[:]),
                            (d["L1_ffn_gate_w"], gate[:]), (d["L1_ffn_shared_gate_w"], shared_gu[:, 0:I1]),
                            (d["L1_ffn_shared_up_w"], shared_gu[:, I1:]),
                            (d["L1_ffn_shared_down_w"].rearrange("(t p) h -> p t h", p=P), shared_d[:])])
            layer_norm(nc, "ln1", x_sb, xln, NT, xlnT, ident)
            await_loads(nc, router_loaded, n_router)
            l0_router(nc, x_sb, xlnT, ident, rw, rb, b2, weight)
            await_loads(nc, experts_loaded, n_experts)
            l0_experts(nc, x_sb, xlnT, w1, b1, w2, weight)

        large = Alloc(nc, whole)
        zeros = large.sb("zeros", [P, 8, E])
        wgu_loaded, wd_loaded, cleared = (large.sem(n) for n in ("wgu_loaded", "wd_loaded", "cleared"))
        n_cleared = start_clearing(nc, zeros, (sorted_x, sorted_y), cleared)
        with ExitStack() as st:
            a = Alloc(nc, st)
            qT, klT, vl = a.sb("qT1", [P, NT * P]), a.sb("klT", [P, NT * P]), a.sb("vl", [P, NT, E])
            await_loads(nc, small_loaded, n_small)
            scale_column(nc, gq[:], SCALE1)
            l1_flags(nc, d["mask_BxS2_bk0"], flag_scratch, flags)
            l1_project(nc, "c_", ident, ctx_gain, ctx_shift, wkv, gk,
                       context=(d["ctx_1024"], flags, kT_scratch, v_scratch))
            layer_norm(nc, "ln2", x_sb, xln, NT)
            l1_project(nc, "l_", ident, lat_gain, lat_shift, wkv, gk, latents=(xln, wq, gq, qT, klT, vl))
            l1_attention(nc, x_sb, ident, flags, d["mask_BxS2_bk0"], qT, klT, vl, kT_scratch, v_scratch, wout, bout,
                         xln[:].rearrange("p (c j k) q -> p c j k q", c=2, j=PAIRS))

        with ExitStack() as st:
            a = Alloc(nc, st)
            xlnT = a.sb("xlnT3", [P, NT * P])
            wgu, wd = a.sb("wgu", [P, E1, 2 * I1]), a.sb("wd", [P, E1, 2, E])
            position = a.sb("position", [P, NT], U32)
            expert_of, n_tiles = a.sb("expert_of", [1, 2 * TP], I32), a.sb("n_tiles", [1, 1], I32)
            n_wgu = start_loads(nc, wgu_loaded, others=[
                (d["L1_ffn_routed_gate_w"].rearrange("e h i -> h e i"), wgu[:, :, 0:I1]),
                (d["L1_ffn_routed_up_w"].rearrange("e h i -> h e i"), wgu[:, :, I1:])])
            n_wd = start_loads(nc, wd_loaded, others=[
                (d["L1_ffn_routed_down_w"].rearrange("e (t p) h -> p e t h", p=P), wd[:])])
            layer_norm(nc, "ln3", x_sb, xln, NT, xlnT, ident)
            l1_route(nc, xln, xlnT, gate, position, expert_of, n_tiles)
            l1_shared(nc, x_sb, xlnT, shared_gu, shared_d, xln, position, sorted_x, cleared, n_cleared)
            await_loads(nc, wgu_loaded, n_wgu)
            await_loads(nc, wd_loaded, n_wd)
            l1_routed(nc, ident, sorted_x, sorted_y, wgu, wd, expert_of, n_tiles)
            l1_gather(nc, x_sb, xln, position, sorted_y, out)


def kernel(**inputs):
    import numpy as _np
    import concourse.bacc as _bacc
    from concourse import mybir as _mybir
    from concourse.bass_utils import run_bass_kernel_spmd as _run

    nc = _bacc.Bacc("TRN2", target_bir_lowering=False, num_devices=1)
    arrays, tensors = {}, {}
    for name in _IN:
        a = _np.ascontiguousarray(inputs[name])
        arrays["in_" + name] = a
        tensors[name] = nc.dram_tensor("in_" + name, a.shape, _mybir.dt.from_np(a.dtype), kind="ExternalInput").ap()
    out = nc.dram_tensor("out_x", (B, S, E), F32, kind="ExternalOutput").ap()
    build_program(nc, tensors, out)
    result = _run(nc, [arrays], core_ids=[0])
    return result.results[0]["out_x"]
```
